# Optimizing a Trainium2 kernel written in Bass

```python
import numpy as np
import jax
import jax.numpy as jnp

def _softmax(x, axis=-1):
    return jax.nn.softmax(x, axis=axis)

def _gelu(x):
    return jax.nn.gelu(x, approximate=True)

def _silu(x):
    return jax.nn.silu(x)

def _sigmoid(x):
    return jax.nn.sigmoid(x)

def _layernorm(x, axis=-1, eps=1e-05):
    m = jnp.mean(x, axis=axis, keepdims=True)
    v = jnp.var(x, axis=axis, keepdims=True)
    return (x - m) / jnp.sqrt(v + eps)

def _scatter_add(tgt, idx, src, axis=0):
    return tgt.at[idx].add(src)

def _segment_sum(src, seg, n):
    return jax.ops.segment_sum(src, seg, n)
kernel_name = 'mk_sandwich_d2_jaxref_r8_8a5b8b'

def setup_inputs(seed: int=0):
    np.random.seed(seed)
    _w = jnp.asarray

    def _L0_attn_setup():
        import jax, jax.numpy as jnp
        import numpy as np
        DEPTH, DIM, DFF, VOCAB = (4, 64, 256, 512)
        EPS = 1e-05

        def layernorm(x, w, b):
            mu = jnp.mean(x, axis=-1, keepdims=True)
            var = jnp.mean((x - mu) ** 2, axis=-1, keepdims=True)
            return (x - mu) * jax.lax.rsqrt(var + EPS) * w + b

        def sconv(x, phazor_c, last_conv_c):
            B, L, D = x.shape
            r = jnp.abs(phazor_c)
            p = jnp.tanh(r) * jnp.exp(1j * jnp.angle(phazor_c))
            prog = p[None, :] ** jnp.arange(L, dtype=jnp.float32)[:, None]
            filt_fft = jnp.fft.fft(prog, n=2 * L, axis=0)
            x_fft = jnp.fft.fft(x.astype(jnp.complex64), n=2 * L, axis=1)
            conv = jnp.fft.ifft(filt_fft[None] * x_fft, axis=1)[:, :L]
            conv = conv + last_conv_c[None, None, :] * prog[None] * p[None, None, :]
            return conv.real.astype(x.dtype)

        def _forward(x, Win, bin, ln1_w, ln1_b, phz_re, phz_im, lc_re, lc_im, sc_lin, ln2_w, ln2_b, W1, b1, W2, b2, lnl_w, lnl_b, Wout, bout):
            h = jnp.einsum('blv,dv->bld', x, Win) + bin

            def body(h, p):
                l1w, l1b, pr, pi, lr, li, scl, l2w, l2b, w1, b1_, w2, b2_ = p
                y = jax.nn.silu(layernorm(h, l1w, l1b))
                y = sconv(y, pr + 1j * pi, lr + 1j * li)
                h = h + y * scl
                y = layernorm(h, l2w, l2b)
                y = jax.nn.silu(jnp.einsum('bld,fd->blf', y, w1) + b1_)
                y = jnp.einsum('blf,df->bld', y, w2) + b2_
                return (h + y, None)
            xs = (ln1_w, ln1_b, phz_re, phz_im, lc_re, lc_im, sc_lin, ln2_w, ln2_b, W1, b1, W2, b2)
            h, _ = jax.lax.scan(body, h, xs)
            h = layernorm(h, lnl_w, lnl_b)
            return jnp.einsum('bld,vd->blv', h, Wout) + bout
        key = jax.random.key(seed)
        ks = jax.random.split(key, 20)
        f32 = jnp.float32
        inp = {}
        inp['x'] = jax.random.normal(ks[0], (2, 512, VOCAB), dtype=f32)
        inp['Win'] = jax.random.normal(ks[1], (DIM, VOCAB), dtype=f32) * VOCAB ** (-0.5)
        inp['bin'] = jnp.zeros((DIM,), f32)
        inp['ln1_w'] = jnp.ones((DEPTH, DIM), f32)
        inp['ln1_b'] = jnp.zeros((DEPTH, DIM), f32)
        ang = 2 * np.pi * jnp.arange(DIM, dtype=f32) / DIM
        mag = jnp.abs(jax.random.normal(ks[2], (DEPTH, DIM), dtype=f32))
        inp['phz_re'] = mag * jnp.cos(ang)[None]
        inp['phz_im'] = mag * jnp.sin(ang)[None]
        inp['lc_re'] = jax.random.normal(ks[3], (DEPTH, DIM), dtype=f32)
        inp['lc_im'] = jax.random.normal(ks[4], (DEPTH, DIM), dtype=f32)
        inp['sc_lin'] = jnp.ones((DEPTH, DIM), f32)
        inp['ln2_w'] = jnp.ones((DEPTH, DIM), f32)
        inp['ln2_b'] = jnp.zeros((DEPTH, DIM), f32)
        inp['W1'] = jax.random.normal(ks[5], (DEPTH, DFF, DIM), dtype=f32) * DIM ** (-0.5)
        inp['b1'] = jnp.zeros((DEPTH, DFF), f32)
        inp['W2'] = jax.random.normal(ks[6], (DEPTH, DIM, DFF), dtype=f32) * DFF ** (-0.5)
        inp['b2'] = jnp.zeros((DEPTH, DIM), f32)
        inp['lnl_w'] = jnp.ones((DIM,), f32)
        inp['lnl_b'] = jnp.zeros((DIM,), f32)
        inp['Wout'] = jax.random.normal(ks[7], (VOCAB, DIM), dtype=f32) * DIM ** (-0.5)
        inp['bout'] = jnp.zeros((VOCAB,), f32)
        return inp
    _L0_attn_in = _L0_attn_setup()

    def _L0_ffn_setup():
        import jax, jax.numpy as jnp
        import numpy as np
        FP4_VALS = jnp.array([0.0, 0.5, 1.0, 1.5, 2.0, 3.0, 4.0, 6.0, -0.0, -0.5, -1.0, -1.5, -2.0, -3.0, -4.0, -6.0], dtype=jnp.float32)
        B, S, IN, OUT, R, GROUP = (4, 256, 512, 512, 16, 16)
        LORA_ALPHA = 16
        SCALING = LORA_ALPHA / R

        def _dequantize(packed_weight, block_scales, global_scale):
            lo = packed_weight & 15
            hi = packed_weight >> 4 & 15
            codes = jnp.stack([lo, hi], axis=-1).reshape(OUT, IN)
            w = FP4_VALS[codes]
            w = w.reshape(OUT, IN // GROUP, GROUP) * block_scales[:, :, None]
            return w.reshape(OUT, IN) * global_scale[0]
        key = jax.random.key(seed)
        k0, k1, k2, k3, k4 = jax.random.split(key, 5)
        x = jax.random.normal(k0, (B, S, IN), dtype=jnp.float32)
        packed_weight = jax.random.randint(k1, (OUT, IN // 2), 0, 32, dtype=jnp.int32)
        block_scales = jax.random.uniform(k2, (OUT, IN // GROUP), dtype=jnp.float32, minval=0.01, maxval=0.2)
        global_scale = jnp.ones((1,), dtype=jnp.float32)
        bound = 1.0 / np.sqrt(IN)
        lora_A = jax.random.uniform(k3, (R, IN), dtype=jnp.float32, minval=-bound, maxval=bound)
        lora_B = jax.random.normal(k4, (OUT, R), dtype=jnp.float32) * 0.02
        return {'x': x, 'packed_weight': packed_weight, 'block_scales': block_scales, 'global_scale': global_scale, 'lora_A': lora_A, 'lora_B': lora_B}
    _L0_ffn_in = _L0_ffn_setup()

    def _L1_attn_setup():
        import jax, jax.numpy as jnp
        import numpy as np
        from jax import lax
        H = 512
        DIN = 1024
        N = 16
        K = 4
        R = 32
        B_SZ = 2
        L = 256
        EPS = 1e-06

        def rmsnorm(x, w):
            return x * lax.rsqrt(jnp.mean(x * x, axis=-1, keepdims=True) + EPS) * w

        def _selective_scan(x, dt, A, Bm, Cm):
            xT = jnp.transpose(x, (2, 0, 1))
            dtT = jnp.transpose(dt, (2, 0, 1))
            BT = jnp.transpose(Bm, (2, 0, 1))
            CT = jnp.transpose(Cm, (2, 0, 1))

            def step(h, inp):
                x_t, dt_t, B_t, C_t = inp
                dA = jnp.exp(dt_t[..., None] * A)
                dBx = dt_t[..., None] * B_t[:, None, :] * x_t[..., None]
                h = dA * h + dBx
                y = jnp.einsum('bdn,bn->bd', h, C_t)
                return (h, y)
            h0 = jnp.zeros((x.shape[0], x.shape[1], A.shape[1]), dtype=x.dtype)
            _, ys = lax.scan(step, h0, (xT, dtT, BT, CT))
            return jnp.transpose(ys, (1, 2, 0))
        key = jax.random.key(seed)
        ks = jax.random.split(key, 8)
        hidden_states = jax.random.normal(ks[0], (B_SZ, L, H), dtype=jnp.float32)
        s = 0.02
        in_proj_w = jax.random.normal(ks[1], (H, 2 * DIN), dtype=jnp.float32) * s
        conv_w = jax.random.normal(ks[2], (DIN, K), dtype=jnp.float32) * 0.2
        conv_b = jax.random.normal(ks[3], (DIN,), dtype=jnp.float32) * 0.02
        x_proj_w = jax.random.normal(ks[4], (R + 2 * N, DIN), dtype=jnp.float32) * s
        dt_proj_w = jax.random.normal(ks[5], (DIN, R), dtype=jnp.float32) * s
        dt_bias = jax.random.normal(ks[6], (DIN,), dtype=jnp.float32) * 0.5 - 4.0
        A_log = jnp.log(jnp.broadcast_to(jnp.arange(1, N + 1, dtype=jnp.float32)[None, :], (DIN, N)))
        D_param = jnp.ones((DIN,), dtype=jnp.float32)
        out_proj_w = jax.random.normal(ks[7], (H, DIN), dtype=jnp.float32) * s
        dt_ln_w = jnp.ones((R,), dtype=jnp.float32)
        B_ln_w = jnp.ones((N,), dtype=jnp.float32)
        C_ln_w = jnp.ones((N,), dtype=jnp.float32)
        return dict(hidden_states=hidden_states, in_proj_w=in_proj_w, conv_w=conv_w, conv_b=conv_b, x_proj_w=x_proj_w, dt_proj_w=dt_proj_w, dt_bias=dt_bias, A_log=A_log, D_param=D_param, out_proj_w=out_proj_w, dt_ln_w=dt_ln_w, B_ln_w=B_ln_w, C_ln_w=C_ln_w)
    _L1_attn_in = _L1_attn_setup()

    def _L1_ffn_setup():
        import jax, jax.numpy as jnp
        import numpy as np
        BS = 128
        FP8_MAX = 448.0

        def act_quant(x):
            T, K = x.shape
            xb = x.reshape(T, K // BS, BS)
            amax = jnp.max(jnp.abs(xb), axis=-1)
            scale = amax / FP8_MAX + 1e-12
            xq = (xb / scale[:, :, None]).reshape(T, K)
            return (xq, scale)

        def linear_dsv3(x, wq, w_scale):
            T, K = x.shape
            N = wq.shape[0]
            xq, xs = act_quant(x)
            xdq = (xq.reshape(T, K // BS, BS) * xs[:, :, None]).reshape(T, K)
            wdq = (wq.reshape(N // BS, BS, K // BS, BS) * w_scale[:, None, :, None]).reshape(N, K)
            return xdq @ wdq.T
        key = jax.random.key(seed)
        ks = jax.random.split(key, 4)
        DIM, INTER = (512, 1792)

        def make_qweight(k, n, m):
            w = jax.random.normal(k, (n, m), dtype=jnp.float32) * 0.02
            wb = w.reshape(n // BS, BS, m // BS, BS)
            amax = jnp.max(jnp.abs(wb), axis=(1, 3))
            scale = amax / FP8_MAX + 1e-12
            wq = (wb / scale[:, None, :, None]).reshape(n, m)
            return (wq, scale)
        x = jax.random.normal(ks[0], (2, 128, DIM), dtype=jnp.float32)
        w1, w1_scale = make_qweight(ks[1], INTER, DIM)
        w3, w3_scale = make_qweight(ks[2], INTER, DIM)
        w2, w2_scale = make_qweight(ks[3], DIM, INTER)
        return {'x': x, 'w1': w1, 'w1_scale': w1_scale, 'w3': w3, 'w3_scale': w3_scale, 'w2': w2, 'w2_scale': w2_scale}
    _L1_ffn_in = _L1_ffn_setup()
    _d = {'L0_attn_x': _L0_attn_in['x'], 'L0_attn_Win': _L0_attn_in['Win'], 'L0_attn_bin': _L0_attn_in['bin'], 'L0_attn_ln1_w': _L0_attn_in['ln1_w'], 'L0_attn_ln1_b': _L0_attn_in['ln1_b'], 'L0_attn_phz_re': _L0_attn_in['phz_re'], 'L0_attn_phz_im': _L0_attn_in['phz_im'], 'L0_attn_lc_re': _L0_attn_in['lc_re'], 'L0_attn_lc_im': _L0_attn_in['lc_im'], 'L0_attn_sc_lin': _L0_attn_in['sc_lin'], 'L0_attn_ln2_w': _L0_attn_in['ln2_w'], 'L0_attn_ln2_b': _L0_attn_in['ln2_b'], 'L0_attn_W1': _L0_attn_in['W1'], 'L0_attn_b1': _L0_attn_in['b1'], 'L0_attn_W2': _L0_attn_in['W2'], 'L0_attn_b2': _L0_attn_in['b2'], 'L0_attn_lnl_w': _L0_attn_in['lnl_w'], 'L0_attn_lnl_b': _L0_attn_in['lnl_b'], 'L0_attn_Wout': _L0_attn_in['Wout'], 'L0_attn_bout': _L0_attn_in['bout'], 'L0_ffn_packed_weight': _L0_ffn_in['packed_weight'], 'L0_ffn_block_scales': _L0_ffn_in['block_scales'], 'L0_ffn_global_scale': _L0_ffn_in['global_scale'], 'L0_ffn_lora_A': _L0_ffn_in['lora_A'], 'L0_ffn_lora_B': _L0_ffn_in['lora_B'], 'L1_attn_in_proj_w': _L1_attn_in['in_proj_w'], 'L1_attn_conv_w': _L1_attn_in['conv_w'], 'L1_attn_conv_b': _L1_attn_in['conv_b'], 'L1_attn_x_proj_w': _L1_attn_in['x_proj_w'], 'L1_attn_dt_proj_w': _L1_attn_in['dt_proj_w'], 'L1_attn_dt_bias': _L1_attn_in['dt_bias'], 'L1_attn_A_log': _L1_attn_in['A_log'], 'L1_attn_D_param': _L1_attn_in['D_param'], 'L1_attn_out_proj_w': _L1_attn_in['out_proj_w'], 'L1_attn_dt_ln_w': _L1_attn_in['dt_ln_w'], 'L1_attn_B_ln_w': _L1_attn_in['B_ln_w'], 'L1_attn_C_ln_w': _L1_attn_in['C_ln_w'], 'L1_ffn_w1': _L1_ffn_in['w1'], 'L1_ffn_w1_scale': _L1_ffn_in['w1_scale'], 'L1_ffn_w3': _L1_ffn_in['w3'], 'L1_ffn_w3_scale': _L1_ffn_in['w3_scale'], 'L1_ffn_w2': _L1_ffn_in['w2'], 'L1_ffn_w2_scale': _L1_ffn_in['w2_scale']}
    _x0 = _d['L0_attn_x']
    _d['L0_attn_x'] = jax.random.normal(jax.random.fold_in(jax.random.key(seed), 1), (2, 512, 512), dtype=_x0.dtype)
    del _x0
    return _d

def reference(L0_attn_x, L0_attn_Win, L0_attn_bin, L0_attn_ln1_w, L0_attn_ln1_b, L0_attn_phz_re, L0_attn_phz_im, L0_attn_lc_re, L0_attn_lc_im, L0_attn_sc_lin, L0_attn_ln2_w, L0_attn_ln2_b, L0_attn_W1, L0_attn_b1, L0_attn_W2, L0_attn_b2, L0_attn_lnl_w, L0_attn_lnl_b, L0_attn_Wout, L0_attn_bout, L0_ffn_packed_weight, L0_ffn_block_scales, L0_ffn_global_scale, L0_ffn_lora_A, L0_ffn_lora_B, L1_attn_in_proj_w, L1_attn_conv_w, L1_attn_conv_b, L1_attn_x_proj_w, L1_attn_dt_proj_w, L1_attn_dt_bias, L1_attn_A_log, L1_attn_D_param, L1_attn_out_proj_w, L1_attn_dt_ln_w, L1_attn_B_ln_w, L1_attn_C_ln_w, L1_ffn_w1, L1_ffn_w1_scale, L1_ffn_w3, L1_ffn_w3_scale, L1_ffn_w2, L1_ffn_w2_scale):

    def _L0_attn_ref(x, Win, bin, ln1_w, ln1_b, phz_re, phz_im, lc_re, lc_im, sc_lin, ln2_w, ln2_b, W1, b1, W2, b2, lnl_w, lnl_b, Wout, bout):
        import jax, jax.numpy as jnp
        import numpy as np
        DEPTH, DIM, DFF, VOCAB = (4, 64, 256, 512)
        EPS = 1e-05

        def layernorm(x, w, b):
            mu = jnp.mean(x, axis=-1, keepdims=True)
            var = jnp.mean((x - mu) ** 2, axis=-1, keepdims=True)
            return (x - mu) * jax.lax.rsqrt(var + EPS) * w + b

        def sconv(x, phazor_c, last_conv_c):
            B, L, D = x.shape
            r = jnp.abs(phazor_c)
            p = jnp.tanh(r) * jnp.exp(1j * jnp.angle(phazor_c))
            prog = p[None, :] ** jnp.arange(L, dtype=jnp.float32)[:, None]
            filt_fft = jnp.fft.fft(prog, n=2 * L, axis=0)
            x_fft = jnp.fft.fft(x.astype(jnp.complex64), n=2 * L, axis=1)
            conv = jnp.fft.ifft(filt_fft[None] * x_fft, axis=1)[:, :L]
            conv = conv + last_conv_c[None, None, :] * prog[None] * p[None, None, :]
            return conv.real.astype(x.dtype)

        def _forward(x, Win, bin, ln1_w, ln1_b, phz_re, phz_im, lc_re, lc_im, sc_lin, ln2_w, ln2_b, W1, b1, W2, b2, lnl_w, lnl_b, Wout, bout):
            h = jnp.einsum('blv,dv->bld', x, Win) + bin

            def body(h, p):
                l1w, l1b, pr, pi, lr, li, scl, l2w, l2b, w1, b1_, w2, b2_ = p
                y = jax.nn.silu(layernorm(h, l1w, l1b))
                y = sconv(y, pr + 1j * pi, lr + 1j * li)
                h = h + y * scl
                y = layernorm(h, l2w, l2b)
                y = jax.nn.silu(jnp.einsum('bld,fd->blf', y, w1) + b1_)
                y = jnp.einsum('blf,df->bld', y, w2) + b2_
                return (h + y, None)
            xs = (ln1_w, ln1_b, phz_re, phz_im, lc_re, lc_im, sc_lin, ln2_w, ln2_b, W1, b1, W2, b2)
            h, _ = jax.lax.scan(body, h, xs)
            h = layernorm(h, lnl_w, lnl_b)
            return jnp.einsum('bld,vd->blv', h, Wout) + bout
        return _forward(x, Win, bin, ln1_w, ln1_b, phz_re, phz_im, lc_re, lc_im, sc_lin, ln2_w, ln2_b, W1, b1, W2, b2, lnl_w, lnl_b, Wout, bout)

    def _L0_ffn_ref(x, packed_weight, block_scales, global_scale, lora_A, lora_B):
        import jax, jax.numpy as jnp
        import numpy as np
        FP4_VALS = jnp.array([0.0, 0.5, 1.0, 1.5, 2.0, 3.0, 4.0, 6.0, -0.0, -0.5, -1.0, -1.5, -2.0, -3.0, -4.0, -6.0], dtype=jnp.float32)
        B, S, IN, OUT, R, GROUP = (4, 256, 512, 512, 16, 16)
        LORA_ALPHA = 16
        SCALING = LORA_ALPHA / R

        def _dequantize(packed_weight, block_scales, global_scale):
            lo = packed_weight & 15
            hi = packed_weight >> 4 & 15
            codes = jnp.stack([lo, hi], axis=-1).reshape(OUT, IN)
            w = FP4_VALS[codes]
            w = w.reshape(OUT, IN // GROUP, GROUP) * block_scales[:, :, None]
            return w.reshape(OUT, IN) * global_scale[0]
        W = _dequantize(packed_weight, block_scales, global_scale)
        base = jnp.einsum('bsi,oi->bso', x, W)
        lora = jnp.einsum('bsr,or->bso', jnp.einsum('bsi,ri->bsr', x, lora_A), lora_B)
        return base + SCALING * lora

    def _L1_attn_ref(hidden_states, in_proj_w, conv_w, conv_b, x_proj_w, dt_proj_w, dt_bias, A_log, D_param, out_proj_w, dt_ln_w, B_ln_w, C_ln_w):
        import jax, jax.numpy as jnp
        import numpy as np
        from jax import lax
        H = 512
        DIN = 1024
        N = 16
        K = 4
        R = 32
        B_SZ = 2
        L = 256
        EPS = 1e-06

        def rmsnorm(x, w):
            return x * lax.rsqrt(jnp.mean(x * x, axis=-1, keepdims=True) + EPS) * w

        def _selective_scan(x, dt, A, Bm, Cm):
            xT = jnp.transpose(x, (2, 0, 1))
            dtT = jnp.transpose(dt, (2, 0, 1))
            BT = jnp.transpose(Bm, (2, 0, 1))
            CT = jnp.transpose(Cm, (2, 0, 1))

            def step(h, inp):
                x_t, dt_t, B_t, C_t = inp
                dA = jnp.exp(dt_t[..., None] * A)
                dBx = dt_t[..., None] * B_t[:, None, :] * x_t[..., None]
                h = dA * h + dBx
                y = jnp.einsum('bdn,bn->bd', h, C_t)
                return (h, y)
            h0 = jnp.zeros((x.shape[0], x.shape[1], A.shape[1]), dtype=x.dtype)
            _, ys = lax.scan(step, h0, (xT, dtT, BT, CT))
            return jnp.transpose(ys, (1, 2, 0))
        proj = hidden_states @ in_proj_w
        x, z = jnp.split(proj, 2, axis=-1)
        x = jnp.transpose(x, (0, 2, 1))
        z = jnp.transpose(z, (0, 2, 1))
        Lq = x.shape[-1]
        xp = jnp.pad(x, ((0, 0), (0, 0), (K - 1, 0)))
        xc = conv_b[None, :, None]
        for k in range(K):
            xc = xc + conv_w[None, :, k:k + 1] * xp[:, :, k:k + Lq]
        xc = jax.nn.silu(xc)
        ssm_p = jnp.einsum('bdl,ed->ble', xc, x_proj_w)
        dt_r = rmsnorm(ssm_p[..., :R], dt_ln_w)
        Bm = rmsnorm(ssm_p[..., R:R + N], B_ln_w)
        Cm = rmsnorm(ssm_p[..., R + N:], C_ln_w)
        dt = jnp.einsum('blr,dr->bdl', dt_r, dt_proj_w)
        dt = jax.nn.softplus(dt + dt_bias[None, :, None])
        A = -jnp.exp(A_log)
        Bm = jnp.transpose(Bm, (0, 2, 1))
        Cm = jnp.transpose(Cm, (0, 2, 1))
        ys = _selective_scan(xc, dt, A, Bm, Cm)
        y = (ys + D_param[None, :, None] * xc) * jax.nn.silu(z)
        return jnp.einsum('bdl,hd->blh', y, out_proj_w)

    def _L1_ffn_ref(x, w1, w1_scale, w3, w3_scale, w2, w2_scale):
        import jax, jax.numpy as jnp
        import numpy as np
        BS = 128
        FP8_MAX = 448.0

        def act_quant(x):
            T, K = x.shape
            xb = x.reshape(T, K // BS, BS)
            amax = jnp.max(jnp.abs(xb), axis=-1)
            scale = amax / FP8_MAX + 1e-12
            xq = (xb / scale[:, :, None]).reshape(T, K)
            return (xq, scale)

        def linear_dsv3(x, wq, w_scale):
            T, K = x.shape
            N = wq.shape[0]
            xq, xs = act_quant(x)
            xdq = (xq.reshape(T, K // BS, BS) * xs[:, :, None]).reshape(T, K)
            wdq = (wq.reshape(N // BS, BS, K // BS, BS) * w_scale[:, None, :, None]).reshape(N, K)
            return xdq @ wdq.T
        B, S, D = x.shape
        xf = x.reshape(-1, D)
        g = linear_dsv3(xf, w1, w1_scale)
        u = linear_dsv3(xf, w3, w3_scale)
        h = jax.nn.silu(g) * u
        y = linear_dsv3(h, w2, w2_scale)
        return y.reshape(B, S, D)
    x = L0_attn_x
    x = x + _layernorm(_L0_attn_ref(_layernorm(x, axis=-1), L0_attn_Win, L0_attn_bin, L0_attn_ln1_w, L0_attn_ln1_b, L0_attn_phz_re, L0_attn_phz_im, L0_attn_lc_re, L0_attn_lc_im, L0_attn_sc_lin, L0_attn_ln2_w, L0_attn_ln2_b, L0_attn_W1, L0_attn_b1, L0_attn_W2, L0_attn_b2, L0_attn_lnl_w, L0_attn_lnl_b, L0_attn_Wout, L0_attn_bout), axis=-1)
    x = x + _layernorm(_L0_ffn_ref(_layernorm(x, axis=-1), L0_ffn_packed_weight, L0_ffn_block_scales, L0_ffn_global_scale, L0_ffn_lora_A, L0_ffn_lora_B), axis=-1)
    x = x + _layernorm(_L1_attn_ref(_layernorm(x, axis=-1), L1_attn_in_proj_w, L1_attn_conv_w, L1_attn_conv_b, L1_attn_x_proj_w, L1_attn_dt_proj_w, L1_attn_dt_bias, L1_attn_A_log, L1_attn_D_param, L1_attn_out_proj_w, L1_attn_dt_ln_w, L1_attn_B_ln_w, L1_attn_C_ln_w), axis=-1)
    x = x + _layernorm(_L1_ffn_ref(_layernorm(x, axis=-1), L1_ffn_w1, L1_ffn_w1_scale, L1_ffn_w3, L1_ffn_w3_scale, L1_ffn_w2, L1_ffn_w2_scale), axis=-1)
    return x

_drawn_inputs = setup_inputs


def setup_inputs(seed=0):
    import zlib

    import numpy as np

    out = dict(_drawn_inputs(seed))
    spreads = {'L0_attn_bin': (0.0, 0.1),
     'L0_attn_ln1_w': (1.0, 0.2),
     'L0_attn_ln1_b': (0.0, 0.1),
     'L0_attn_sc_lin': (1.0, 0.2),
     'L0_attn_ln2_w': (1.0, 0.2),
     'L0_attn_ln2_b': (0.0, 0.1),
     'L0_attn_b1': (0.0, 0.1),
     'L0_attn_b2': (0.0, 0.1),
     'L0_attn_lnl_w': (1.0, 0.2),
     'L0_attn_lnl_b': (0.0, 0.1),
     'L0_attn_bout': (0.0, 0.1),
     'L1_attn_D_param': (1.0, 0.2),
     'L1_attn_dt_ln_w': (1.0, 0.6),
     'L1_attn_B_ln_w': (1.0, 0.2),
     'L1_attn_C_ln_w': (1.0, 0.6)}
    factors = {'L0_ffn_lora_A': 8.0, 'L0_ffn_lora_B': 8.0, 'L1_attn_dt_proj_w': 3.737}
    for name, (base, spread) in spreads.items():
        noise = np.random.default_rng([zlib.crc32(name.encode()), seed]).standard_normal(out[name].shape)
        drawn = base * np.exp(spread * noise) if base else spread * noise
        out[name] = jnp.asarray(drawn.astype(out[name].dtype))
    for name, factor in factors.items():
        out[name] = (out[name] * factor).astype(out[name].dtype)
    return out
```

```python
from contextlib import ExitStack

import concourse.bass as bass
from concourse import mybir

F32 = mybir.dt.float32
I32 = mybir.dt.int32
ALU = mybir.AluOpType
ACT = mybir.ActivationFunctionType
AX_X = mybir.AxisListType.X

P = 128
W = 512
TOK = 1024
SEQ = 512
CH = 256
NCHUNK = TOK // CH
TB = CH // P
KT = W // P
DEPTH, DIM, DFF = 4, 64, 256
DIN, NS, RK = 1024, 16, 32
CT = DIN // P
HCT = CT // 2
INTER = 1792
NJ = INTER // P
SLOTS = 3
UNITS = 2 * NS
DRING = 4
BRING = 3
FINE, COARSE = 32, 16

CST = {}
_at = 0
for _name, _n in [("ident", 128), ("cen", 128), ("avg", 128), ("eps", 1), ("bin", 1),
                  ("ln1_w", 4), ("ln1_b", 4), ("scl", 4), ("ln2_w", 4), ("ln2_b", 4), ("b2", 4),
                  ("phz_re", 4), ("phz_im", 4), ("lc_re", 4), ("lc_im", 4), ("lnl_w", 1), ("lnl_b", 1),
                  ("b1", 8), ("dt_bias", 8), ("D", 8), ("conv_b", 8), ("conv_w", 32), ("A_log", 128)]:
    CST[_name] = (_at, _at + _n)
    _at += _n
NCST = _at
WP = {}
_at = 0
for _name, _n in [("wout", W), ("xp", CT * 64)]:
    WP[_name] = (_at, _at + _n)
    _at += _n
NWP = _at
NLW = DIN

AT = {
    0: ["R.attn_out", "P.z0", "Q.final_stats"],
    1: ["Q.final", "R.ln_a", "P.z1"],
    2: ["R.xn", "P.y_turn"],
    3: ["R.ffn0", "P.out_proj"],
    4: ["R.f_stats", "P.o_stats"],
    5: ["R.x2", "P.x3"],
    6: ["R.x2n", "P.x3n"],
    7: ["R.in01", "P.j0"],
    8: ["R.conv01", "P.j1", "P.j2"],
    9: ["R.in23", "P.j3"],
    10: ["R.conv23", "P.j4", "P.j5"],
    11: ["R.x_proj", "P.j6", "P.j7"],
    12: ["R.bc", "P.j8", "P.j9"],
    13: ["R.dt", "P.j10"],
    14: ["R.skip", "P.j11", "P.j12"],
    15: ["R.dtx", "P.j13", "P.y_done"],
}


def pieces(k, n):
    for name in AT[n]:
        who, what = name.split(".")
        c = k + {"R": 1, "P": -1, "Q": -2}[who]
        if 0 <= c < NCHUNK:
            yield what, c


def build(nc, a, out):
    ctx = ExitStack()
    with ctx:
        def sb(name, shape, dt=F32):
            return ctx.enter_context(nc.sbuf_tensor(name, shape, dt))

        def sem(name):
            return ctx.enter_context(nc.semaphore(name))

        PS = ctx.enter_context(nc.psum_tensor("PS", [P, 8, 512], F32))
        TR = (0, 1)
        MMB = (2, 3)
        GUB = (4, 5)
        YAB = (6, 7)

        cst = sb("cst", [P, NCST])
        wp = sb("wp", [P, NWP])
        lw = sb("lw", [RK, NLW])
        boutb = sb("boutb", [P, W])
        rmsb = sb("rmsb", [P, 64])
        XR = sb("XR", [P, TOK // P, W])
        HT = sb("HT", [P, 2, KT, CH])
        XF = sb("XF", [P, KT, CH])
        LR = sb("LR", [P, TB, W])
        LP = sb("LP", [P, TB, W])
        weff = sb("weff", [P, 4, W])
        diagD = sb("diagD", [P, CT, P])
        ring = sb("ring", [P, SLOTS, 2048])
        DT = sb("DT", [P, 2, CT, CH])
        DTX = sb("DTX", [P, 2, CT, CH])
        XI = sb("XI", [P, CT, CH + 4])
        XC = sb("XC", [P, CT, CH])
        TH = sb("TH", [P, 2, CH])
        Y = sb("Y", [P, 2, TB, DIN])
        BB = sb("BB", [P, 2, 2, CH])
        DA = sb("DA", [P, DRING, HCT, CH])
        DBX = sb("DBX", [P, BRING, HCT, CH])
        H = sb("H", [P, 2, HCT, CH])
        HC = sb("HC", [P, UNITS, HCT])
        G = sb("G", [P, 2, W])
        GT = sb("GT", [P, 2, CH])
        HJ = sb("HJ", [P, 2, CH])
        SP = sb("SP", [P, TB, 64])
        SPN = sb("SPN", [P, 2, TB, 64])
        DR = sb("DR", [48, CH])
        HN = sb("HN", [P, SEQ])
        BS = sb("BS", [P, 8, TB, 6])
        MV = sb("MV", [P, 8, TB, 2])
        VE = sb("VE", [P, 8, TB])
        RS = sb("RS", [P, 8, TB])
        MS = sb("MS", [P, 3, TB])
        MSR = sb("MSR", [P, 3, TB])
        half = sb("half", [P, 8])
        NA = sb("NA", [P, P])
        scb = sb("scb", [P, 12 * NJ])
        cv = sb("cv", [P, CT, 3])

        XN0 = DTX[:, :, :, :].rearrange("p a c t -> p (a c t)").rearrange("p (n w) -> p n w", w=W)
        XT0 = DT[:, :, :, :].rearrange("p b (k e) t -> p b k (e t)", k=KT)
        COS = Y[:, 0, :, :].rearrange("p a (b t) -> p (a b) t", t=SEQ)
        SIN = Y[:, 1, :, :].rearrange("p a (b t) -> p (a b) t", t=SEQ)
        wk = DA[:, :, :, :].rearrange("p a c t -> p (a c t)").rearrange("p (n t) -> p n t", t=SEQ)
        wk2 = DBX[:, :, :, :].rearrange("p a c t -> p (a c t)").rearrange("p (n t) -> p n t", t=SEQ)
        hid = XC[:, :, :].rearrange("p c t -> p (c t)").rearrange("p (n t) -> p n t", t=SEQ)
        hth = H[:, :, :, :].rearrange("p a c t -> p (a c t)").rearrange("p (n t) -> p n t", t=SEQ)
        Hs, SQ, RSTD, Z, S, MR, MI = (wk[:, i, :] for i in range(7))
        T0 = wk[:, 7, :]
        UR, VI, HB = (wk2[:, i, :] for i in range(3))
        xi4 = XI[:, :, :].rearrange("p c t -> p (c t)")
        codes = LR[:, :, :].rearrange("p a t -> p (a t)").bitcast(I32).rearrange("p (h o) -> p h o", h=2)
        fieldf = LP[:, :, :].rearrange("p a t -> p (a t)").rearrange("p (h o) -> p h o", h=2)
        packed = XF[:, :, :].rearrange("p k t -> p (k t)").bitcast(I32).rearrange("p (h o) -> p h o", h=2)
        bsc = HT[:, 1, :, :].rearrange("p k t -> p (k t)").rearrange("p (h o) -> p h o", h=2)
        dtmp = wk2[:, 3:5, :]
        gsb = sb("gsb", [P, 1])
        FR = sb("FR", [P, DEPTH, FINE + 1])
        FI = sb("FI", [P, DEPTH, FINE + 1])
        CR = sb("CR", [P, DEPTH, COARSE + 1])
        CI = sb("CI", [P, DEPTH, COARSE + 1])
        tt4 = [xi4[:, i * 512:(i + 1) * 512] for i in range(4)]
        pz = sb("pz", [P, 16, DEPTH])
        b1h = sb("b1h", [P, 8])

        def C(name, i=None):
            lo, hi = CST[name]
            return cst[:, lo:hi] if i is None else cst[:, lo + i:lo + i + 1]

        ident, cen_m, avg_m = C("ident"), C("cen"), C("avg")
        w1_at = BB[:, :, :, :].rearrange("p a b t -> p (a b t)")
        w2_at = G[:, 0, :]
        win_at = G[:, 1, 0:KT * DIM]
        winT = win_at.rearrange("p (k d) -> p k d", k=KT)
        w1T = w1_at.rearrange("p (l f) -> p l f", l=DEPTH)
        w2T = w2_at.rearrange("p (l f d) -> p l f d", l=DEPTH, f=2)
        woutT = wp[:, WP["wout"][0]:WP["wout"][1]]
        xpT = wp[:, WP["xp"][0]:WP["xp"][1]].rearrange("p (c e) -> p c e", c=CT)
        la_at = GT[0:16, :, :].rearrange("r a t -> r (a t)")
        loraA = la_at.rearrange("r (k i) -> r k i", k=4)
        loraB = HJ[0:16, :, :].rearrange("r a t -> r (a t)")
        dpT = lw[0:RK, :]
        convw = C("conv_w").rearrange("p (c k) -> p c k", c=CT)

        wsc = nc.dram_tensor("w_scaled", (NJ, P, 1536), F32, kind="Internal").ap()
        b_rows = nc.dram_tensor("b_rows", (NCHUNK, NS, CH), F32, kind="Internal").ap()

        names = """cst_in x_in0 x_in1 w_in deq_in misc_in
            pw0 pw1 pw2 scaled st0 st1 st2
            unit tables table_in half_set
            ln0_stats ln0_rstd xn0 xn0_turned xt0_copied h_in
            h_new centred squared variance rstd0 normed tanh0 hidden_sum hidden ffn_sum hn
            lora_prod weff_ready diag_ready na_ready na_exp
            ld0 ld1 ld2 slot_free
            attn_out a_read r1_stats r1_rstd xn turned_xn xt
            ffn0_prod ffn0_copied r3_stats r3_rstd x2n turned_x2 ht r2_stats r2_rstd r4_stats r4_rstd
            in_prod in_copied carry tail_kept conv conv_tanh xc
            xp_prod sp ms ms_rstd spn turned_bc dr b_stored
            dt_prod dt_split dt_log dt_ready dtx
            skip_prod skip_copied
            bb0 bb1 dbx decay states state_kept turned_h y_sum
            z_prod z_tanh z_read gated turned_y yt out_prod out_copied
            p5_stats p5_rstd p6_stats p6_rstd x3n turned_x3 xf gu_prod gate_tanh gu_read hj w2_prod y_copied
            p7_stats p7_rstd result stored_out
            dve_step act_step pool_step""".split()
        s = {n: sem(n) for n in names}

        readers = [("xt0_copied", i + 1) for i in range(8)]
        readers += [("weff_ready", i + 1) for i in range(4)]
        for k in range(-1, NCHUNK + 1):
            for n in range(NS):
                for what, c in pieces(k, n):
                    if what == "attn_out":
                        readers += [("a_read", TB * c + i + 1) for i in range(TB)]
                    elif what in ("z0", "z1"):
                        readers += [("z_read", 4 * c + 2 * int(what[1]) + i + 1) for i in range(2)]
                    elif what == "xn":
                        readers += [("xt", TB * c + i + 1) for i in range(TB)]
                    elif what == "y_turn":
                        readers += [("yt", 4 * c + i + 1) for i in range(4)]
                    elif what == "ffn0":
                        readers += [("ffn0_copied", TB * c + i + 1) for i in range(TB)]
                    elif what == "out_proj":
                        readers += [("out_copied", TB * c + i + 1) for i in range(TB)]
                    elif what == "x2n":
                        readers += [("ht", TB * c + i + 1) for i in range(TB)]
                    elif what == "x3n":
                        readers += [("xf", TB * c + i + 1) for i in range(TB)]
                    elif what in ("in01", "in23"):
                        readers += [("in_copied", 4 * c + int(what[2]) + i + 1) for i in range(2)]
                    elif what == "x_proj":
                        readers += [("sp", c + 1)]
                    elif what == "bc":
                        readers += [("dr", c + 1)]
                    elif what == "dt":
                        readers += [("dt_split", 4 * c + i + 1) for i in range(4)]
                    elif what == "skip":
                        readers += [("skip_copied", 4 * c + i + 1) for i in range(4)]
        mm_index = {r: i for i, r in enumerate(readers)}

        def bank(name, value):
            return PS[:, MMB[mm_index[(name, value)] % 2], :]

        stream = []
        for k in range(-1, NCHUNK + 1):
            for n in range(NS):
                for what, c in pieces(k, n):
                    if what in ("z0", "z1"):
                        stream.append((k, n, "ip", c, 2 + int(what[1])))
                    elif what == "out_proj":
                        stream += [(k, n, "op", c, 0), (k, n, "op", c, 1)]
                    elif what in ("in01", "in23"):
                        stream.append((k, n, "ip", c, int(what[2]) // 2))
                    elif what[0] == "j":
                        stream.append((k, n, "w", c, int(what[1:])))
        item = {(kind, c, i): q for q, (_, _, kind, c, i) in enumerate(stream)}

        def loaded(kind, c, i):
            q = item[(kind, c, i)]
            return q % SLOTS, s[f"ld{q % SLOTS}"], 16 * (q // SLOTS + 1)

        block = ctx.enter_context(nc.Block())

        @block.sync
        def _(sp):
            sp.dma_start(cst[:, :], a["cst"]).then_inc(s["cst_in"], 16)
            for b in range(2):
                sp.dma_start(XR[:, 4 * b:4 * b + 4, :],
                             a["x"].rearrange("(n p) v -> p n v", p=P)[:, 4 * b:4 * b + 4, :]
                             ).then_inc(s[f"x_in{b}"], 16)
            for dst, n in ((w1_at, "w1"), (w2_at, "w2"), (win_at, "win"), (wp[:, :], "wp")):
                sp.dma_start(dst, a[n]).then_inc(s["w_in"], 16)
            sp.dma_start(packed, a["packed"].rearrange("h p o -> p h o")).then_inc(s["deq_in"], 16)
            for g in range(2):
                sp.dma_start(bsc[:, g, :], a["bs"][16 * g:16 * g + 16, None, :].to_broadcast((16, 8, W))
                             ).then_inc(s["deq_in"], 16)
            sp.dma_start(gsb[:, :], a["gs"][None, :].to_broadcast((P, 1))).then_inc(s["deq_in"], 16)
            for dst, n in ((lw[:, :], "lw"), (la_at, "la"), (loraB, "lb")):
                sp.dma_start(dst, a[n]).then_inc(s["deq_in"], 16)
            sp.dma_start(scb[:, :], a["sc"][None, :].to_broadcast((P, 12 * NJ))).then_inc(s["misc_in"], 16)
            sp.dma_start(boutb[:, :], a["bout"][None, :].to_broadcast((P, W))).then_inc(s["misc_in"], 16)
            sp.dma_start(rmsb[:, :], a["rms"][None, :].to_broadcast((P, 64))).then_inc(s["misc_in"], 16)
            for j in range(NJ + 1):
                if j < NJ:
                    if j >= SLOTS:
                        sp.wait_ge(s[f"st{j % SLOTS}"], 16 * (j // SLOTS))
                    sp.dma_start(ring[:, j % SLOTS, 0:1536], a["wq"][j]).then_inc(s[f"pw{j % SLOTS}"], 16)
                if j >= 1:
                    sp.wait_ge(s["scaled"], j)
                    sp.dma_start(wsc[j - 1], ring[:, (j - 1) % SLOTS, 0:1536]).then_inc(s[f"st{(j - 1) % SLOTS}"], 16)
            for i in range(SLOTS):
                sp.wait_ge(s[f"st{i}"], 16 * len(range(i, NJ, SLOTS)))

            def fetch(q):
                _, _, kind, c, i = stream[q]
                if q >= SLOTS:
                    sp.wait_ge(s["slot_free"], q - SLOTS + 1)
                dst = ring[:, q % SLOTS, :]
                src = {"ip": a["ip"], "op": a["op"], "w": wsc}[kind][i]
                if kind == "w":
                    dst = dst[:, 0:1536]
                sp.dma_start(dst, src).then_inc(s[f"ld{q % SLOTS}"], 16)

            def spread_b(c, m):
                g = 8 * c + m
                if m == 0:
                    sp.wait_ge(s["b_stored"], 16 * (c + 1))
                if g >= 2:
                    sp.wait_ge(s["dbx"], 4 * (g - 1))
                sp.dma_start(BB[:, g % 2, :, :], b_rows[c, 2 * m:2 * m + 2, :][None, :, :].to_broadcast((P, 2, CH))
                             ).then_inc(s[f"bb{g % 2}"], 16)

            q = 0
            for k in range(-1, NCHUNK + 1):
                for n in range(NS):
                    if k == -1 and n == 0:
                        for _ in range(SLOTS):
                            fetch(q)
                            q += 1
                    if 0 <= k < NCHUNK and n % 2 == 0 and n // 2 + 2 < NS // 2:
                        spread_b(k, n // 2 + 2)
                    while q < len(stream) and stream[q - SLOTS][0:2] <= (k, n):
                        fetch(q)
                        q += 1
                    for what, c in pieces(k, n):
                        if what == "bc":
                            sp.wait_ge(s["dr"], c + 1)
                            sp.dma_start(b_rows[c], DR[RK:RK + NS, :]).then_inc(s["b_stored"], 16)
                        if what == "skip":
                            spread_b(c, 0)
                        if what == "dtx":
                            spread_b(c, 1)
                        if what == "final":
                            sp.wait_ge(s["result"], TB * (c + 1))
                            sp.dma_start(out.rearrange("(n p) v -> p n v", p=P)[:, TB * c:TB * c + TB, :],
                                         XR[:, TB * c:TB * c + TB, :]).then_inc(s["stored_out"], 16)
            c = NCHUNK - 1
            sp.wait_ge(s["result"], TB * (c + 1))
            sp.dma_start(out.rearrange("(n p) v -> p n v", p=P)[:, TB * c:TB * c + TB, :],
                         XR[:, TB * c:TB * c + TB, :]).then_inc(s["stored_out"], 16)
            sp.wait_ge(s["stored_out"], 16 * NCHUNK)

        @block.tensor
        def _(pe):
            def turn(dst, src, srcs=4):
                for i in range(srcs):
                    last = pe.transpose(dst[:, i * P:(i + 1) * P], src(i), ident)
                return last

            def free(name, value):
                i = mm_index[(name, value)]
                if i >= 2:
                    pe.wait_ge(s[readers[i - 2][0]], readers[i - 2][1])

            pe.wait_ge(s["cst_in"], 16)
            for t in range(TOK // P):
                pe.wait_ge(s["xn0"], t + 1)
                free("xt0_copied", t + 1)
                turn(bank("xt0_copied", t + 1), lambda i: XN0[:, t, i * P:(i + 1) * P]).then_inc(s["xn0_turned"], 1)
            pe.wait_ge(s["w_in"], 64)
            pe.wait_ge(s["xt0_copied"], 8)
            for b in range(2):
                for kk in range(KT):
                    last = pe.matmul(PS[64 * b:64 * b + 64, 0, :], winT[:, kk, :], XT0[:, b, kk, :],
                                     start=kk == 0, stop=kk == KT - 1)
            last.then_inc(s["h_in"], 1)
            def norm0(i):
                pe.wait_ge(s["h_new"], i + 1)
                pe.matmul(PS[:, 0, :], cen_m, Hs, start=True, stop=True).then_inc(s["centred"], 1)
                pe.wait_ge(s["squared"], i + 1)
                pe.matmul(PS[:, 1, :], avg_m, SQ, start=True, stop=True).then_inc(s["variance"], 1)

            for l in range(DEPTH):
                norm0(2 * l)
                if l == 1:
                    pe.wait_ge(s["deq_in"], 16 * 7)
                    for i in range(4):
                        free("weff_ready", i + 1)
                        pe.matmul(bank("weff_ready", i + 1), loraA[:, i, :], loraB, start=True, stop=True
                                  ).then_inc(s["lora_prod"], 1)
                norm0(2 * l + 1)
                pe.wait_ge(s["normed"], 3 * l + 3)
                for b in range(2):
                    for f in range(2):
                        if l:
                            pe.wait_ge(s["hidden"], 4 * (l - 1) + 2 * b + f + 1)
                        pe.matmul(PS[:, 4 + 2 * b + f, :], w1T[64 * b:64 * b + 64, l, f * P:(f + 1) * P],
                                  Z[64 * b:64 * b + 64, :], start=True, stop=True).then_inc(s["hidden_sum"], 1)
                for b in range(2):
                    for f in range(2):
                        pe.wait_ge(s["hidden"], 4 * l + 2 * b + f + 1)
                        last = pe.matmul(PS[64 * b:64 * b + 64, 1, :], w2T[:, l, f, :], hid[:, 2 * b + f, :],
                                         start=f == 0, stop=f == 1)
                last.then_inc(s["ffn_sum"], 1)
            norm0(2 * DEPTH)
            pe.wait_ge(s["hn"], 1)

            def scan_turn(k, n):
                for u in (2 * n, 2 * n + 1):
                    g = UNITS * k + u
                    pe.wait_ge(s["states"], g + 1)
                    for tb in range(TB):
                        if g >= 1:
                            pe.wait_ge(s["y_sum"], 2 * (g - 1) + tb + 1)
                        turn(PS[:, TR[tb], :], lambda i: H[:, g % 2, i, tb * P:(tb + 1) * P]
                             ).then_inc(s["turned_h"], 1)

            def ffn_out(c, j):
                slot, _, _ = loaded("w", c, j)
                pe.wait_ge(s["hj"], NJ * c + j + 1)
                if j == 0 and c >= 1:
                    pe.wait_ge(s["y_copied"], TB * c)
                for tb in range(TB):
                    last = pe.matmul(PS[:, YAB[tb], :], HJ[:, j % 2, tb * P:(tb + 1) * P],
                                     ring[:, slot, 1024:1536], start=j == 0, stop=j == NJ - 1)
                last.then_inc(s["slot_free"], 1)

            for k in range(-1, NCHUNK + 1):
                for n in range(NS):
                    if 0 <= k < NCHUNK:
                        scan_turn(k, n)
                    for what, c in pieces(k, n):
                        b, cp = c // 2, c % 2
                        if what == "attn_out":
                            for tb in range(TB):
                                free("a_read", TB * c + tb + 1)
                                t0 = (c % 2) * CH + tb * P
                                pe.matmul(bank("a_read", TB * c + tb + 1), HN[64 * b:64 * b + 64, t0:t0 + P],
                                          woutT[64 * b:64 * b + 64, :], start=True, stop=True
                                          ).then_inc(s["attn_out"], 1)
                        elif what == "xn":
                            for tb in range(TB):
                                pe.wait_ge(s["xn"], TB * c + tb + 1)
                                free("xt", TB * c + tb + 1)
                                turn(bank("xt", TB * c + tb + 1),
                                     lambda i: LR[:, tb, 256 * (i // 2) + i % 2:256 * (i // 2) + 256:2]
                                     ).then_inc(s["turned_xn"], 1)
                        elif what == "ffn0":
                            pe.wait_ge(s["weff_ready"], 4)
                            for tb in range(TB):
                                pe.wait_ge(s["xt"], TB * c + tb + 1)
                                free("ffn0_copied", TB * c + tb + 1)
                                for i in range(4):
                                    last = pe.matmul(bank("ffn0_copied", TB * c + tb + 1),
                                                     HT[:, c % 2, i, tb * P:(tb + 1) * P], weff[:, i, :],
                                                     start=i == 0, stop=i == 3)
                                last.then_inc(s["ffn0_prod"], 1)
                        elif what == "x2n":
                            for tb in range(TB):
                                pe.wait_ge(s["x2n"], TB * c + tb + 1)
                                free("ht", TB * c + tb + 1)
                                turn(bank("ht", TB * c + tb + 1), lambda i: LR[:, tb, i * P:(i + 1) * P]
                                     ).then_inc(s["turned_x2"], 1)
                        elif what in ("in01", "in23"):
                            h = int(what[2]) // 2
                            slot, ld, v = loaded("ip", c, h)
                            pe.wait_ge(ld, v)
                            pe.wait_ge(s["ht"], TB * (c + 1))
                            wi = ring[:, slot, :].rearrange("p (k n) -> p k n", k=KT)
                            for m in (2 * h, 2 * h + 1):
                                free("in_copied", 4 * c + m + 1)
                                dst = bank("in_copied", 4 * c + m + 1)
                                for e in range(2):
                                    o = ((2 * m + e) % HCT) * P
                                    for kk in range(KT):
                                        last = pe.matmul(dst[:, e * CH:(e + 1) * CH], wi[:, kk, o:o + P],
                                                         HT[:, c % 2, kk, :], start=kk == 0, stop=kk == KT - 1)
                                if m % 2 == 1:
                                    last.then_inc(s["slot_free"], 1)
                                    pe.wait_ge(s["slot_free"], item[("ip", c, h)] + 1)
                                    pe.nop().then_inc(s["in_prod"], 1)
                                else:
                                    last.then_inc(s["in_prod"], 1)
                        elif what == "x_proj":
                            pe.wait_ge(s["xc"], 4 * (c + 1))
                            free("sp", c + 1)
                            dst = bank("sp", c + 1)
                            for tb in range(TB):
                                for i in range(CT):
                                    last = pe.matmul(dst[:, 64 * tb:64 * tb + 64], XC[:, i, tb * P:(tb + 1) * P],
                                                     xpT[:, i, :], start=i == 0, stop=i == CT - 1)
                            last.then_inc(s["xp_prod"], 1)
                        elif what == "bc":
                            pe.wait_ge(s["spn"], 6 * (c + 1))
                            free("dr", c + 1)
                            dst = bank("dr", c + 1)
                            for tb in range(TB):
                                last = pe.transpose(dst[0:48, tb * P:(tb + 1) * P], SPN[:, c % 2, tb, 0:48], ident)
                            last.then_inc(s["turned_bc"], 1)
                        elif what == "dt":
                            pe.wait_ge(s["dr"], c + 1)
                            for m in range(4):
                                free("dt_split", 4 * c + m + 1)
                                dst = bank("dt_split", 4 * c + m + 1)
                                for e in range(2):
                                    o = (2 * m + e) * P
                                    last = pe.matmul(dst[:, e * CH:(e + 1) * CH], dpT[:, o:o + P], DR[0:RK, :],
                                                     start=True, stop=True)
                                last.then_inc(s["dt_prod"], 1)
                        elif what == "skip":
                            pe.wait_ge(s["diag_ready"], 1)
                            for m in range(4):
                                tb, h = m // 2, m % 2
                                free("skip_copied", 4 * c + m + 1)
                                dst = bank("skip_copied", 4 * c + m + 1)
                                for i in range(HCT):
                                    last = pe.matmul(dst[:, i * P:(i + 1) * P],
                                                     XC[:, HCT * h + i, tb * P:(tb + 1) * P],
                                                     diagD[:, HCT * h + i, :], start=True, stop=True)
                                last.then_inc(s["skip_prod"], 1)
                        elif what in ("z0", "z1"):
                            h = int(what[1])
                            slot, ld, v = loaded("ip", c, 2 + h)
                            pe.wait_ge(ld, v)
                            wi = ring[:, slot, :].rearrange("p (k n) -> p k n", k=KT)
                            for tb in range(TB):
                                r = 4 * c + 2 * h + tb + 1
                                free("z_read", r)
                                for kk in range(KT):
                                    last = pe.matmul(bank("z_read", r), HT[:, c % 2, kk, tb * P:(tb + 1) * P],
                                                     wi[:, kk, :], start=kk == 0, stop=kk == KT - 1)
                                if tb == TB - 1:
                                    last.then_inc(s["slot_free"], 1)
                                    pe.wait_ge(s["slot_free"], item[("ip", c, 2 + h)] + 1)
                                    pe.nop().then_inc(s["z_prod"], 1)
                                else:
                                    last.then_inc(s["z_prod"], 1)
                        elif what == "y_turn":
                            for m in range(4):
                                tb, h = m // 2, m % 2
                                pe.wait_ge(s["gated"], 4 * c + 2 * h + tb + 1)
                                free("yt", 4 * c + m + 1)
                                turn(bank("yt", 4 * c + m + 1),
                                     lambda i: Y[:, c % 2, tb, h * 512 + i * P:h * 512 + (i + 1) * P]
                                     ).then_inc(s["turned_y"], 1)
                        elif what == "out_proj":
                            for h in range(2):
                                _, ld, v = loaded("op", c, h)
                                pe.wait_ge(ld, v)
                            for tb in range(TB):
                                pe.wait_ge(s["yt"], 4 * c + 2 * tb + 2)
                                free("out_copied", TB * c + tb + 1)
                                for i in range(CT):
                                    wo = ring[:, loaded("op", c, i // HCT)[0], :].rearrange("p (k n) -> p k n", k=HCT)
                                    last = pe.matmul(bank("out_copied", TB * c + tb + 1),
                                                     XC[:, i, tb * P:(tb + 1) * P], wo[:, i % HCT, :],
                                                     start=i == 0, stop=i == CT - 1)
                                last.then_inc(s["out_prod"], 1)
                            pe.wait_ge(s["out_prod"], TB * (c + 1))
                            pe.nop().then_inc(s["slot_free"], 1)
                            pe.nop().then_inc(s["slot_free"], 1)
                        elif what == "x3n":
                            for tb in range(TB):
                                pe.wait_ge(s["x3n"], TB * c + tb + 1)
                                free("xf", TB * c + tb + 1)
                                turn(bank("xf", TB * c + tb + 1), lambda i: LP[:, tb, i * P:(i + 1) * P]
                                     ).then_inc(s["turned_x3"], 1)
                        elif what[0] == "j":
                            j = int(what[1:])
                            slot, ld, v = loaded("w", c, j)
                            pe.wait_ge(ld, v)
                            pe.wait_ge(s["xf"], TB * (c + 1))
                            g = NJ * c + j
                            if g >= 2:
                                pe.wait_ge(s["hj"], g - 1)
                            for e in range(2):
                                for kk in range(KT):
                                    last = pe.matmul(PS[:, GUB[g % 2], e * CH:(e + 1) * CH],
                                                     ring[:, slot, (e * KT + kk) * P:(e * KT + kk + 1) * P],
                                                     XF[:, kk, :], start=kk == 0, stop=kk == KT - 1)
                            last.then_inc(s["gu_prod"], 1)
                            ffn_out(c, j)
                        elif what == "y_done":
                            pe.wait_ge(s["slot_free"], item[("w", c, NJ - 1)] + 1)
                            pe.nop().then_inc(s["w2_prod"], 1)

        @block.scalar
        def _(act):
            step = [0]

            def link(ins):
                step[0] += 1
                ins.then_inc(s["act_step"], 1)
                act.wait_ge(s["act_step"], step[0])

            act.wait_ge(s["cst_in"], 16)
            link(act.activation(NA[:, :], C("A_log"), ACT.Exp))
            act.mul(NA[:, :], NA[:, :], -1.0).then_inc(s["na_exp"], 1)
            act.wait_ge(s["unit"], 1)
            link(act.activation(pz[:, 1, :], pz[:, 0, :], ACT.Ln))
            act.activation(pz[:, 1, :], pz[:, 1, :], ACT.Exp, scale=-0.5).then_inc(s["table_in"], 1)
            act.wait_ge(s["unit"], 2)
            act.activation(pz[:, 8, :], pz[:, 7, :], ACT.Exp, scale=-2.0).then_inc(s["table_in"], 1)
            for t in range(TOK // P):
                act.wait_ge(s["xn0_turned"], t + 1)
                act.activation(XT0[:, t // 4, :, (t % 4) * P:(t % 4 + 1) * P],
                               bank("xt0_copied", t + 1).rearrange("p (k t) -> p k t", k=KT), ACT.Copy
                               ).then_inc(s["xt0_copied"], 1)

            def norm0(i):
                act.wait_ge(s["centred"], i + 1)
                act.activation(SQ, PS[:, 0, :], ACT.Square).then_inc(s["squared"], 1)
                act.wait_ge(s["variance"], i + 1)
                link(act.activation(RSTD, PS[:, 1, :], ACT.Ln, bias=C("eps")))
                act.activation(RSTD, RSTD, ACT.Exp, scale=-0.5).then_inc(s["rstd0"], 1)

            for l in range(DEPTH):
                norm0(2 * l)
                act.wait_ge(s["normed"], 3 * l + 2)
                act.activation(T0, Z, ACT.Tanh, scale=0.5).then_inc(s["tanh0"], 1)
                norm0(2 * l + 1)
                for m in range(4):
                    act.wait_ge(s["hidden_sum"], 4 * l + m + 1)
                    act.activation(hth[:, m, :], PS[:, 4 + m, :], ACT.Tanh, scale=0.5,
                                   bias=b1h[:, 2 * l + m % 2:2 * l + m % 2 + 1]).then_inc(s["tanh0"], 1)
            norm0(2 * DEPTH)

            def decays(g):
                k, u = g // UNITS, g % UNITS
                n, h = u // 2, u % 2
                if u == 0:
                    act.wait_ge(s["dt_ready"], k + 1)
                    if k == 0:
                        act.wait_ge(s["na_exp"], 1)
                if g >= DRING:
                    act.wait_ge(s["states"], g - DRING + 1)
                for i in range(HCT):
                    ct = HCT * h + i
                    last = act.activation(DA[:, g % DRING, i, :], DT[:, k % 2, ct, :], ACT.Exp,
                                          scale=NA[:, ct * NS + n:ct * NS + n + 1])
                last.then_inc(s["decay"], 1)

            for k in range(-1, NCHUNK + 1):
                for n in range(NS):
                    if 0 <= k < NCHUNK:
                        if n == 0:
                            decays(UNITS * k)
                            decays(UNITS * k + 1)
                        if n + 1 < NS:
                            decays(UNITS * k + 2 * n + 2)
                            decays(UNITS * k + 2 * n + 3)
                    for what, c in pieces(k, n):
                        if what == "xn":
                            for tb in range(TB):
                                act.wait_ge(s["turned_xn"], TB * c + tb + 1)
                                if c >= 2 and tb == 0:
                                    act.wait_ge(s["z_prod"], 4 * (c - 1))
                                if c == 1 and tb == 0:
                                    act.wait_ge(s["weff_ready"], 4)
                                act.activation(HT[:, c % 2, :, tb * P:(tb + 1) * P],
                                               bank("xt", TB * c + tb + 1).rearrange("p (k t) -> p k t", k=KT),
                                               ACT.Copy).then_inc(s["xt"], 1)
                        elif what == "ffn0":
                            for tb in range(TB):
                                act.wait_ge(s["ffn0_prod"], TB * c + tb + 1)
                                act.activation(LR[:, tb, :], bank("ffn0_copied", TB * c + tb + 1), ACT.Copy
                                               ).then_inc(s["ffn0_copied"], 1)
                        elif what == "x2n":
                            for tb in range(TB):
                                act.wait_ge(s["turned_x2"], TB * c + tb + 1)
                                act.wait_ge(s["ffn0_prod"], TB * (c + 1))
                                act.activation(HT[:, c % 2, :, tb * P:(tb + 1) * P],
                                               bank("ht", TB * c + tb + 1).rearrange("p (k t) -> p k t", k=KT),
                                               ACT.Copy).then_inc(s["ht"], 1)
                        elif what in ("in01", "in23"):
                            for m in (int(what[2]), int(what[2]) + 1):
                                act.wait_ge(s["in_prod"], 4 * c + m + 1)
                                if m == 0:
                                    act.wait_ge(s["carry"], c + 1)
                                act.activation(XI[:, 2 * m:2 * m + 2, 3:3 + CH],
                                               bank("in_copied", 4 * c + m + 1).rearrange("p (e t) -> p e t", e=2),
                                               ACT.Copy).then_inc(s["in_copied"], 1)
                        elif what in ("conv01", "conv23"):
                            for m in (int(what[4]), int(what[4]) + 1):
                                act.wait_ge(s["conv"], 4 * c + m + 1)
                                act.activation(TH[:, :, :], XC[:, 2 * m:2 * m + 2, :], ACT.Tanh, scale=0.5
                                               ).then_inc(s["conv_tanh"], 1)
                        elif what == "x_proj":
                            act.wait_ge(s["xp_prod"], c + 1)
                            act.activation(SP[:, :, :],
                                           bank("sp", c + 1)[:, 0:64 * TB].rearrange("p (b e) -> p b e", b=TB),
                                           ACT.Copy).then_inc(s["sp"], 1)
                        elif what == "bc":
                            act.wait_ge(s["turned_bc"], c + 1)
                            if c:
                                act.wait_ge(s["b_stored"], 16 * c)
                                act.wait_ge(s["dt_prod"], 4 * c)
                            act.activation(DR[:, :], bank("dr", c + 1)[0:48, 0:CH], ACT.Copy).then_inc(s["dr"], 1)
                        elif what == "dt":
                            if c >= 2:
                                act.wait_ge(s["states"], UNITS * (c - 1))
                            act.wait_ge(s["tail_kept"], c + 1)
                            for m in range(4):
                                act.wait_ge(s["dt_prod"], 4 * c + m + 1)
                                src = bank("dt_split", 4 * c + m + 1)
                                for e in range(2):
                                    ct = 2 * m + e
                                    act.activation(XI[:, ct, 3:3 + CH], src[:, e * CH:(e + 1) * CH], ACT.Abs,
                                                   bias=C("dt_bias", ct))
                                    last = act.activation(DT[:, c % 2, ct, :], src[:, e * CH:(e + 1) * CH],
                                                          ACT.Relu, bias=C("dt_bias", ct))
                                last.then_inc(s["dt_split"], 1)
                            act.wait_ge(s["dt_split"], 4 * (c + 1))
                            link(act.activation(XI[:, :, 3:3 + CH], XI[:, :, 3:3 + CH], ACT.Exp, scale=-1.0))
                            act.activation(XI[:, :, 3:3 + CH], XI[:, :, 3:3 + CH], ACT.Ln, bias=1.0
                                           ).then_inc(s["dt_log"], 1)
                        elif what == "skip":
                            for m in range(4):
                                act.wait_ge(s["skip_prod"], 4 * c + m + 1)
                                if m == 0 and c >= 2:
                                    act.wait_ge(s["turned_y"], 4 * (c - 1))
                                act.activation(Y[:, c % 2, m // 2, (m % 2) * 512:(m % 2) * 512 + 512],
                                               bank("skip_copied", 4 * c + m + 1), ACT.Copy
                                               ).then_inc(s["skip_copied"], 1)
                        elif what in ("z0", "z1"):
                            for tb in range(TB):
                                r = 4 * c + 2 * int(what[1]) + tb + 1
                                act.wait_ge(s["z_prod"], r)
                                if r > 2:
                                    act.wait_ge(s["gated"], r - 2)
                                act.activation(G[:, r % 2, :], bank("z_read", r), ACT.Tanh, scale=0.5
                                               ).then_inc(s["z_tanh"], 1)
                        elif what == "y_turn":
                            for m in range(4):
                                act.wait_ge(s["turned_y"], 4 * c + m + 1)
                                if m == 0:
                                    d = min(c + 1, NCHUNK - 1)
                                    act.wait_ge(s["skip_prod"], 4 * (d + 1))
                                    act.wait_ge(s["dtx"], d + 1)
                                tb, h = m // 2, m % 2
                                act.activation(XC[:, HCT * h:HCT * h + HCT, tb * P:(tb + 1) * P],
                                               bank("yt", 4 * c + m + 1).rearrange("p (k t) -> p k t", k=HCT),
                                               ACT.Copy).then_inc(s["yt"], 1)
                        elif what == "out_proj":
                            for tb in range(TB):
                                act.wait_ge(s["out_prod"], TB * c + tb + 1)
                                if c and tb == 0:
                                    act.wait_ge(s["result"], TB * c)
                                if c == 0 and tb == 0:
                                    act.wait_ge(s["weff_ready"], 4)
                                act.activation(LP[:, tb, :], bank("out_copied", TB * c + tb + 1), ACT.Copy
                                               ).then_inc(s["out_copied"], 1)
                        elif what == "x3n":
                            for tb in range(TB):
                                act.wait_ge(s["turned_x3"], TB * c + tb + 1)
                                if c and tb == 0:
                                    act.wait_ge(s["gu_prod"], NJ * c)
                                act.activation(XF[:, :, tb * P:(tb + 1) * P],
                                               bank("xf", TB * c + tb + 1).rearrange("p (k t) -> p k t", k=KT),
                                               ACT.Copy).then_inc(s["xf"], 1)
                        elif what[0] == "j":
                            g = NJ * c + int(what[1:])
                            act.wait_ge(s["gu_prod"], g + 1)
                            if g >= 2:
                                act.wait_ge(s["hj"], g - 1)
                            act.activation(GT[:, g % 2, :], PS[:, GUB[g % 2], 0:CH], ACT.Tanh, scale=0.5
                                           ).then_inc(s["gate_tanh"], 1)
                        elif what == "y_done":
                            act.wait_ge(s["w2_prod"], c + 1)
                            for tb in range(TB):
                                act.activation(LP[:, tb, :], PS[:, YAB[tb], :], ACT.Copy).then_inc(s["y_copied"], 1)

        @block.gpsimd
        def _(pool):
            step = [0]

            def link(ins):
                step[0] += 1
                ins.then_inc(s["pool_step"], 1)
                pool.wait_ge(s["pool_step"], step[0])

            link(pool.memset(half[:, :], -0.5))
            pool.memset(cv[:, :, :], 0.0)
            link(pool.memset(HC[:, :, :], 0.0))
            pool.wait_ge(s["cst_in"], 16)

            def rstd(st, v, dst, src, n, done):
                pool.wait_ge(s[st], v)
                pool.tensor_tensor(dst, src, half[:, 0:n], ALU.pow).then_inc(s[done], 1)

            for i in range(4):
                rstd("ln0_stats", i + 1, RS[:, i, :], VE[:, i, :], TB, "ln0_rstd")
            for ct in range(CT):
                last = pool.tensor_scalar(diagD[:, ct, :], ident, C("D", ct), None, ALU.mult)
            last.then_inc(s["diag_ready"], 1)
            pool.wait_ge(s["misc_in"], 48)
            for j in range(NJ):
                pool.wait_ge(s[f"pw{j % SLOTS}"], 16 * (j // SLOTS + 1))
                w = ring[:, j % SLOTS, 0:1536].rearrange("p (q m) -> p q m", q=12)
                pool.tensor_tensor(w, w, scb[:, 12 * j:12 * j + 12][:, :, None].to_broadcast((P, 12, P)), ALU.mult
                                   ).then_inc(s["scaled"], 1)

            def inputs(g):
                k, u = g // UNITS, g % UNITS
                n, h = u // 2, u % 2
                pair = 8 * k + n // 2
                if u == 0:
                    pool.wait_ge(s["dtx"], k + 1)
                if u % 4 == 0:
                    pool.wait_ge(s[f"bb{pair % 2}"], 16 * (pair // 2 + 1))
                if g >= BRING:
                    pool.wait_ge(s["states"], g - BRING + 1)
                pool.tensor_tensor(DBX[:, g % BRING, :, :], DTX[:, k % 2, HCT * h:HCT * h + HCT, :],
                                   BB[:, pair % 2, n % 2, :][:, None, :].to_broadcast((P, HCT, CH)), ALU.mult
                                   ).then_inc(s["dbx"], 1)

            def keep(g):
                pool.wait_ge(s["states"], g + 1)
                pool.tensor_copy(HC[:, g % UNITS, :], H[:, g % 2, :, CH - 1]).then_inc(s["state_kept"], 1)

            for k in range(-1, NCHUNK + 1):
                for n in range(NS):
                    if 0 <= k < NCHUNK:
                        if n == 0:
                            inputs(UNITS * k)
                            inputs(UNITS * k + 1)
                        for u in (2 * n, 2 * n + 1):
                            if u + 2 < UNITS:
                                inputs(UNITS * k + u + 2)
                            keep(UNITS * k + u)
                    for what, c in pieces(k, n):
                        if what == "attn_out":
                            rstd("r1_stats", c + 1, RS[:, 0, :], VE[:, 0, :], TB, "r1_rstd")
                        elif what == "ln_a":
                            rstd("r2_stats", c + 1, RS[:, 1, :], VE[:, 1, :], TB, "r2_rstd")
                        elif what == "f_stats":
                            rstd("r3_stats", c + 1, RS[:, 2, :], VE[:, 2, :], TB, "r3_rstd")
                        elif what == "x2":
                            rstd("r4_stats", c + 1, RS[:, 3, :], VE[:, 3, :], TB, "r4_rstd")
                        elif what == "o_stats":
                            rstd("p5_stats", c + 1, RS[:, 4, :], VE[:, 4, :], TB, "p5_rstd")
                        elif what == "x3":
                            rstd("p6_stats", c + 1, RS[:, 5, :], VE[:, 5, :], TB, "p6_rstd")
                        elif what == "final_stats":
                            rstd("p7_stats", c + 1, RS[:, 6, :], VE[:, 6, :], TB, "p7_rstd")
                        elif what == "in01":
                            if c:
                                pool.wait_ge(s["dt_ready"], c)
                            pool.tensor_scalar(XI[:, :, 0:3], cv[:, :, :], 0.0 if c % 2 == 0 else 1.0, None, ALU.mult
                                               ).then_inc(s["carry"], 1)
                        elif what == "dt":
                            pool.wait_ge(s["conv"], 4 * (c + 1))
                            pool.tensor_copy(cv[:, :, :], XI[:, :, CH:CH + 3]).then_inc(s["tail_kept"], 1)
                        elif what == "bc":
                            rstd("ms", c + 1, MSR[:, :, :].rearrange("p a b -> p (a b)"),
                                 MS[:, :, :].rearrange("p a b -> p (a b)"), 3 * TB, "ms_rstd")
            rstd("p7_stats", NCHUNK, RS[:, 6, :], VE[:, 6, :], TB, "p7_rstd")

        @block.vector
        def _(dve):
            step = [0]

            def mark(ins):
                step[0] += 1
                ins.then_inc(s["dve_step"], 1)

            def settle():
                dve.wait_ge(s["dve_step"], step[0])

            def link(ins):
                mark(ins)
                settle()

            def tt(o, x, y, op):
                return dve.tensor_tensor(o, x, y, op)

            def ts(o, x, s1, s2, op0, op1=None):
                return dve.tensor_scalar(o, x, s1, s2, op0) if op1 is None else dve.tensor_scalar(o, x, s1, s2, op0, op1)

            def stt(o, x, sc, y, op0, op1):
                return dve.scalar_tensor_tensor(o, x, sc, y, op0, op1)

            def stats(src, i, eps, done):
                for tb in range(TB):
                    mark(dve.bn_stats(BS[:, i, tb, :], src(tb)))
                settle()
                for tb in range(TB):
                    mark(dve.bn_aggr(MV[:, i, tb, :], BS[:, i, tb, :]))
                settle()
                ts(VE[:, i, :], MV[:, i, :, 1], eps, None, ALU.add).then_inc(s[done], 1)

            def normalise(dst, src, i, tb):
                return ts(dst, src, MV[:, i, tb, 0:1], RS[:, i, tb:tb + 1], ALU.subtract, ALU.mult)

            dve.wait_ge(s["cst_in"], 16)
            re, im = C("phz_re"), C("phz_im")
            mark(tt(pz[:, 2, :], re, re, ALU.mult))
            mark(tt(pz[:, 3, :], im, im, ALU.mult))
            settle()
            link(tt(pz[:, 4, :], pz[:, 2, :], pz[:, 3, :], ALU.add))
            ts(pz[:, 0, :], pz[:, 4, :], 1e-19, None, ALU.max).then_inc(s["unit"], 1)
            mark(ts(pz[:, 5, :], pz[:, 4, :], 1e-19, None, ALU.is_gt))
            mark(ts(pz[:, 6, :], pz[:, 4, :], 1e-19, None, ALU.is_le))
            mark(ts(b1h[:, :], C("b1"), 0.5, None, ALU.mult))
            dve.wait_ge(s["table_in"], 1)
            for _ in range(2):
                link(tt(pz[:, 9, :], pz[:, 1, :], pz[:, 1, :], ALU.mult))
                link(tt(pz[:, 9, :], pz[:, 9, :], pz[:, 0, :], ALU.mult))
                link(ts(pz[:, 9, :], pz[:, 9, :], -0.5, 1.5, ALU.mult, ALU.add))
                link(tt(pz[:, 1, :], pz[:, 1, :], pz[:, 9, :], ALU.mult))
            tt(pz[:, 7, :], pz[:, 4, :], pz[:, 1, :], ALU.mult).then_inc(s["unit"], 1)
            link(tt(pz[:, 10, :], pz[:, 1, :], pz[:, 5, :], ALU.mult))
            for F in (FR, CR):
                mark(dve.memset(F[:, :, 0:1], 1.0))
            for F in (FI, CI):
                mark(dve.memset(F[:, :, 0:1], 0.0))
            mark(tt(FR[:, :, 1], re, pz[:, 10, :], ALU.mult))
            mark(tt(FI[:, :, 1], im, pz[:, 10, :], ALU.mult))
            settle()
            link(tt(FR[:, :, 1], FR[:, :, 1], pz[:, 6, :], ALU.add))
            dve.wait_ge(s["table_in"], 2)
            link(ts(pz[:, 11, :], pz[:, 8, :], 1.0, None, ALU.add))
            link(dve.reciprocal(pz[:, 11, :], pz[:, 11, :]))
            link(ts(pz[:, 12, :], pz[:, 8, :], -1.0, 1.0, ALU.mult, ALU.add))
            mark(tt(pz[:, 12, :], pz[:, 12, :], pz[:, 11, :], ALU.mult))
            settle()

            def cmul(outs, x, y, shape):
                (xr, xi), (yr, yi) = x, y
                n = 1
                for d in shape:
                    n *= d
                tmp = [t[:, 0:n] for t in tt4]
                if len(shape) == 2:
                    tmp = [t.rearrange("p (a b) -> p a b", a=shape[0]) for t in tmp]
                mark(tt(tmp[0], xr, yr, ALU.mult))
                mark(tt(tmp[1], xi, yi, ALU.mult))
                mark(tt(tmp[2], xr, yi, ALU.mult))
                mark(tt(tmp[3], xi, yr, ALU.mult))
                settle()
                mark(tt(outs[0], tmp[0], tmp[1], ALU.subtract))
                mark(tt(outs[1], tmp[2], tmp[3], ALU.add))
                settle()

            def powers(R, I, top):
                m = 1
                while m < top:
                    bc = (P, DEPTH, m)
                    cmul((R[:, :, m + 1:2 * m + 1], I[:, :, m + 1:2 * m + 1]),
                         (R[:, :, 1:m + 1], I[:, :, 1:m + 1]),
                         (R[:, :, m:m + 1].to_broadcast(bc), I[:, :, m:m + 1].to_broadcast(bc)), (DEPTH, m))
                    m *= 2

            for i in range(4):
                if i % 2 == 0:
                    dve.wait_ge(s[f"x_in{i // 2}"], 16)
                stats(lambda tb: XR[:, 2 * i + tb, :], i, 1e-5, "ln0_stats")
            for i in range(4):
                dve.wait_ge(s["ln0_rstd"], i + 1)
                for tb in range(TB):
                    normalise(XN0[:, 2 * i + tb, :], XR[:, 2 * i + tb, :], i, tb).then_inc(s["xn0"], 1)

            powers(FR, FI, FINE)
            mark(dve.tensor_copy(CR[:, :, 1], FR[:, :, FINE]))
            link(dve.tensor_copy(CI[:, :, 1], FI[:, :, FINE]))
            powers(CR, CI, COARSE)

            def table(l):
                shape = (P, COARSE, FINE)
                cr = CR[:, l, 0:COARSE][:, :, None].to_broadcast(shape)
                ci = CI[:, l, 0:COARSE][:, :, None].to_broadcast(shape)
                fr = FR[:, l, 0:FINE][:, None, :].to_broadcast(shape)
                fi = FI[:, l, 0:FINE][:, None, :].to_broadcast(shape)
                cmul((COS[:, l, :].rearrange("p (a b) -> p a b", a=COARSE),
                      SIN[:, l, :].rearrange("p (a b) -> p a b", a=COARSE)), (cr, ci), (fr, fi), (COARSE, FINE))

            cmul((pz[:, 13, :], pz[:, 14, :]), (C("lc_re"), C("lc_im")), (FR[:, :, 1], FI[:, :, 1]), (DEPTH,))
            link(ts(pz[:, 14, :], pz[:, 14, :], -1.0, None, ALU.mult))

            dve.wait_ge(s["h_in"], 1)
            ts(Hs, PS[:, 0, :], C("bin"), None, ALU.add).then_inc(s["h_new"], 1)

            def unpack(par):
                if par == 0:
                    dve.wait_ge(s["deq_in"], 16 * 7)
                w = weff[:, :, :].rearrange("p (h e) o -> p e h o", e=2)[:, par, :, :]
                link(ts(codes, packed, 4 * par, 7, ALU.logical_shift_right, ALU.bitwise_and))
                mark(ts(w, codes, 0.5, None, ALU.mult))
                mark(ts(fieldf, codes, 4.0, 0.0, ALU.subtract, ALU.max))
                mark(ts(dtmp, codes, 6.0, 0.0, ALU.subtract, ALU.max))
                settle()
                link(stt(w, fieldf, 0.5, w, ALU.mult, ALU.add))
                mark(tt(w, w, dtmp, ALU.add))
                mark(ts(codes, packed, 4 * par + 3, 1, ALU.logical_shift_right, ALU.bitwise_and))
                settle()
                mark(ts(fieldf, codes, -2.0, 1.0, ALU.mult, ALU.add))
                link(tt(dtmp, bsc, w, ALU.mult))
                link(tt(w, dtmp, fieldf, ALU.mult))
                link(ts(w, w, gsb[:, 0:1], None, ALU.mult))

            def add_lora(i):
                dve.wait_ge(s["lora_prod"], i + 1)
                tt(weff[:, i, :], weff[:, i, :], bank("weff_ready", i + 1), ALU.add).then_inc(s["weff_ready"], 1)

            for l in range(DEPTH):
                table(l)
                dve.wait_ge(s["rstd0"], 2 * l + 1)
                tt(S, PS[:, 0, :], RSTD, ALU.mult).then_inc(s["normed"], 1)
                dve.wait_ge(s["normed"], 3 * l + 1)
                if l:
                    dve.wait_ge(s["hidden_sum"], 4 * l)
                ts(Z, S, C("ln1_w", l), C("ln1_b", l), ALU.mult, ALU.add).then_inc(s["normed"], 1)
                dve.wait_ge(s["tanh0"], 5 * l + 1)
                link(stt(S, T0, 1.0, Z, ALU.add, ALU.mult))
                mark(stt(MR, S, 0.5, COS[:, l, :], ALU.mult, ALU.mult))
                mark(stt(MI, S, 0.5, SIN[:, l, :], ALU.mult, ALU.mult))
                settle()
                decay = pz[:, 12, l:l + 1].to_broadcast((P, SEQ))
                mark(dve.tensor_tensor_scan(UR, decay, MR, pz[:, 13, l:l + 1], ALU.mult, ALU.add))
                mark(dve.tensor_tensor_scan(VI, decay, MI, pz[:, 14, l:l + 1], ALU.mult, ALU.add))
                settle()
                mark(tt(UR, UR, COS[:, l, :], ALU.mult))
                mark(tt(VI, VI, SIN[:, l, :], ALU.mult))
                settle()
                link(tt(UR, UR, VI, ALU.add))
                stt(Hs, UR, C("scl", l), Hs, ALU.mult, ALU.add).then_inc(s["h_new"], 1)
                dve.wait_ge(s["h_new"], 2 * l + 2)
                mark(ts(HB, Hs, C("b2", l), None, ALU.add))
                if l == 0:
                    unpack(0)
                    unpack(1)
                if l == 1:
                    for i in range(4):
                        add_lora(i)
                dve.wait_ge(s["rstd0"], 2 * l + 2)
                link(tt(S, PS[:, 0, :], RSTD, ALU.mult))
                ts(Z, S, C("ln2_w", l), C("ln2_b", l), ALU.mult, ALU.add).then_inc(s["normed"], 1)
                for m in range(4):
                    bias = C("b1", 2 * l + m % 2)
                    dve.wait_ge(s["tanh0"], 5 * l + 2 + m)
                    link(stt(hth[:, m, :], PS[:, 4 + m, :], bias, hth[:, m, :], ALU.add, ALU.mult))
                    if l:
                        dve.wait_ge(s["ffn_sum"], l)
                    stt(hid[:, m, :], PS[:, 4 + m, :], bias, hth[:, m, :], ALU.add, ALU.add).then_inc(s["hidden"], 1)
                dve.wait_ge(s["ffn_sum"], l + 1)
                stt(Hs, PS[:, 1, :], 0.5, HB, ALU.mult, ALU.add).then_inc(s["h_new"], 1)
            dve.wait_ge(s["rstd0"], 2 * DEPTH + 1)
            link(tt(S, PS[:, 0, :], RSTD, ALU.mult))
            ts(HN[:, :], S, C("lnl_w"), C("lnl_b"), ALU.mult, ALU.add).then_inc(s["hn"], 1)

            def scan(g):
                k, u = g // UNITS, g % UNITS
                dve.wait_ge(s["decay"], g + 1)
                dve.wait_ge(s["dbx"], g + 1)
                if g >= 2:
                    dve.wait_ge(s["turned_h"], 2 * (g - 1))
                    dve.wait_ge(s["state_kept"], g - 1)
                for i in range(HCT):
                    first = HC[:, u, i:i + 1] if k % 2 else 0.0
                    last = dve.tensor_tensor_scan(H[:, g % 2, i, :], DA[:, g % DRING, i, :], DBX[:, g % BRING, i, :],
                                                  first, ALU.mult, ALU.add)
                last.then_inc(s["states"], 1)

            def add_y(g):
                k, u = g // UNITS, g % UNITS
                n, h = u // 2, u % 2
                if u == 0:
                    dve.wait_ge(s["skip_copied"], 4 * (k + 1))
                for tb in range(TB):
                    dve.wait_ge(s["turned_h"], 2 * g + tb + 1)
                    if u >= 2:
                        dve.wait_ge(s["y_sum"], 2 * (g - 2) + tb + 1)
                    y = Y[:, k % 2, tb, 512 * h:512 * h + 512]
                    cn = SPN[:, k % 2, tb, 48 + n:49 + n]
                    stt(y, PS[:, TR[tb], :], cn, y, ALU.mult, ALU.add).then_inc(s["y_sum"], 1)

            for k in range(-1, NCHUNK + 1):
                for n in range(NS):
                    if 0 <= k < NCHUNK:
                        for u in (2 * n, 2 * n + 1):
                            scan(UNITS * k + u)
                            if u:
                                add_y(UNITS * k + u - 1)
                        if n == NS - 1:
                            add_y(UNITS * k + UNITS - 1)
                    for what, c in pieces(k, n):
                        blk = [TB * c + tb for tb in range(TB)]
                        if what == "attn_out":
                            dve.wait_ge(s["misc_in"], 48)
                            if c:
                                dve.wait_ge(s["turned_x2"], TB * c)
                            for tb in range(TB):
                                dve.wait_ge(s["attn_out"], blk[tb] + 1)
                                tt(LR[:, tb, :], bank("a_read", blk[tb] + 1), boutb[:, :], ALU.add
                                   ).then_inc(s["a_read"], 1)
                            dve.wait_ge(s["a_read"], TB * (c + 1))
                            stats(lambda tb: LR[:, tb, :], 0, 1e-5, "r1_stats")
                        elif what == "ln_a":
                            dve.wait_ge(s["r1_rstd"], c + 1)
                            for tb in range(TB):
                                mark(normalise(LR[:, tb, :], LR[:, tb, :], 0, tb))
                            settle()
                            for tb in range(TB):
                                mark(tt(XR[:, blk[tb], :], XR[:, blk[tb], :], LR[:, tb, :], ALU.add))
                            settle()
                            stats(lambda tb: XR[:, blk[tb], :], 1, 1e-5, "r2_stats")
                        elif what == "xn":
                            dve.wait_ge(s["r2_rstd"], c + 1)
                            for tb in range(TB):
                                normalise(LR[:, tb, :], XR[:, blk[tb], :], 1, tb).then_inc(s["xn"], 1)
                        elif what == "f_stats":
                            dve.wait_ge(s["ffn0_copied"], TB * (c + 1))
                            stats(lambda tb: LR[:, tb, :], 2, 1e-5, "r3_stats")
                        elif what == "x2":
                            dve.wait_ge(s["r3_rstd"], c + 1)
                            for tb in range(TB):
                                mark(normalise(LR[:, tb, :], LR[:, tb, :], 2, tb))
                            settle()
                            for tb in range(TB):
                                mark(tt(XR[:, blk[tb], :], XR[:, blk[tb], :], LR[:, tb, :], ALU.add))
                            settle()
                            stats(lambda tb: XR[:, blk[tb], :], 3, 1e-5, "r4_stats")
                        elif what == "x2n":
                            dve.wait_ge(s["r4_rstd"], c + 1)
                            for tb in range(TB):
                                normalise(LR[:, tb, :], XR[:, blk[tb], :], 3, tb).then_inc(s["x2n"], 1)
                        elif what in ("conv01", "conv23"):
                            if what == "conv01" and c >= 2:
                                dve.wait_ge(s["out_prod"], TB * (c - 1))
                            for m in (int(what[4]), int(what[4]) + 1):
                                dve.wait_ge(s["in_copied"], 4 * c + m + 1)
                                for tap in range(4):
                                    for e in range(2):
                                        ct = 2 * m + e
                                        wt = convw[:, ct, tap:tap + 1]
                                        if tap == 0:
                                            mark(ts(XC[:, ct, :], XI[:, ct, 0:CH], wt, C("conv_b", ct),
                                                    ALU.mult, ALU.add))
                                        else:
                                            ins = stt(XC[:, ct, :], XI[:, ct, tap:tap + CH], wt, XC[:, ct, :],
                                                      ALU.mult, ALU.add)
                                            if tap < 3 or e == 0:
                                                mark(ins)
                                            else:
                                                ins.then_inc(s["conv"], 1)
                                    if tap < 3:
                                        settle()
                                dve.wait_ge(s["conv_tanh"], 4 * c + m + 1)
                                link(stt(TH[:, :, :], TH[:, :, :], 1.0, XC[:, 2 * m:2 * m + 2, :], ALU.add, ALU.mult))
                                ts(XC[:, 2 * m:2 * m + 2, :], TH[:, :, :], 0.5, None, ALU.mult).then_inc(s["xc"], 1)
                                dve.wait_ge(s["xc"], 4 * c + m + 1)
                        elif what == "x_proj":
                            pass
                        elif what == "bc":
                            dve.wait_ge(s["sp"], c + 1)
                            tmp = TH[:, 0, 0:64 * TB].rearrange("p (b e) -> p b e", b=TB)
                            link(tt(tmp, SP[:, :, :], SP[:, :, :], ALU.mult))
                            segs = [(0, RK), (RK, RK + NS), (RK + NS, RK + 2 * NS)]
                            for i, (lo, hi) in enumerate(segs):
                                mark(dve.tensor_reduce(MS[:, i, :], tmp[:, :, lo:hi], AX_X, ALU.add))
                            settle()
                            mark(ts(MS[:, 0, :], MS[:, 0, :], 1.0 / RK, 1e-6, ALU.mult, ALU.add))
                            settle()
                            ts(MS[:, 1:3, :], MS[:, 1:3, :], 1.0 / NS, 1e-6, ALU.mult, ALU.add).then_inc(s["ms"], 1)
                            dve.wait_ge(s["ms_rstd"], c + 1)
                            for i, (lo, hi) in enumerate(segs):
                                for tb in range(TB):
                                    stt(SPN[:, c % 2, tb, lo:hi], SP[:, tb, lo:hi], MSR[:, i, tb:tb + 1],
                                        rmsb[:, lo:hi], ALU.mult, ALU.mult).then_inc(s["spn"], 1)
                        elif what == "dtx":
                            dve.wait_ge(s["dt_log"], c + 1)
                            tt(DT[:, c % 2, :, :], DT[:, c % 2, :, :], XI[:, :, 3:3 + CH], ALU.add
                               ).then_inc(s["dt_ready"], 1)
                            dve.wait_ge(s["dt_ready"], c + 1)
                            tt(DTX[:, c % 2, :, :], DT[:, c % 2, :, :], XC[:, :, :], ALU.mult).then_inc(s["dtx"], 1)
                        elif what in ("z0", "z1"):
                            h = int(what[1])
                            for tb in range(TB):
                                r = 4 * c + 2 * h + tb + 1
                                dve.wait_ge(s["z_tanh"], r)
                                stt(G[:, r % 2, :], G[:, r % 2, :], 1.0, bank("z_read", r), ALU.add, ALU.mult
                                    ).then_inc(s["z_read"], 1)
                                dve.wait_ge(s["z_read"], r)
                                if h == 0 and tb == 0:
                                    dve.wait_ge(s["y_sum"], 2 * UNITS * (c + 1))
                                y = Y[:, c % 2, tb, 512 * h:512 * h + 512]
                                stt(y, G[:, r % 2, :], 0.5, y, ALU.mult, ALU.mult).then_inc(s["gated"], 1)
                        elif what == "o_stats":
                            dve.wait_ge(s["out_copied"], TB * (c + 1))
                            stats(lambda tb: LP[:, tb, :], 4, 1e-5, "p5_stats")
                        elif what == "x3":
                            dve.wait_ge(s["p5_rstd"], c + 1)
                            for tb in range(TB):
                                mark(normalise(LP[:, tb, :], LP[:, tb, :], 4, tb))
                            settle()
                            for tb in range(TB):
                                mark(tt(XR[:, blk[tb], :], XR[:, blk[tb], :], LP[:, tb, :], ALU.add))
                            settle()
                            stats(lambda tb: XR[:, blk[tb], :], 5, 1e-5, "p6_stats")
                        elif what == "x3n":
                            dve.wait_ge(s["p6_rstd"], c + 1)
                            for tb in range(TB):
                                normalise(LP[:, tb, :], XR[:, blk[tb], :], 5, tb).then_inc(s["x3n"], 1)
                        elif what[0] == "j":
                            g = NJ * c + int(what[1:])
                            dve.wait_ge(s["gate_tanh"], g + 1)
                            link(stt(GT[:, g % 2, :], GT[:, g % 2, :], 1.0, PS[:, GUB[g % 2], 0:CH],
                                     ALU.add, ALU.mult))
                            if g >= 2:
                                q = item[("w", (g - 2) // NJ, (g - 2) % NJ)]
                                dve.wait_ge(s["slot_free"], q + 1)
                            stt(HJ[:, g % 2, :], GT[:, g % 2, :], 0.5, PS[:, GUB[g % 2], CH:2 * CH],
                                ALU.mult, ALU.mult).then_inc(s["hj"], 1)
                        elif what == "final_stats":
                            dve.wait_ge(s["y_copied"], TB * (c + 1))
                            stats(lambda tb: LP[:, tb, :], 6, 1e-5, "p7_stats")
                        elif what == "final":
                            final(dve, c, s, LP, XR, normalise, mark, settle, tt)
            c = NCHUNK - 1
            dve.wait_ge(s["y_copied"], TB * NCHUNK)
            stats(lambda tb: LP[:, tb, :], 6, 1e-5, "p7_stats")
            final(dve, c, s, LP, XR, normalise, mark, settle, tt)


def final(dve, c, s, LP, XR, normalise, mark, settle, tt):
    dve.wait_ge(s["p7_rstd"], c + 1)
    for tb in range(TB):
        mark(normalise(LP[:, tb, :], LP[:, tb, :], 6, tb))
    settle()
    for tb in range(TB):
        x = XR[:, TB * c + tb, :]
        tt(x, x, LP[:, tb, :], ALU.add).then_inc(s["result"], 1)


def kernel(**inputs):
    import numpy as np
    import concourse.bacc as bacc
    from concourse.bass_utils import run_bass_kernel_spmd

    v = {n: np.ascontiguousarray(np.asarray(x)) for n, x in inputs.items()}
    A0, F0, A1, F1 = "L0_attn_", "L0_ffn_", "L1_attn_", "L1_ffn_"

    def twice(m):
        m = m.reshape(-1, DIM).T
        return np.concatenate([m, m])

    def tiles(m):
        return m.reshape(CT, P, -1).transpose(1, 0, 2).reshape(P, -1)

    one = np.zeros((P, P), np.float32)
    one[:DIM, :DIM] = one[DIM:, DIM:] = 1.0 / DIM
    eye = np.eye(P, dtype=np.float32)
    c = {"ident": eye, "cen": eye - one, "avg": one, "eps": np.full((P, 1), 1e-5, np.float32),
         "bin": twice(v[A0 + "bin"]), "b1": v[A0 + "b1"].reshape(DEPTH * 2, P).T,
         "lnl_w": twice(v[A0 + "lnl_w"]), "lnl_b": twice(v[A0 + "lnl_b"]), "scl": twice(v[A0 + "sc_lin"]),
         "dt_bias": tiles(v[A1 + "dt_bias"]), "D": tiles(v[A1 + "D_param"]), "conv_b": tiles(v[A1 + "conv_b"]),
         "conv_w": tiles(v[A1 + "conv_w"]), "A_log": tiles(v[A1 + "A_log"])}
    for n in ("ln1_w", "ln1_b", "ln2_w", "ln2_b", "b2", "phz_re", "phz_im", "lc_re", "lc_im"):
        c[n] = twice(v[A0 + n])
    cst = np.concatenate([c[n].reshape(P, -1) for n in CST], axis=1)
    assert cst.shape == (P, NCST)

    w1 = v[A0 + "W1"].transpose(2, 0, 1).reshape(DIM, -1)
    w2 = v[A0 + "W2"].reshape(DEPTH, DIM, 2, P).transpose(3, 0, 2, 1).reshape(P, -1)
    wo = v[A0 + "Wout"].T
    win = v[A0 + "Win"].T.reshape(KT, P, DIM).transpose(1, 0, 2).reshape(P, -1)
    wp = np.concatenate([np.concatenate([wo, wo]), tiles(v[A1 + "x_proj_w"].T)], axis=1)
    assert wp.shape == (P, NWP)

    la = v[F0 + "lora_A"].reshape(16, 2, P, 2).transpose(0, 1, 3, 2).reshape(16, 4 * P)
    lw = v[A1 + "dt_proj_w"].T
    packed = v[F0 + "packed_weight"].astype(np.int32).T.reshape(2, P, W)

    ipw = v[A1 + "in_proj_w"].reshape(KT, P, 4, 512).transpose(2, 1, 0, 3).reshape(4, P, 2048)
    opw = v[A1 + "out_proj_w"].T.reshape(2, HCT, P, W).transpose(0, 2, 1, 3).reshape(2, P, 2048)
    g = v[F1 + "w1"].T.reshape(KT, P, NJ, P).transpose(2, 1, 0, 3).reshape(NJ, P, 512)
    u = v[F1 + "w3"].T.reshape(KT, P, NJ, P).transpose(2, 1, 0, 3).reshape(NJ, P, 512)
    d = v[F1 + "w2"].T.reshape(NJ, P, W)
    wq = np.concatenate([g, u, d], axis=2)
    sc = np.concatenate([v[F1 + "w1_scale"], v[F1 + "w3_scale"], v[F1 + "w2_scale"].T], axis=1).reshape(-1)
    arrays = {"cst": cst, "x": v[A0 + "x"].reshape(TOK, W), "wp": wp, "w1": np.concatenate([w1, w1]), "w2": w2,
              "win": win, "lw": lw, "la": la, "lb": v[F0 + "lora_B"].T, "packed": packed,
              "bs": v[F0 + "block_scales"].T, "gs": v[F0 + "global_scale"], "sc": sc, "bout": v[A0 + "bout"],
              "rms": np.concatenate([v[A1 + "dt_ln_w"], v[A1 + "B_ln_w"], v[A1 + "C_ln_w"]]),
              "ip": ipw, "op": opw, "wq": wq}
    arrays = {n: np.ascontiguousarray(x) for n, x in arrays.items()}
    nc = bacc.Bacc("TRN2", target_bir_lowering=False, num_devices=1)
    aps = {n: nc.dram_tensor(f"in_{n}", x.shape, mybir.dt.from_np(x.dtype), kind="ExternalInput").ap()
           for n, x in arrays.items()}
    out = nc.dram_tensor("out_0", (TOK, W), F32, kind="ExternalOutput").ap()
    build(nc, aps, out)
    r = run_bass_kernel_spmd(nc, [{f"in_{n}": x for n, x in arrays.items()}], core_ids=[0])
    return r.results[0]["out_0"].reshape(2, SEQ, W)
```

```python
from contextlib import ExitStack

import concourse.bass as bass
from concourse import mybir

F32 = mybir.dt.float32
I32 = mybir.dt.int32
ALU = mybir.AluOpType
ACT = mybir.ActivationFunctionType
AX_X = mybir.AxisListType.X

P = 128
W = 512
TOK = 1024
SEQ = 512
CH = 256
NCHUNK = TOK // CH
TB = CH // P
KT = W // P
DEPTH, DIM, DFF = 4, 64, 256
DIN, NS, RK = 1024, 16, 32
CT = DIN // P
HCT = CT // 2
INTER = 1792
NJ = INTER // P
SLOTS = 3
UNITS = 2 * NS
DRING = 4
BRING = 3
FINE, COARSE = 32, 16

CST = {}
_at = 0
for _name, _n in [("ident", 128), ("cen", 128), ("avg", 128), ("eps", 1), ("bin", 1),
                  ("ln1_w", 4), ("ln1_b", 4), ("scl", 4), ("ln2_w", 4), ("ln2_b", 4), ("b2", 4),
                  ("phz_re", 4), ("phz_im", 4), ("lc_re", 4), ("lc_im", 4), ("lnl_w", 1), ("lnl_b", 1),
                  ("b1", 8), ("dt_bias", 8), ("D", 8), ("conv_b", 8), ("conv_w", 32), ("A_log", 128)]:
    CST[_name] = (_at, _at + _n)
    _at += _n
NCST = _at
WP = {}
_at = 0
for _name, _n in [("wout", W), ("xp", CT * 64)]:
    WP[_name] = (_at, _at + _n)
    _at += _n
NWP = _at
NLW = DIN

AT = {
    0: ["Q.h11", "Q.w10", "R.attn_out", "Q.g12"],
    1: ["R.a_norm", "Q.w11", "Q.h12", "P.z0"],
    2: ["R.x1", "P.gate0", "Q.g13", "P.z1"],
    3: ["R.xn", "P.gate1", "Q.w12", "Q.h13", "P.z2"],
    4: ["P.gate2", "Q.w13", "P.z3", "R.turn_xn", "Q.y_done"],
    5: ["P.gate3", "P.turn_y0"],
    6: ["Q.y_stats", "P.turn_y1", "R.ffn0", "Q.result"],
    7: ["R.ffn1"],
    8: ["R.f_stats", "P.out0"],
    9: ["R.x2", "P.out1"],
    10: ["R.x2n", "P.out2"],
    11: ["P.out3", "R.turn_x2"],
    12: ["P.o_stats", "R.in0"],
    13: ["P.x3", "R.in1"],
    14: ["P.x3n", "R.conv0", "R.in2"],
    15: ["P.turn_x3", "R.conv1", "R.in3"],
    16: ["R.conv2", "P.g0"],
    17: ["P.h0", "R.conv3", "P.g1"],
    18: ["P.w0", "P.h1", "R.x_proj"],
    19: ["P.w1", "R.ms", "P.g2"],
    20: ["P.h2", "R.norm_bc", "P.g3"],
    21: ["P.w2", "P.h3", "R.turn_bc", "P.g4"],
    22: ["P.w3", "P.h4", "R.dt0"],
    23: ["P.w4", "P.g5", "R.dt1"],
    24: ["P.h5", "P.g6", "R.dt_log"],
    25: ["P.w5", "P.h6", "R.skip0", "P.g7"],
    26: ["P.w6", "P.h7", "R.skip1", "R.dtx", "P.g8"],
    27: ["P.w7", "P.h8"],
    28: ["P.w8", "P.g9"],
    29: ["P.h9", "P.g10"],
    30: ["P.w9", "P.h10"],
    31: ["P.g11"],
}


def pieces(k, u):
    for name in AT[u]:
        who, what = name.split(".")
        c = k + {"R": 1, "P": -1, "Q": -2}[who]
        if 0 <= c < NCHUNK:
            yield what, c


RSTD_OF = {"a_norm": ("r1", 0), "x1": ("r2", 1), "f_stats": ("r3", 2), "x2": ("r4", 3),
           "o_stats": ("p5", 4), "x3": ("p6", 5), "y_stats": ("p7", 6)}


def parts(what):
    name = what.rstrip("0123456789")
    return name, int(what[len(name):] or 0)


SEGS = [(0, RK), (RK, RK + NS), (RK + NS, RK + 2 * NS)]

ROUNDS = range(-1, NCHUNK + 2)


def build(nc, a, out):
    ctx = ExitStack()
    with ctx:
        def sb(name, shape, dt=F32):
            return ctx.enter_context(nc.sbuf_tensor(name, shape, dt))

        def sem(name):
            return ctx.enter_context(nc.semaphore(name))

        PS = ctx.enter_context(nc.psum_tensor("PS", [P, 8, 512], F32))
        TR = (0, 1)
        MMB = (2, 3)
        GUB = (4, 5)
        YAB = (6, 7)

        cst = sb("cst", [P, NCST])
        wp = sb("wp", [P, NWP])
        lw = sb("lw", [RK, NLW])
        boutb = sb("boutb", [P, W])
        rmsb = sb("rmsb", [P, 64])
        XR = sb("XR", [P, TOK // P, W])
        HT = sb("HT", [P, 2, KT, CH])
        XF = sb("XF", [P, KT, CH])
        LR = sb("LR", [P, TB, W])
        LP = sb("LP", [P, TB, W])
        weff = sb("weff", [P, 4, W])
        diagD = sb("diagD", [P, CT, P])
        ring = sb("ring", [P, SLOTS, 2048])
        DT = sb("DT", [P, 2, CT, CH])
        DTX = sb("DTX", [P, 2, CT, CH])
        XI = sb("XI", [P, CT, CH + 4])
        XC = sb("XC", [P, CT, CH])
        TH = sb("TH", [P, 2, CH])
        Y = sb("Y", [P, 2, TB, DIN])
        BB = sb("BB", [P, 2, 2, CH])
        DA = sb("DA", [P, DRING, HCT, CH])
        DBX = sb("DBX", [P, BRING, HCT, CH])
        H = sb("H", [P, 2, HCT, CH])
        HC = sb("HC", [P, UNITS, HCT])
        G = sb("G", [P, 2, W])
        GT = sb("GT", [P, 2, CH])
        HJ = sb("HJ", [P, 2, CH])
        SP = sb("SP", [P, TB, 64])
        SPN = sb("SPN", [P, 2, TB, 64])
        DR = sb("DR", [48, CH])
        HN = sb("HN", [P, SEQ])
        BS = sb("BS", [P, 8, TB, 6])
        MV = sb("MV", [P, 8, TB, 2])
        VE = sb("VE", [P, 8, TB])
        RS = sb("RS", [P, 8, TB])
        MS = sb("MS", [P, 3, TB])
        MSR = sb("MSR", [P, 3, TB])
        half = sb("half", [P, 8])
        NA = sb("NA", [P, P])
        scb = sb("scb", [P, 12 * NJ])
        cv = sb("cv", [P, CT, 3])

        XN0 = DTX[:, :, :, :].rearrange("p a c t -> p (a c t)").rearrange("p (n w) -> p n w", w=W)
        XT0 = DT[:, :, :, :].rearrange("p b (k e) t -> p b k (e t)", k=KT)
        COS = Y[:, 0, :, :].rearrange("p a (b t) -> p (a b) t", t=SEQ)
        SIN = Y[:, 1, :, :].rearrange("p a (b t) -> p (a b) t", t=SEQ)
        wk = DA[:, :, :, :].rearrange("p a c t -> p (a c t)").rearrange("p (n t) -> p n t", t=SEQ)
        wk2 = DBX[:, :, :, :].rearrange("p a c t -> p (a c t)").rearrange("p (n t) -> p n t", t=SEQ)
        hid = XC[:, :, :].rearrange("p c t -> p (c t)").rearrange("p (n t) -> p n t", t=SEQ)
        hth = H[:, :, :, :].rearrange("p a c t -> p (a c t)").rearrange("p (n t) -> p n t", t=SEQ)
        Hs, SQ, RSTD, Z, S, MR, MI = (wk[:, i, :] for i in range(7))
        T0 = wk[:, 7, :]
        UR, VI, HB = (wk2[:, i, :] for i in range(3))
        xi4 = XI[:, :, :].rearrange("p c t -> p (c t)")
        codes = LR[:, :, :].rearrange("p a t -> p (a t)").bitcast(I32).rearrange("p (h o) -> p h o", h=2)
        fieldf = LP[:, :, :].rearrange("p a t -> p (a t)").rearrange("p (h o) -> p h o", h=2)
        packed = XF[:, :, :].rearrange("p k t -> p (k t)").bitcast(I32).rearrange("p (h o) -> p h o", h=2)
        bsc = HT[:, 1, :, :].rearrange("p k t -> p (k t)").rearrange("p (h o) -> p h o", h=2)
        dtmp = wk2[:, 3:5, :]
        gsb = sb("gsb", [P, 1])
        FR = sb("FR", [P, DEPTH, FINE + 1])
        FI = sb("FI", [P, DEPTH, FINE + 1])
        CR = sb("CR", [P, DEPTH, COARSE + 1])
        CI = sb("CI", [P, DEPTH, COARSE + 1])
        tt4 = [xi4[:, i * 512:(i + 1) * 512] for i in range(4)]
        pz = sb("pz", [P, 16, DEPTH])
        b1h = sb("b1h", [P, 8])

        def C(name, i=None):
            lo, hi = CST[name]
            return cst[:, lo:hi] if i is None else cst[:, lo + i:lo + i + 1]

        ident, cen_m, avg_m = C("ident"), C("cen"), C("avg")
        w1_at = BB[:, :, :, :].rearrange("p a b t -> p (a b t)")
        w2_at = G[:, 0, :]
        win_at = G[:, 1, 0:KT * DIM]
        winT = win_at.rearrange("p (k d) -> p k d", k=KT)
        w1T = w1_at.rearrange("p (l f) -> p l f", l=DEPTH)
        w2T = w2_at.rearrange("p (l f d) -> p l f d", l=DEPTH, f=2)
        woutT = wp[:, WP["wout"][0]:WP["wout"][1]]
        xpT = wp[:, WP["xp"][0]:WP["xp"][1]].rearrange("p (c e) -> p c e", c=CT)
        la_at = GT[0:16, :, :].rearrange("r a t -> r (a t)")
        loraA = la_at.rearrange("r (k i) -> r k i", k=4)
        loraB = HJ[0:16, :, :].rearrange("r a t -> r (a t)")
        dpT = lw[0:RK, :]
        convw = C("conv_w").rearrange("p (c k) -> p c k", c=CT)

        wsc = nc.dram_tensor("w_scaled", (NJ, P, 1536), F32, kind="Internal").ap()
        b_rows = nc.dram_tensor("b_rows", (NCHUNK, NS, CH), F32, kind="Internal").ap()

        names = """cst_in x_in0 x_in1 w_in deq_in misc_in
            pw0 pw1 pw2 scaled st0 st1 st2
            unit tables table_in half_set
            ln0_stats ln0_rstd xn0 xn0_turned xt0_copied h_in
            h_new centred squared variance rstd0 normed tanh0 hidden_sum hidden ffn_sum hn
            lora_prod weff_ready diag_ready na_ready na_exp
            ld0 ld1 ld2 free0 free1 free2
            attn_out a_read r1_stats r1_rstd xn turned_xn xt
            ffn0_prod ffn0_copied r3_stats r3_rstd x2n turned_x2 ht r2_stats r2_rstd r4_stats r4_rstd
            in_prod in_copied carry tail_kept conv conv_tanh xc
            xp_prod sp ms ms_rstd spn turned_bc dr b_stored
            dt_prod dt_split dt_log dt_ready dtx
            skip_prod skip_copied
            bb0 bb1 dbx decay states state_kept turned_h y_sum
            z_prod z_tanh z_read gated turned_y yt out_prod out_copied
            p5_stats p5_rstd p6_stats p6_rstd x3n turned_x3 xf gu_prod gate_tanh gu_read hj w2_prod y_copied
            p7_stats p7_rstd result stored_out
            dve_step act_step pool_step""".split()
        s = {n: sem(n) for n in names}

        readers = [("xt0_copied", i + 1) for i in range(8)]
        readers += [("weff_ready", i + 1) for i in range(4)]
        for k in ROUNDS:
            for n in range(UNITS):
                for what, c in pieces(k, n):
                    name, i = parts(what)
                    if what == "attn_out":
                        readers += [("a_read", TB * c + tb + 1) for tb in range(TB)]
                    elif name == "z":
                        readers.append(("z_read", 4 * c + i + 1))
                    elif what == "turn_xn":
                        readers += [("xt", TB * c + tb + 1) for tb in range(TB)]
                    elif name == "turn_y":
                        readers += [("yt", 4 * c + 2 * i + h + 1) for h in range(2)]
                    elif name == "ffn":
                        readers.append(("ffn0_copied", TB * c + i + 1))
                    elif name == "out" and i % 2 == 0:
                        readers.append(("out_copied", TB * c + i // 2 + 1))
                    elif what == "turn_x2":
                        readers += [("ht", TB * c + tb + 1) for tb in range(TB)]
                    elif what == "turn_x3":
                        readers += [("xf", TB * c + tb + 1) for tb in range(TB)]
                    elif name == "in":
                        readers.append(("in_copied", 4 * c + i + 1))
                    elif what == "x_proj":
                        readers.append(("sp", c + 1))
                    elif what == "turn_bc":
                        readers.append(("dr", c + 1))
                    elif what in ("dt0", "dt1"):
                        readers += [("dt_split", 4 * c + 2 * i + m + 1) for m in range(2)]
                    elif name == "skip":
                        readers += [("skip_copied", 4 * c + 2 * i + m + 1) for m in range(2)]
        mm_index = {r: i for i, r in enumerate(readers)}

        def bank(name, value):
            return PS[:, MMB[mm_index[(name, value)] % 2], :]

        stream, last_use = [], {}
        for k in ROUNDS:
            for n in range(UNITS):
                for what, c in pieces(k, n):
                    name, i = parts(what)
                    uses = {"z": [("ip", c, 2 + i // 2)], "in": [("ip", c, i // 2)], "g": [("w", c, i)],
                            "w": [("w", c, i)], "out": [("op", c, 0), ("op", c, 1)] if i == 0 else [("op", c, i % 2)]
                            }.get(name, [])
                    for it in uses:
                        if it not in last_use:
                            stream.append(it)
                        last_use[it] = (k, n)
        item = {it: q for q, it in enumerate(stream)}

        def loaded(kind, c, i):
            q = item[(kind, c, i)]
            return q % SLOTS, s[f"ld{q % SLOTS}"], 16 * (q // SLOTS + 1)

        def freed(kind, c, i):
            q = item[(kind, c, i)]
            return s[f"free{q % SLOTS}"], q // SLOTS + 1

        def in_done(c, m):
            return freed("ip", c, m // 2) if m % 2 else (s["in_prod"], 2 * c + m // 2 + 1)

        def z_done(c, i):
            return freed("ip", c, 2 + i // 2) if i % 2 else (s["z_prod"], 2 * c + i // 2 + 1)

        def out_done(c, tb):
            return freed("op", c, 1) if tb else (s["out_prod"], c + 1)

        block = ctx.enter_context(nc.Block())

        @block.sync
        def _(sp):
            sp.dma_start(cst[:, :], a["cst"]).then_inc(s["cst_in"], 16)
            for b in range(2):
                sp.dma_start(XR[:, 4 * b:4 * b + 4, :],
                             a["x"].rearrange("(n p) v -> p n v", p=P)[:, 4 * b:4 * b + 4, :]
                             ).then_inc(s[f"x_in{b}"], 16)
            for dst, n in ((w1_at, "w1"), (w2_at, "w2"), (win_at, "win"), (wp[:, :], "wp")):
                sp.dma_start(dst, a[n]).then_inc(s["w_in"], 16)
            sp.dma_start(packed, a["packed"].rearrange("h p o -> p h o")).then_inc(s["deq_in"], 16)
            for g in range(2):
                sp.dma_start(bsc[:, g, :], a["bs"][16 * g:16 * g + 16, None, :].to_broadcast((16, 8, W))
                             ).then_inc(s["deq_in"], 16)
            sp.dma_start(gsb[:, :], a["gs"][None, :].to_broadcast((P, 1))).then_inc(s["deq_in"], 16)
            for dst, n in ((lw[:, :], "lw"), (la_at, "la"), (loraB, "lb")):
                sp.dma_start(dst, a[n]).then_inc(s["deq_in"], 16)
            sp.dma_start(scb[:, :], a["sc"][None, :].to_broadcast((P, 12 * NJ))).then_inc(s["misc_in"], 16)
            sp.dma_start(boutb[:, :], a["bout"][None, :].to_broadcast((P, W))).then_inc(s["misc_in"], 16)
            sp.dma_start(rmsb[:, :], a["rms"][None, :].to_broadcast((P, 64))).then_inc(s["misc_in"], 16)
            for j in range(NJ + 1):
                if j < NJ:
                    if j >= SLOTS:
                        sp.wait_ge(s[f"st{j % SLOTS}"], 16 * (j // SLOTS))
                    sp.dma_start(ring[:, j % SLOTS, 0:1536], a["wq"][j]).then_inc(s[f"pw{j % SLOTS}"], 16)
                if j >= 1:
                    sp.wait_ge(s["scaled"], j)
                    sp.dma_start(wsc[j - 1], ring[:, (j - 1) % SLOTS, 0:1536]).then_inc(s[f"st{(j - 1) % SLOTS}"], 16)
            for i in range(SLOTS):
                sp.wait_ge(s[f"st{i}"], 16 * len(range(i, NJ, SLOTS)))

            def fetch(q):
                kind, c, i = stream[q]
                if q >= SLOTS:
                    sp.wait_ge(*freed(*stream[q - SLOTS]))
                dst = ring[:, q % SLOTS, :]
                src = {"ip": a["ip"], "op": a["op"], "w": wsc}[kind][i]
                if kind == "w":
                    dst = dst[:, 0:1536]
                sp.dma_start(dst, src).then_inc(s[f"ld{q % SLOTS}"], 16)

            def spread_b(c, m):
                g = 8 * c + m
                if m == 0:
                    sp.wait_ge(s["b_stored"], 16 * (c + 1))
                if g >= 2:
                    sp.wait_ge(s["dbx"], 4 * (g - 1))
                sp.dma_start(BB[:, g % 2, :, :], b_rows[c, 2 * m:2 * m + 2, :][None, :, :].to_broadcast((P, 2, CH))
                             ).then_inc(s[f"bb{g % 2}"], 16)

            q = 0
            for _ in range(SLOTS):
                fetch(q)
                q += 1
            for k in ROUNDS:
                for u in range(UNITS):
                    if 0 <= k < NCHUNK and u % 4 == 0 and u // 4 + 2 < NS // 2:
                        spread_b(k, u // 4 + 2)
                    for what, c in pieces(k, u):
                        if what == "turn_bc":
                            sp.wait_ge(s["dr"], c + 1)
                            sp.dma_start(b_rows[c], DR[RK:RK + NS, :]).then_inc(s["b_stored"], 16)
                        if what == "g11" or (what == "dtx" and c == 0):
                            n = c + 2 if what == "g11" else 0
                            if n < NCHUNK:
                                spread_b(n, 0)
                                spread_b(n, 1)
                        if what == "dtx" and c == 1:
                            spread_b(1, 0)
                            spread_b(1, 1)
                    while q < len(stream) and last_use[stream[q - SLOTS]] <= (k, u):
                        fetch(q)
                        q += 1
                    for what, c in pieces(k, u):
                        if what == "result":
                            sp.wait_ge(s["result"], TB * (c + 1))
                            sp.dma_start(out.rearrange("(n p) v -> p n v", p=P)[:, TB * c:TB * c + TB, :],
                                         XR[:, TB * c:TB * c + TB, :]).then_inc(s["stored_out"], 16)
            while q < len(stream):
                fetch(q)
                q += 1
            sp.wait_ge(s["stored_out"], 16 * NCHUNK)

        @block.tensor
        def _(pe):
            def turn(dst, src, srcs=4):
                for i in range(srcs):
                    last = pe.transpose(dst[:, i * P:(i + 1) * P], src(i), ident)
                return last

            def free(name, value):
                i = mm_index[(name, value)]
                if i >= 2:
                    pe.wait_ge(s[readers[i - 2][0]], readers[i - 2][1])

            pe.wait_ge(s["cst_in"], 16)
            for t in range(TOK // P):
                pe.wait_ge(s["xn0"], t + 1)
                free("xt0_copied", t + 1)
                turn(bank("xt0_copied", t + 1), lambda i: XN0[:, t, i * P:(i + 1) * P]).then_inc(s["xn0_turned"], 1)
            pe.wait_ge(s["w_in"], 64)
            pe.wait_ge(s["xt0_copied"], 8)
            for b in range(2):
                for kk in range(KT):
                    last = pe.matmul(PS[64 * b:64 * b + 64, 0, :], winT[:, kk, :], XT0[:, b, kk, :],
                                     start=kk == 0, stop=kk == KT - 1)
            last.then_inc(s["h_in"], 1)
            def norm0(i):
                pe.wait_ge(s["h_new"], i + 1)
                pe.matmul(PS[:, 0, :], cen_m, Hs, start=True, stop=True).then_inc(s["centred"], 1)
                pe.wait_ge(s["squared"], i + 1)
                pe.matmul(PS[:, 1, :], avg_m, SQ, start=True, stop=True).then_inc(s["variance"], 1)

            for l in range(DEPTH):
                norm0(2 * l)
                if l == 1:
                    pe.wait_ge(s["deq_in"], 16 * 7)
                    for i in range(4):
                        free("weff_ready", i + 1)
                        pe.matmul(bank("weff_ready", i + 1), loraA[:, i, :], loraB, start=True, stop=True
                                  ).then_inc(s["lora_prod"], 1)
                norm0(2 * l + 1)
                pe.wait_ge(s["normed"], 3 * l + 3)
                for b in range(2):
                    for f in range(2):
                        if l:
                            pe.wait_ge(s["hidden"], 4 * (l - 1) + 2 * b + f + 1)
                        pe.matmul(PS[:, 4 + 2 * b + f, :], w1T[64 * b:64 * b + 64, l, f * P:(f + 1) * P],
                                  Z[64 * b:64 * b + 64, :], start=True, stop=True).then_inc(s["hidden_sum"], 1)
                for b in range(2):
                    for f in range(2):
                        pe.wait_ge(s["hidden"], 4 * l + 2 * b + f + 1)
                        last = pe.matmul(PS[64 * b:64 * b + 64, 1, :], w2T[:, l, f, :], hid[:, 2 * b + f, :],
                                         start=f == 0, stop=f == 1)
                last.then_inc(s["ffn_sum"], 1)
            norm0(2 * DEPTH)
            pe.wait_ge(s["hn"], 1)

            def scan_turn(g):
                pe.wait_ge(s["states"], g + 1)
                for tb in range(TB):
                    if g >= 1:
                        pe.wait_ge(s["y_sum"], 2 * (g - 1) + tb + 1)
                    turn(PS[:, TR[tb], :], lambda i: H[:, g % 2, i, tb * P:(tb + 1) * P]
                         ).then_inc(s["turned_h"], 1)

            for k in ROUNDS:
                for u in range(UNITS):
                    if 0 <= k < NCHUNK:
                        scan_turn(UNITS * k + u)
                    for what, c in pieces(k, u):
                        name, i = parts(what)
                        b = c // 2
                        if what == "attn_out":
                            for tb in range(TB):
                                free("a_read", TB * c + tb + 1)
                                t0 = (c % 2) * CH + tb * P
                                pe.matmul(bank("a_read", TB * c + tb + 1), HN[64 * b:64 * b + 64, t0:t0 + P],
                                          woutT[64 * b:64 * b + 64, :], start=True, stop=True
                                          ).then_inc(s["attn_out"], 1)
                        elif what == "turn_xn":
                            for tb in range(TB):
                                pe.wait_ge(s["xn"], TB * c + tb + 1)
                                free("xt", TB * c + tb + 1)
                                turn(bank("xt", TB * c + tb + 1),
                                     lambda e: LR[:, tb, 256 * (e // 2) + e % 2:256 * (e // 2) + 256:2]
                                     ).then_inc(s["turned_xn"], 1)
                        elif name == "ffn":
                            pe.wait_ge(s["weff_ready"], 4)
                            pe.wait_ge(s["xt"], TB * c + i + 1)
                            free("ffn0_copied", TB * c + i + 1)
                            for e in range(4):
                                last = pe.matmul(bank("ffn0_copied", TB * c + i + 1),
                                                 HT[:, c % 2, e, i * P:(i + 1) * P], weff[:, e, :],
                                                 start=e == 0, stop=e == 3)
                            last.then_inc(s["ffn0_prod"], 1)
                        elif what == "turn_x2":
                            for tb in range(TB):
                                pe.wait_ge(s["x2n"], TB * c + tb + 1)
                                free("ht", TB * c + tb + 1)
                                turn(bank("ht", TB * c + tb + 1), lambda e: LR[:, tb, e * P:(e + 1) * P]
                                     ).then_inc(s["turned_x2"], 1)
                        elif name == "in":
                            slot, ld, v = loaded("ip", c, i // 2)
                            if i % 2 == 0:
                                pe.wait_ge(ld, v)
                                pe.wait_ge(s["ht"], TB * (c + 1))
                            wi = ring[:, slot, :].rearrange("p (k n) -> p k n", k=KT)
                            free("in_copied", 4 * c + i + 1)
                            dst = bank("in_copied", 4 * c + i + 1)
                            for e in range(2):
                                o = ((2 * i + e) % HCT) * P
                                for kk in range(KT):
                                    last = pe.matmul(dst[:, e * CH:(e + 1) * CH], wi[:, kk, o:o + P],
                                                     HT[:, c % 2, kk, :], start=kk == 0, stop=kk == KT - 1)
                            last.then_inc(in_done(c, i)[0], 1)
                        elif what == "x_proj":
                            pe.wait_ge(s["xc"], 4 * (c + 1))
                            free("sp", c + 1)
                            dst = bank("sp", c + 1)
                            for tb in range(TB):
                                for e in range(CT):
                                    last = pe.matmul(dst[:, 64 * tb:64 * tb + 64], XC[:, e, tb * P:(tb + 1) * P],
                                                     xpT[:, e, :], start=e == 0, stop=e == CT - 1)
                            last.then_inc(s["xp_prod"], 1)
                        elif what == "turn_bc":
                            pe.wait_ge(s["spn"], 6 * (c + 1))
                            free("dr", c + 1)
                            dst = bank("dr", c + 1)
                            for tb in range(TB):
                                last = pe.transpose(dst[0:48, tb * P:(tb + 1) * P], SPN[:, c % 2, tb, 0:48], ident)
                            last.then_inc(s["turned_bc"], 1)
                        elif what in ("dt0", "dt1"):
                            pe.wait_ge(s["dr"], c + 1)
                            for m in (2 * i, 2 * i + 1):
                                free("dt_split", 4 * c + m + 1)
                                dst = bank("dt_split", 4 * c + m + 1)
                                for e in range(2):
                                    o = (2 * m + e) * P
                                    last = pe.matmul(dst[:, e * CH:(e + 1) * CH], dpT[:, o:o + P], DR[0:RK, :],
                                                     start=True, stop=True)
                                last.then_inc(s["dt_prod"], 1)
                        elif name == "skip":
                            pe.wait_ge(s["diag_ready"], 1)
                            for h in range(2):
                                r = 4 * c + 2 * i + h + 1
                                free("skip_copied", r)
                                for e in range(HCT):
                                    last = pe.matmul(bank("skip_copied", r)[:, e * P:(e + 1) * P],
                                                     XC[:, HCT * h + e, i * P:(i + 1) * P],
                                                     diagD[:, HCT * h + e, :], start=True, stop=True)
                                last.then_inc(s["skip_prod"], 1)
                        elif name == "z":
                            h, tb = i // 2, i % 2
                            slot, ld, v = loaded("ip", c, 2 + h)
                            pe.wait_ge(ld, v)
                            wi = ring[:, slot, :].rearrange("p (k n) -> p k n", k=KT)
                            free("z_read", 4 * c + i + 1)
                            for kk in range(KT):
                                last = pe.matmul(bank("z_read", 4 * c + i + 1), HT[:, c % 2, kk, tb * P:(tb + 1) * P],
                                                 wi[:, kk, :], start=kk == 0, stop=kk == KT - 1)
                            last.then_inc(z_done(c, i)[0], 1)
                        elif name == "turn_y":
                            for h in range(2):
                                r = 4 * c + 2 * i + h + 1
                                pe.wait_ge(s["gated"], 4 * c + 2 * h + i + 1)
                                free("yt", r)
                                turn(bank("yt", r), lambda e: Y[:, c % 2, i, h * 512 + e * P:h * 512 + (e + 1) * P]
                                     ).then_inc(s["turned_y"], 1)
                        elif name == "out":
                            tb, h = i // 2, i % 2
                            if h == 0:
                                free("out_copied", TB * c + tb + 1)
                            slot, ld, v = loaded("op", c, h)
                            pe.wait_ge(ld, v)
                            pe.wait_ge(s["yt"], 4 * c + 2 * tb + h + 1)
                            wo = ring[:, slot, :].rearrange("p (k n) -> p k n", k=HCT)
                            for e in range(HCT):
                                last = pe.matmul(bank("out_copied", TB * c + tb + 1),
                                                 XC[:, HCT * h + e, tb * P:(tb + 1) * P], wo[:, e, :],
                                                 start=h == 0 and e == 0, stop=h == 1 and e == HCT - 1)
                            if tb == 1:
                                last.then_inc(freed("op", c, h)[0], 1)
                            elif h == 1:
                                last.then_inc(s["out_prod"], 1)
                        elif what == "turn_x3":
                            for tb in range(TB):
                                pe.wait_ge(s["x3n"], TB * c + tb + 1)
                                free("xf", TB * c + tb + 1)
                                turn(bank("xf", TB * c + tb + 1), lambda e: LP[:, tb, e * P:(e + 1) * P]
                                     ).then_inc(s["turned_x3"], 1)
                        elif name == "g":
                            slot, ld, v = loaded("w", c, i)
                            pe.wait_ge(ld, v)
                            pe.wait_ge(s["xf"], TB * (c + 1))
                            g = NJ * c + i
                            if g >= 2:
                                pe.wait_ge(s["hj"], g - 1)
                            for e in range(2):
                                for kk in range(KT):
                                    last = pe.matmul(PS[:, GUB[g % 2], e * CH:(e + 1) * CH],
                                                     ring[:, slot, (e * KT + kk) * P:(e * KT + kk + 1) * P],
                                                     XF[:, kk, :], start=kk == 0, stop=kk == KT - 1)
                            last.then_inc(s["gu_prod"], 1)
                        elif name == "w":
                            slot, _, _ = loaded("w", c, i)
                            g = NJ * c + i
                            pe.wait_ge(s["hj"], g + 1)
                            if i == 0 and c >= 1:
                                pe.wait_ge(s["y_copied"], TB * c)
                            for tb in range(TB):
                                last = pe.matmul(PS[:, YAB[tb], :], HJ[:, g % 2, tb * P:(tb + 1) * P],
                                                 ring[:, slot, 1024:1536], start=i == 0, stop=i == NJ - 1)
                            last.then_inc(freed("w", c, i)[0], 1)

        @block.scalar
        def _(act):
            step = [0]

            def link(ins):
                step[0] += 1
                ins.then_inc(s["act_step"], 1)
                act.wait_ge(s["act_step"], step[0])

            act.wait_ge(s["cst_in"], 16)
            link(act.activation(NA[:, :], C("A_log"), ACT.Exp))
            act.mul(NA[:, :], NA[:, :], -1.0).then_inc(s["na_exp"], 1)
            act.wait_ge(s["unit"], 1)
            link(act.activation(pz[:, 1, :], pz[:, 0, :], ACT.Ln))
            act.activation(pz[:, 1, :], pz[:, 1, :], ACT.Exp, scale=-0.5).then_inc(s["table_in"], 1)
            act.wait_ge(s["unit"], 2)
            act.activation(pz[:, 8, :], pz[:, 7, :], ACT.Exp, scale=-2.0).then_inc(s["table_in"], 1)
            for t in range(TOK // P):
                act.wait_ge(s["xn0_turned"], t + 1)
                act.activation(XT0[:, t // 4, :, (t % 4) * P:(t % 4 + 1) * P],
                               bank("xt0_copied", t + 1).rearrange("p (k t) -> p k t", k=KT), ACT.Copy
                               ).then_inc(s["xt0_copied"], 1)

            def norm0(i):
                act.wait_ge(s["centred"], i + 1)
                act.activation(SQ, PS[:, 0, :], ACT.Square).then_inc(s["squared"], 1)
                act.wait_ge(s["variance"], i + 1)
                link(act.activation(RSTD, PS[:, 1, :], ACT.Ln, bias=C("eps")))
                act.activation(RSTD, RSTD, ACT.Exp, scale=-0.5).then_inc(s["rstd0"], 1)

            for l in range(DEPTH):
                norm0(2 * l)
                act.wait_ge(s["normed"], 3 * l + 2)
                act.activation(T0, Z, ACT.Tanh, scale=0.5).then_inc(s["tanh0"], 1)
                norm0(2 * l + 1)
                for m in range(4):
                    act.wait_ge(s["hidden_sum"], 4 * l + m + 1)
                    act.activation(hth[:, m, :], PS[:, 4 + m, :], ACT.Tanh, scale=0.5,
                                   bias=b1h[:, 2 * l + m % 2:2 * l + m % 2 + 1]).then_inc(s["tanh0"], 1)
            norm0(2 * DEPTH)

            def decays(g):
                k, u = g // UNITS, g % UNITS
                n, h = u // 2, u % 2
                if u == 0:
                    act.wait_ge(s["dt_ready"], k + 1)
                    if k == 0:
                        act.wait_ge(s["na_exp"], 1)
                if g >= DRING:
                    act.wait_ge(s["states"], g - DRING + 1)
                for i in range(HCT):
                    ct = HCT * h + i
                    last = act.activation(DA[:, g % DRING, i, :], DT[:, k % 2, ct, :], ACT.Exp,
                                          scale=NA[:, ct * NS + n:ct * NS + n + 1])
                last.then_inc(s["decay"], 1)

            for k in ROUNDS:
                for u in range(UNITS):
                    if 0 <= k < NCHUNK:
                        if u == 0:
                            decays(UNITS * k)
                            decays(UNITS * k + 1)
                        if u + 2 < UNITS:
                            decays(UNITS * k + u + 2)
                    for what, c in pieces(k, u):
                        name, i = parts(what)
                        if what == "turn_xn":
                            for tb in range(TB):
                                act.wait_ge(s["turned_xn"], TB * c + tb + 1)
                                if c >= 2 and tb == 0:
                                    act.wait_ge(*z_done(c - 2, 3))
                                if c == 1 and tb == 0:
                                    act.wait_ge(s["weff_ready"], 4)
                                act.activation(HT[:, c % 2, :, tb * P:(tb + 1) * P],
                                               bank("xt", TB * c + tb + 1).rearrange("p (k t) -> p k t", k=KT),
                                               ACT.Copy).then_inc(s["xt"], 1)
                        elif name == "ffn":
                            act.wait_ge(s["ffn0_prod"], TB * c + i + 1)
                            act.activation(LR[:, i, :], bank("ffn0_copied", TB * c + i + 1), ACT.Copy
                                           ).then_inc(s["ffn0_copied"], 1)
                        elif what == "turn_x2":
                            for tb in range(TB):
                                act.wait_ge(s["turned_x2"], TB * c + tb + 1)
                                act.wait_ge(s["ffn0_prod"], TB * (c + 1))
                                act.activation(HT[:, c % 2, :, tb * P:(tb + 1) * P],
                                               bank("ht", TB * c + tb + 1).rearrange("p (k t) -> p k t", k=KT),
                                               ACT.Copy).then_inc(s["ht"], 1)
                        elif name == "in":
                            act.wait_ge(*in_done(c, i))
                            if i == 0:
                                act.wait_ge(s["carry"], c + 1)
                            act.activation(XI[:, 2 * i:2 * i + 2, 3:3 + CH],
                                           bank("in_copied", 4 * c + i + 1).rearrange("p (e t) -> p e t", e=2),
                                           ACT.Copy).then_inc(s["in_copied"], 1)
                        elif name == "conv":
                            act.wait_ge(s["conv"], 4 * c + i + 1)
                            act.activation(TH[:, :, :], XC[:, 2 * i:2 * i + 2, :], ACT.Tanh, scale=0.5
                                           ).then_inc(s["conv_tanh"], 1)
                        elif what == "x_proj":
                            act.wait_ge(s["xp_prod"], c + 1)
                            act.activation(SP[:, :, :],
                                           bank("sp", c + 1)[:, 0:64 * TB].rearrange("p (b e) -> p b e", b=TB),
                                           ACT.Copy).then_inc(s["sp"], 1)
                        elif what == "turn_bc":
                            act.wait_ge(s["turned_bc"], c + 1)
                            if c:
                                act.wait_ge(s["b_stored"], 16 * c)
                                act.wait_ge(s["dt_prod"], 4 * c)
                            act.activation(DR[:, :], bank("dr", c + 1)[0:48, 0:CH], ACT.Copy).then_inc(s["dr"], 1)
                        elif what in ("dt0", "dt1"):
                            if i == 0:
                                if c >= 2:
                                    act.wait_ge(s["states"], UNITS * (c - 1))
                                act.wait_ge(s["tail_kept"], c + 1)
                            for m in (2 * i, 2 * i + 1):
                                act.wait_ge(s["dt_prod"], 4 * c + m + 1)
                                src = bank("dt_split", 4 * c + m + 1)
                                for e in range(2):
                                    ct = 2 * m + e
                                    act.activation(XI[:, ct, 3:3 + CH], src[:, e * CH:(e + 1) * CH], ACT.Abs,
                                                   bias=C("dt_bias", ct))
                                    last = act.activation(DT[:, c % 2, ct, :], src[:, e * CH:(e + 1) * CH],
                                                          ACT.Relu, bias=C("dt_bias", ct))
                                last.then_inc(s["dt_split"], 1)
                        elif what == "dt_log":
                            act.wait_ge(s["dt_split"], 4 * (c + 1))
                            link(act.activation(XI[:, :, 3:3 + CH], XI[:, :, 3:3 + CH], ACT.Exp, scale=-1.0))
                            act.activation(XI[:, :, 3:3 + CH], XI[:, :, 3:3 + CH], ACT.Ln, bias=1.0
                                           ).then_inc(s["dt_log"], 1)
                        elif name == "skip":
                            for h in range(2):
                                r = 4 * c + 2 * i + h + 1
                                act.wait_ge(s["skip_prod"], r)
                                if r == 4 * c + 1 and c >= 2:
                                    act.wait_ge(s["turned_y"], 4 * (c - 1))
                                act.activation(Y[:, c % 2, i, h * 512:h * 512 + 512], bank("skip_copied", r), ACT.Copy
                                               ).then_inc(s["skip_copied"], 1)
                        elif name == "z":
                            r = 4 * c + i + 1
                            act.wait_ge(*z_done(c, i))
                            if r > 2:
                                act.wait_ge(s["gated"], r - 2)
                            act.activation(G[:, r % 2, :], bank("z_read", r), ACT.Tanh, scale=0.5
                                           ).then_inc(s["z_tanh"], 1)
                        elif name == "turn_y":
                            for h in range(2):
                                r = 4 * c + 2 * i + h + 1
                                act.wait_ge(s["turned_y"], r)
                                if r == 4 * c + 1:
                                    d = min(c + 1, NCHUNK - 1)
                                    act.wait_ge(s["skip_prod"], 4 * (d + 1))
                                    act.wait_ge(s["dtx"], d + 1)
                                act.activation(XC[:, HCT * h:HCT * h + HCT, i * P:(i + 1) * P],
                                               bank("yt", r).rearrange("p (k t) -> p k t", k=HCT),
                                               ACT.Copy).then_inc(s["yt"], 1)
                        elif name == "out" and i % 2:
                            tb = i // 2
                            act.wait_ge(*out_done(c, tb))
                            if c and tb == 0:
                                act.wait_ge(s["result"], TB * c)
                            if c == 0 and tb == 0:
                                act.wait_ge(s["weff_ready"], 4)
                            act.activation(LP[:, tb, :], bank("out_copied", TB * c + tb + 1), ACT.Copy
                                           ).then_inc(s["out_copied"], 1)
                        elif what == "turn_x3":
                            for tb in range(TB):
                                act.wait_ge(s["turned_x3"], TB * c + tb + 1)
                                if c and tb == 0:
                                    act.wait_ge(s["gu_prod"], NJ * c)
                                act.activation(XF[:, :, tb * P:(tb + 1) * P],
                                               bank("xf", TB * c + tb + 1).rearrange("p (k t) -> p k t", k=KT),
                                               ACT.Copy).then_inc(s["xf"], 1)
                        elif name == "g":
                            g = NJ * c + i
                            act.wait_ge(s["gu_prod"], g + 1)
                            if g >= 2:
                                act.wait_ge(s["hj"], g - 1)
                            act.activation(GT[:, g % 2, :], PS[:, GUB[g % 2], 0:CH], ACT.Tanh, scale=0.5
                                           ).then_inc(s["gate_tanh"], 1)
                        elif what == "y_done":
                            act.wait_ge(*freed("w", c, NJ - 1))
                            act.wait_ge(s["turned_x3"], TB * (c + 1))
                            for tb in range(TB):
                                act.activation(LP[:, tb, :], PS[:, YAB[tb], :], ACT.Copy).then_inc(s["y_copied"], 1)

        @block.gpsimd
        def _(pool):
            step = [0]

            def link(ins):
                step[0] += 1
                ins.then_inc(s["pool_step"], 1)
                pool.wait_ge(s["pool_step"], step[0])

            link(pool.memset(half[:, :], -0.5))
            pool.memset(cv[:, :, :], 0.0)
            link(pool.memset(HC[:, :, :], 0.0))
            pool.wait_ge(s["cst_in"], 16)

            def rstd(st, v, dst, src, n, done):
                pool.wait_ge(s[st], v)
                pool.tensor_tensor(dst, src, half[:, 0:n], ALU.pow).then_inc(s[done], 1)

            for i in range(4):
                rstd("ln0_stats", i + 1, RS[:, i, :], VE[:, i, :], TB, "ln0_rstd")
            for ct in range(CT):
                last = pool.tensor_scalar(diagD[:, ct, :], ident, C("D", ct), None, ALU.mult)
            last.then_inc(s["diag_ready"], 1)
            pool.wait_ge(s["misc_in"], 48)
            for j in range(NJ):
                pool.wait_ge(s[f"pw{j % SLOTS}"], 16 * (j // SLOTS + 1))
                w = ring[:, j % SLOTS, 0:1536].rearrange("p (q m) -> p q m", q=12)
                pool.tensor_tensor(w, w, scb[:, 12 * j:12 * j + 12][:, :, None].to_broadcast((P, 12, P)), ALU.mult
                                   ).then_inc(s["scaled"], 1)

            def inputs(g):
                k, u = g // UNITS, g % UNITS
                n, h = u // 2, u % 2
                pair = 8 * k + n // 2
                if u == 0:
                    pool.wait_ge(s["dtx"], k + 1)
                if u % 4 == 0:
                    pool.wait_ge(s[f"bb{pair % 2}"], 16 * (pair // 2 + 1))
                if g >= BRING:
                    pool.wait_ge(s["states"], g - BRING + 1)
                pool.tensor_tensor(DBX[:, g % BRING, :, :], DTX[:, k % 2, HCT * h:HCT * h + HCT, :],
                                   BB[:, pair % 2, n % 2, :][:, None, :].to_broadcast((P, HCT, CH)), ALU.mult
                                   ).then_inc(s["dbx"], 1)

            def keep(g):
                pool.wait_ge(s["states"], g + 1)
                pool.tensor_copy(HC[:, g % UNITS, :], H[:, g % 2, :, CH - 1]).then_inc(s["state_kept"], 1)

            for k in ROUNDS:
                for u in range(UNITS):
                    if 0 <= k < NCHUNK:
                        if u == 0:
                            inputs(UNITS * k)
                            inputs(UNITS * k + 1)
                        if u + 2 < UNITS:
                            inputs(UNITS * k + u + 2)
                        keep(UNITS * k + u)
                    for what, c in pieces(k, u):
                        if what in RSTD_OF:
                            kind, i = RSTD_OF[what]
                            rstd(kind + "_stats", c + 1, RS[:, i, :], VE[:, i, :], TB, kind + "_rstd")
                        elif what == "in0":
                            if c:
                                pool.wait_ge(s["dt_ready"], c)
                            pool.tensor_scalar(XI[:, :, 0:3], cv[:, :, :], 0.0 if c % 2 == 0 else 1.0, None, ALU.mult
                                               ).then_inc(s["carry"], 1)
                        elif what == "x_proj":
                            pool.wait_ge(s["conv"], 4 * (c + 1))
                            pool.tensor_copy(cv[:, :, :], XI[:, :, CH:CH + 3]).then_inc(s["tail_kept"], 1)
                        elif what == "ms":
                            rstd("ms", c + 1, MSR[:, :, :].rearrange("p a b -> p (a b)"),
                                 MS[:, :, :].rearrange("p a b -> p (a b)"), 3 * TB, "ms_rstd")

        @block.vector
        def _(dve):
            step = [0]

            def mark(ins):
                step[0] += 1
                ins.then_inc(s["dve_step"], 1)

            def settle():
                dve.wait_ge(s["dve_step"], step[0])

            def link(ins):
                mark(ins)
                settle()

            def tt(o, x, y, op):
                return dve.tensor_tensor(o, x, y, op)

            def ts(o, x, s1, s2, op0, op1=None):
                return dve.tensor_scalar(o, x, s1, s2, op0) if op1 is None else dve.tensor_scalar(o, x, s1, s2, op0, op1)

            def stt(o, x, sc, y, op0, op1):
                return dve.scalar_tensor_tensor(o, x, sc, y, op0, op1)

            def stats(src, i, eps, done):
                for tb in range(TB):
                    mark(dve.bn_stats(BS[:, i, tb, :], src(tb)))
                settle()
                for tb in range(TB):
                    mark(dve.bn_aggr(MV[:, i, tb, :], BS[:, i, tb, :]))
                settle()
                ts(VE[:, i, :], MV[:, i, :, 1], eps, None, ALU.add).then_inc(s[done], 1)

            def normalise(dst, src, i, tb):
                return ts(dst, src, MV[:, i, tb, 0:1], RS[:, i, tb:tb + 1], ALU.subtract, ALU.mult)

            dve.wait_ge(s["cst_in"], 16)
            re, im = C("phz_re"), C("phz_im")
            mark(tt(pz[:, 2, :], re, re, ALU.mult))
            mark(tt(pz[:, 3, :], im, im, ALU.mult))
            settle()
            link(tt(pz[:, 4, :], pz[:, 2, :], pz[:, 3, :], ALU.add))
            ts(pz[:, 0, :], pz[:, 4, :], 1e-19, None, ALU.max).then_inc(s["unit"], 1)
            mark(ts(pz[:, 5, :], pz[:, 4, :], 1e-19, None, ALU.is_gt))
            mark(ts(pz[:, 6, :], pz[:, 4, :], 1e-19, None, ALU.is_le))
            mark(ts(b1h[:, :], C("b1"), 0.5, None, ALU.mult))
            dve.wait_ge(s["table_in"], 1)
            for _ in range(2):
                link(tt(pz[:, 9, :], pz[:, 1, :], pz[:, 1, :], ALU.mult))
                link(tt(pz[:, 9, :], pz[:, 9, :], pz[:, 0, :], ALU.mult))
                link(ts(pz[:, 9, :], pz[:, 9, :], -0.5, 1.5, ALU.mult, ALU.add))
                link(tt(pz[:, 1, :], pz[:, 1, :], pz[:, 9, :], ALU.mult))
            tt(pz[:, 7, :], pz[:, 4, :], pz[:, 1, :], ALU.mult).then_inc(s["unit"], 1)
            link(tt(pz[:, 10, :], pz[:, 1, :], pz[:, 5, :], ALU.mult))
            for F in (FR, CR):
                mark(dve.memset(F[:, :, 0:1], 1.0))
            for F in (FI, CI):
                mark(dve.memset(F[:, :, 0:1], 0.0))
            mark(tt(FR[:, :, 1], re, pz[:, 10, :], ALU.mult))
            mark(tt(FI[:, :, 1], im, pz[:, 10, :], ALU.mult))
            settle()
            link(tt(FR[:, :, 1], FR[:, :, 1], pz[:, 6, :], ALU.add))
            dve.wait_ge(s["table_in"], 2)
            link(ts(pz[:, 11, :], pz[:, 8, :], 1.0, None, ALU.add))
            link(dve.reciprocal(pz[:, 11, :], pz[:, 11, :]))
            link(ts(pz[:, 12, :], pz[:, 8, :], -1.0, 1.0, ALU.mult, ALU.add))
            mark(tt(pz[:, 12, :], pz[:, 12, :], pz[:, 11, :], ALU.mult))
            settle()

            def cmul(outs, x, y, shape):
                (xr, xi), (yr, yi) = x, y
                n = 1
                for d in shape:
                    n *= d
                tmp = [t[:, 0:n] for t in tt4]
                if len(shape) == 2:
                    tmp = [t.rearrange("p (a b) -> p a b", a=shape[0]) for t in tmp]
                mark(tt(tmp[0], xr, yr, ALU.mult))
                mark(tt(tmp[1], xi, yi, ALU.mult))
                mark(tt(tmp[2], xr, yi, ALU.mult))
                mark(tt(tmp[3], xi, yr, ALU.mult))
                settle()
                mark(tt(outs[0], tmp[0], tmp[1], ALU.subtract))
                mark(tt(outs[1], tmp[2], tmp[3], ALU.add))
                settle()

            def powers(R, I, top):
                m = 1
                while m < top:
                    bc = (P, DEPTH, m)
                    cmul((R[:, :, m + 1:2 * m + 1], I[:, :, m + 1:2 * m + 1]),
                         (R[:, :, 1:m + 1], I[:, :, 1:m + 1]),
                         (R[:, :, m:m + 1].to_broadcast(bc), I[:, :, m:m + 1].to_broadcast(bc)), (DEPTH, m))
                    m *= 2

            for i in range(4):
                if i % 2 == 0:
                    dve.wait_ge(s[f"x_in{i // 2}"], 16)
                stats(lambda tb: XR[:, 2 * i + tb, :], i, 1e-5, "ln0_stats")
            for i in range(4):
                dve.wait_ge(s["ln0_rstd"], i + 1)
                for tb in range(TB):
                    normalise(XN0[:, 2 * i + tb, :], XR[:, 2 * i + tb, :], i, tb).then_inc(s["xn0"], 1)

            powers(FR, FI, FINE)
            mark(dve.tensor_copy(CR[:, :, 1], FR[:, :, FINE]))
            link(dve.tensor_copy(CI[:, :, 1], FI[:, :, FINE]))
            powers(CR, CI, COARSE)

            def table(l):
                shape = (P, COARSE, FINE)
                cr = CR[:, l, 0:COARSE][:, :, None].to_broadcast(shape)
                ci = CI[:, l, 0:COARSE][:, :, None].to_broadcast(shape)
                fr = FR[:, l, 0:FINE][:, None, :].to_broadcast(shape)
                fi = FI[:, l, 0:FINE][:, None, :].to_broadcast(shape)
                cmul((COS[:, l, :].rearrange("p (a b) -> p a b", a=COARSE),
                      SIN[:, l, :].rearrange("p (a b) -> p a b", a=COARSE)), (cr, ci), (fr, fi), (COARSE, FINE))

            cmul((pz[:, 13, :], pz[:, 14, :]), (C("lc_re"), C("lc_im")), (FR[:, :, 1], FI[:, :, 1]), (DEPTH,))
            link(ts(pz[:, 14, :], pz[:, 14, :], -1.0, None, ALU.mult))

            dve.wait_ge(s["h_in"], 1)
            ts(Hs, PS[:, 0, :], C("bin"), None, ALU.add).then_inc(s["h_new"], 1)

            def unpack(par):
                if par == 0:
                    dve.wait_ge(s["deq_in"], 16 * 7)
                w = weff[:, :, :].rearrange("p (h e) o -> p e h o", e=2)[:, par, :, :]
                link(ts(codes, packed, 4 * par, 7, ALU.logical_shift_right, ALU.bitwise_and))
                mark(ts(w, codes, 0.5, None, ALU.mult))
                mark(ts(fieldf, codes, 4.0, 0.0, ALU.subtract, ALU.max))
                mark(ts(dtmp, codes, 6.0, 0.0, ALU.subtract, ALU.max))
                settle()
                link(stt(w, fieldf, 0.5, w, ALU.mult, ALU.add))
                mark(tt(w, w, dtmp, ALU.add))
                mark(ts(codes, packed, 4 * par + 3, 1, ALU.logical_shift_right, ALU.bitwise_and))
                settle()
                mark(ts(fieldf, codes, -2.0, 1.0, ALU.mult, ALU.add))
                link(tt(dtmp, bsc, w, ALU.mult))
                link(tt(w, dtmp, fieldf, ALU.mult))
                link(ts(w, w, gsb[:, 0:1], None, ALU.mult))

            def add_lora(i):
                dve.wait_ge(s["lora_prod"], i + 1)
                tt(weff[:, i, :], weff[:, i, :], bank("weff_ready", i + 1), ALU.add).then_inc(s["weff_ready"], 1)

            for l in range(DEPTH):
                table(l)
                dve.wait_ge(s["rstd0"], 2 * l + 1)
                tt(S, PS[:, 0, :], RSTD, ALU.mult).then_inc(s["normed"], 1)
                dve.wait_ge(s["normed"], 3 * l + 1)
                if l:
                    dve.wait_ge(s["hidden_sum"], 4 * l)
                ts(Z, S, C("ln1_w", l), C("ln1_b", l), ALU.mult, ALU.add).then_inc(s["normed"], 1)
                dve.wait_ge(s["tanh0"], 5 * l + 1)
                link(stt(S, T0, 1.0, Z, ALU.add, ALU.mult))
                mark(stt(MR, S, 0.5, COS[:, l, :], ALU.mult, ALU.mult))
                mark(stt(MI, S, 0.5, SIN[:, l, :], ALU.mult, ALU.mult))
                settle()
                decay = pz[:, 12, l:l + 1].to_broadcast((P, SEQ))
                mark(dve.tensor_tensor_scan(UR, decay, MR, pz[:, 13, l:l + 1], ALU.mult, ALU.add))
                mark(dve.tensor_tensor_scan(VI, decay, MI, pz[:, 14, l:l + 1], ALU.mult, ALU.add))
                settle()
                mark(tt(UR, UR, COS[:, l, :], ALU.mult))
                mark(tt(VI, VI, SIN[:, l, :], ALU.mult))
                settle()
                link(tt(UR, UR, VI, ALU.add))
                stt(Hs, UR, C("scl", l), Hs, ALU.mult, ALU.add).then_inc(s["h_new"], 1)
                dve.wait_ge(s["h_new"], 2 * l + 2)
                mark(ts(HB, Hs, C("b2", l), None, ALU.add))
                if l == 0:
                    unpack(0)
                    unpack(1)
                if l == 1:
                    for i in range(4):
                        add_lora(i)
                dve.wait_ge(s["rstd0"], 2 * l + 2)
                link(tt(S, PS[:, 0, :], RSTD, ALU.mult))
                ts(Z, S, C("ln2_w", l), C("ln2_b", l), ALU.mult, ALU.add).then_inc(s["normed"], 1)
                for m in range(4):
                    bias = C("b1", 2 * l + m % 2)
                    dve.wait_ge(s["tanh0"], 5 * l + 2 + m)
                    link(stt(hth[:, m, :], PS[:, 4 + m, :], bias, hth[:, m, :], ALU.add, ALU.mult))
                    if l:
                        dve.wait_ge(s["ffn_sum"], l)
                    stt(hid[:, m, :], PS[:, 4 + m, :], bias, hth[:, m, :], ALU.add, ALU.add).then_inc(s["hidden"], 1)
                dve.wait_ge(s["ffn_sum"], l + 1)
                stt(Hs, PS[:, 1, :], 0.5, HB, ALU.mult, ALU.add).then_inc(s["h_new"], 1)
            dve.wait_ge(s["rstd0"], 2 * DEPTH + 1)
            link(tt(S, PS[:, 0, :], RSTD, ALU.mult))
            ts(HN[:, :], S, C("lnl_w"), C("lnl_b"), ALU.mult, ALU.add).then_inc(s["hn"], 1)

            def scan(g):
                k, u = g // UNITS, g % UNITS
                dve.wait_ge(s["decay"], g + 1)
                dve.wait_ge(s["dbx"], g + 1)
                if g >= 2:
                    dve.wait_ge(s["turned_h"], 2 * (g - 1))
                    dve.wait_ge(s["state_kept"], g - 1)
                for i in range(HCT):
                    first = HC[:, u, i:i + 1] if k % 2 else 0.0
                    last = dve.tensor_tensor_scan(H[:, g % 2, i, :], DA[:, g % DRING, i, :], DBX[:, g % BRING, i, :],
                                                  first, ALU.mult, ALU.add)
                last.then_inc(s["states"], 1)

            def add_y(g):
                k, u = g // UNITS, g % UNITS
                n, h = u // 2, u % 2
                if u == 0:
                    dve.wait_ge(s["skip_copied"], 4 * (k + 1))
                for tb in range(TB):
                    dve.wait_ge(s["turned_h"], 2 * g + tb + 1)
                    if u >= 2:
                        dve.wait_ge(s["y_sum"], 2 * (g - 2) + tb + 1)
                    y = Y[:, k % 2, tb, 512 * h:512 * h + 512]
                    cn = SPN[:, k % 2, tb, 48 + n:49 + n]
                    stt(y, PS[:, TR[tb], :], cn, y, ALU.mult, ALU.add).then_inc(s["y_sum"], 1)

            def norm_and_add(src, i, c, stat):
                for tb in range(TB):
                    mark(normalise(src[:, tb, :], src[:, tb, :], i, tb))
                settle()
                for tb in range(TB):
                    x = XR[:, TB * c + tb, :]
                    mark(tt(x, x, src[:, tb, :], ALU.add))
                settle()
                stats(lambda tb: XR[:, TB * c + tb, :], i + 1, 1e-5, stat)

            for k in ROUNDS:
                for u in range(UNITS):
                    if 0 <= k < NCHUNK:
                        scan(UNITS * k + u)
                        if u:
                            add_y(UNITS * k + u - 1)
                        if u == UNITS - 1:
                            add_y(UNITS * k + u)
                    for what, c in pieces(k, u):
                        name, i = parts(what)
                        if what == "a_norm":
                            dve.wait_ge(s["misc_in"], 48)
                            if c:
                                dve.wait_ge(s["turned_x2"], TB * c)
                            for tb in range(TB):
                                dve.wait_ge(s["attn_out"], TB * c + tb + 1)
                                tt(LR[:, tb, :], bank("a_read", TB * c + tb + 1), boutb[:, :], ALU.add
                                   ).then_inc(s["a_read"], 1)
                            dve.wait_ge(s["a_read"], TB * (c + 1))
                            stats(lambda tb: LR[:, tb, :], 0, 1e-5, "r1_stats")
                        elif what == "x1":
                            dve.wait_ge(s["r1_rstd"], c + 1)
                            norm_and_add(LR, 0, c, "r2_stats")
                        elif what == "xn":
                            dve.wait_ge(s["r2_rstd"], c + 1)
                            for tb in range(TB):
                                normalise(LR[:, tb, :], XR[:, TB * c + tb, :], 1, tb).then_inc(s["xn"], 1)
                        elif what == "f_stats":
                            dve.wait_ge(s["ffn0_copied"], TB * (c + 1))
                            stats(lambda tb: LR[:, tb, :], 2, 1e-5, "r3_stats")
                        elif what == "x2":
                            dve.wait_ge(s["r3_rstd"], c + 1)
                            norm_and_add(LR, 2, c, "r4_stats")
                        elif what == "x2n":
                            dve.wait_ge(s["r4_rstd"], c + 1)
                            for tb in range(TB):
                                normalise(LR[:, tb, :], XR[:, TB * c + tb, :], 3, tb).then_inc(s["x2n"], 1)
                        elif name == "conv":
                            if i == 0 and c >= 2:
                                dve.wait_ge(*out_done(c - 2, 1))
                            dve.wait_ge(s["in_copied"], 4 * c + i + 1)
                            for tap in range(4):
                                for e in range(2):
                                    ct = 2 * i + e
                                    wt = convw[:, ct, tap:tap + 1]
                                    if tap == 0:
                                        mark(ts(XC[:, ct, :], XI[:, ct, 0:CH], wt, C("conv_b", ct),
                                                ALU.mult, ALU.add))
                                        continue
                                    ins = stt(XC[:, ct, :], XI[:, ct, tap:tap + CH], wt, XC[:, ct, :],
                                              ALU.mult, ALU.add)
                                    if tap < 3 or e == 0:
                                        mark(ins)
                                    else:
                                        ins.then_inc(s["conv"], 1)
                                if tap < 3:
                                    settle()
                            dve.wait_ge(s["conv_tanh"], 4 * c + i + 1)
                            link(stt(TH[:, :, :], TH[:, :, :], 1.0, XC[:, 2 * i:2 * i + 2, :], ALU.add, ALU.mult))
                            ts(XC[:, 2 * i:2 * i + 2, :], TH[:, :, :], 0.5, None, ALU.mult).then_inc(s["xc"], 1)
                            dve.wait_ge(s["xc"], 4 * c + i + 1)
                        elif what == "ms":
                            dve.wait_ge(s["sp"], c + 1)
                            tmp = TH[:, 0, 0:64 * TB].rearrange("p (b e) -> p b e", b=TB)
                            link(tt(tmp, SP[:, :, :], SP[:, :, :], ALU.mult))
                            for e, (lo, hi) in enumerate(SEGS):
                                mark(dve.tensor_reduce(MS[:, e, :], tmp[:, :, lo:hi], AX_X, ALU.add))
                            settle()
                            link(ts(MS[:, 0, :], MS[:, 0, :], 1.0 / RK, 1e-6, ALU.mult, ALU.add))
                            ts(MS[:, 1:3, :], MS[:, 1:3, :], 1.0 / NS, 1e-6, ALU.mult, ALU.add).then_inc(s["ms"], 1)
                        elif what == "norm_bc":
                            dve.wait_ge(s["ms_rstd"], c + 1)
                            for e, (lo, hi) in enumerate(SEGS):
                                for tb in range(TB):
                                    stt(SPN[:, c % 2, tb, lo:hi], SP[:, tb, lo:hi], MSR[:, e, tb:tb + 1],
                                        rmsb[:, lo:hi], ALU.mult, ALU.mult).then_inc(s["spn"], 1)
                        elif what == "dtx":
                            dve.wait_ge(s["dt_log"], c + 1)
                            tt(DT[:, c % 2, :, :], DT[:, c % 2, :, :], XI[:, :, 3:3 + CH], ALU.add
                               ).then_inc(s["dt_ready"], 1)
                            dve.wait_ge(s["dt_ready"], c + 1)
                            tt(DTX[:, c % 2, :, :], DT[:, c % 2, :, :], XC[:, :, :], ALU.mult).then_inc(s["dtx"], 1)
                        elif name == "gate":
                            h, tb = i // 2, i % 2
                            r = 4 * c + i + 1
                            dve.wait_ge(s["z_tanh"], r)
                            stt(G[:, r % 2, :], G[:, r % 2, :], 1.0, bank("z_read", r), ALU.add, ALU.mult
                                ).then_inc(s["z_read"], 1)
                            dve.wait_ge(s["z_read"], r)
                            if i == 0:
                                dve.wait_ge(s["y_sum"], 2 * UNITS * (c + 1))
                            y = Y[:, c % 2, tb, 512 * h:512 * h + 512]
                            stt(y, G[:, r % 2, :], 0.5, y, ALU.mult, ALU.mult).then_inc(s["gated"], 1)
                        elif what == "o_stats":
                            dve.wait_ge(s["out_copied"], TB * (c + 1))
                            stats(lambda tb: LP[:, tb, :], 4, 1e-5, "p5_stats")
                        elif what == "x3":
                            dve.wait_ge(s["p5_rstd"], c + 1)
                            norm_and_add(LP, 4, c, "p6_stats")
                        elif what == "x3n":
                            dve.wait_ge(s["p6_rstd"], c + 1)
                            for tb in range(TB):
                                normalise(LP[:, tb, :], XR[:, TB * c + tb, :], 5, tb).then_inc(s["x3n"], 1)
                        elif name == "h":
                            g = NJ * c + i
                            dve.wait_ge(s["gate_tanh"], g + 1)
                            link(stt(GT[:, g % 2, :], GT[:, g % 2, :], 1.0, PS[:, GUB[g % 2], 0:CH],
                                     ALU.add, ALU.mult))
                            if g >= 2:
                                dve.wait_ge(*freed("w", (g - 2) // NJ, (g - 2) % NJ))
                            stt(HJ[:, g % 2, :], GT[:, g % 2, :], 0.5, PS[:, GUB[g % 2], CH:2 * CH],
                                ALU.mult, ALU.mult).then_inc(s["hj"], 1)
                        elif what == "y_stats":
                            dve.wait_ge(s["y_copied"], TB * (c + 1))
                            stats(lambda tb: LP[:, tb, :], 6, 1e-5, "p7_stats")
                        elif what == "result":
                            dve.wait_ge(s["p7_rstd"], c + 1)
                            for tb in range(TB):
                                mark(normalise(LP[:, tb, :], LP[:, tb, :], 6, tb))
                            settle()
                            for tb in range(TB):
                                x = XR[:, TB * c + tb, :]
                                tt(x, x, LP[:, tb, :], ALU.add).then_inc(s["result"], 1)


def kernel(**inputs):
    import numpy as np
    import concourse.bacc as bacc
    from concourse.bass_utils import run_bass_kernel_spmd

    v = {n: np.ascontiguousarray(np.asarray(x)) for n, x in inputs.items()}
    A0, F0, A1, F1 = "L0_attn_", "L0_ffn_", "L1_attn_", "L1_ffn_"

    def twice(m):
        m = m.reshape(-1, DIM).T
        return np.concatenate([m, m])

    def tiles(m):
        return m.reshape(CT, P, -1).transpose(1, 0, 2).reshape(P, -1)

    one = np.zeros((P, P), np.float32)
    one[:DIM, :DIM] = one[DIM:, DIM:] = 1.0 / DIM
    eye = np.eye(P, dtype=np.float32)
    c = {"ident": eye, "cen": eye - one, "avg": one, "eps": np.full((P, 1), 1e-5, np.float32),
         "bin": twice(v[A0 + "bin"]), "b1": v[A0 + "b1"].reshape(DEPTH * 2, P).T,
         "lnl_w": twice(v[A0 + "lnl_w"]), "lnl_b": twice(v[A0 + "lnl_b"]), "scl": twice(v[A0 + "sc_lin"]),
         "dt_bias": tiles(v[A1 + "dt_bias"]), "D": tiles(v[A1 + "D_param"]), "conv_b": tiles(v[A1 + "conv_b"]),
         "conv_w": tiles(v[A1 + "conv_w"]), "A_log": tiles(v[A1 + "A_log"])}
    for n in ("ln1_w", "ln1_b", "ln2_w", "ln2_b", "b2", "phz_re", "phz_im", "lc_re", "lc_im"):
        c[n] = twice(v[A0 + n])
    cst = np.concatenate([c[n].reshape(P, -1) for n in CST], axis=1)
    assert cst.shape == (P, NCST)

    w1 = v[A0 + "W1"].transpose(2, 0, 1).reshape(DIM, -1)
    w2 = v[A0 + "W2"].reshape(DEPTH, DIM, 2, P).transpose(3, 0, 2, 1).reshape(P, -1)
    wo = v[A0 + "Wout"].T
    win = v[A0 + "Win"].T.reshape(KT, P, DIM).transpose(1, 0, 2).reshape(P, -1)
    wp = np.concatenate([np.concatenate([wo, wo]), tiles(v[A1 + "x_proj_w"].T)], axis=1)
    assert wp.shape == (P, NWP)

    la = v[F0 + "lora_A"].reshape(16, 2, P, 2).transpose(0, 1, 3, 2).reshape(16, 4 * P)
    lw = v[A1 + "dt_proj_w"].T
    packed = v[F0 + "packed_weight"].astype(np.int32).T.reshape(2, P, W)

    ipw = v[A1 + "in_proj_w"].reshape(KT, P, 4, 512).transpose(2, 1, 0, 3).reshape(4, P, 2048)
    opw = v[A1 + "out_proj_w"].T.reshape(2, HCT, P, W).transpose(0, 2, 1, 3).reshape(2, P, 2048)
    g = v[F1 + "w1"].T.reshape(KT, P, NJ, P).transpose(2, 1, 0, 3).reshape(NJ, P, 512)
    u = v[F1 + "w3"].T.reshape(KT, P, NJ, P).transpose(2, 1, 0, 3).reshape(NJ, P, 512)
    d = v[F1 + "w2"].T.reshape(NJ, P, W)
    wq = np.concatenate([g, u, d], axis=2)
    sc = np.concatenate([v[F1 + "w1_scale"], v[F1 + "w3_scale"], v[F1 + "w2_scale"].T], axis=1).reshape(-1)
    arrays = {"cst": cst, "x": v[A0 + "x"].reshape(TOK, W), "wp": wp, "w1": np.concatenate([w1, w1]), "w2": w2,
              "win": win, "lw": lw, "la": la, "lb": v[F0 + "lora_B"].T, "packed": packed,
              "bs": v[F0 + "block_scales"].T, "gs": v[F0 + "global_scale"], "sc": sc, "bout": v[A0 + "bout"],
              "rms": np.concatenate([v[A1 + "dt_ln_w"], v[A1 + "B_ln_w"], v[A1 + "C_ln_w"]]),
              "ip": ipw, "op": opw, "wq": wq}
    arrays = {n: np.ascontiguousarray(x) for n, x in arrays.items()}
    nc = bacc.Bacc("TRN2", target_bir_lowering=False, num_devices=1)
    aps = {n: nc.dram_tensor(f"in_{n}", x.shape, mybir.dt.from_np(x.dtype), kind="ExternalInput").ap()
           for n, x in arrays.items()}
    out = nc.dram_tensor("out_0", (TOK, W), F32, kind="ExternalOutput").ap()
    build(nc, aps, out)
    r = run_bass_kernel_spmd(nc, [{f"in_{n}": x for n, x in arrays.items()}], core_ids=[0])
    return r.results[0]["out_0"].reshape(2, SEQ, W)
```

```python
from contextlib import ExitStack

import concourse.bass as bass
from concourse import mybir

F32 = mybir.dt.float32
I32 = mybir.dt.int32
ALU = mybir.AluOpType
ACT = mybir.ActivationFunctionType
AX_X = mybir.AxisListType.X

P = 128
W = 512
TOK = 1024
SEQ = 512
CH = 256
NCHUNK = TOK // CH
TB = CH // P
KT = W // P
DEPTH, DIM, DFF = 4, 64, 256
DIN, NS, RK = 1024, 16, 32
CT = DIN // P
HCT = CT // 2
INTER = 1792
NJ = INTER // P
SLOTS = 3
UNITS = 2 * NS
DRING = 4
BRING = 3
FINE, COARSE = 32, 16

CST = {}
_at = 0
for _name, _n in [("ident", 128), ("cen", 128), ("avg", 128), ("eps", 1), ("bin", 1),
                  ("ln1_w", 4), ("ln1_b", 4), ("scl", 4), ("ln2_w", 4), ("ln2_b", 4), ("b2", 4),
                  ("phz_re", 4), ("phz_im", 4), ("lc_re", 4), ("lc_im", 4), ("lnl_w", 1), ("lnl_b", 1),
                  ("b1", 8), ("dt_bias", 8), ("D", 8), ("conv_b", 8), ("conv_w", 32), ("A_log", 128)]:
    CST[_name] = (_at, _at + _n)
    _at += _n
NCST = _at
WP = {}
_at = 0
for _name, _n in [("wout", W), ("xp", CT * 64)]:
    WP[_name] = (_at, _at + _n)
    _at += _n
NWP = _at
NLW = DIN

BEFORE = {
    "attn_out": -2.5, "a_norm": -2, "x1": -1, "xn": 0, "turn_xn": 4.4, "ffn0": 5.5, "ffn1": 6.5,
    "f_stats": 8, "x2": 9, "x2n": 10, "turn_x2": 11.2,
    "in0": 12.2, "in1": 13.2, "in2": 14.2, "in3": 15.2,
    "conv0": 14.5, "silu_conv0": 15.1, "conv1": 15.5, "silu_conv1": 16.1, "x_proj0": 16.5,
    "conv2": 17.1, "silu_conv2": 18.1, "conv3": 18.6, "silu_conv3": 19.1, "x_proj1": 19.6, "ms": 21,
    "norm_bc": 22, "turn_bc": 22.5, "dt0": 23.5, "log0": 24, "dt1": 24.5, "dtx0": 25.5, "log1": 25.6, "dtx1": 27,
    "skip0": 26.8, "skip1": 27.5}
BEFORE_FIRST = {0: {"log1": 30.2, "dtx1": 30.3, "skip0": 30.5, "skip1": 31.2},
                1: {"attn_out": 0.5, "a_norm": 1, "x1": 2, "xn": 3}}
AFTER = {
    "z0": 0.5, "z1": 1.5, "silu0": 2.2, "gate0": 2.3, "z2": 2.5, "silu1": 2.8, "gate1": 2.9,
    "z3": 3.5, "silu2": 3.8, "gate2": 3.9, "silu3": 4.3, "gate3": 4.31, "turn_y0": 5.2, "turn_y1": 6.2,
    "out0": 7.2, "out1": 8.2, "out2": 9.2, "out3": 10.2,
    "o_stats": 11, "x3": 12, "x3n": 13, "turn_x3": 14.1}
FIRST_G, PER_BLOCK = 15, 1.2
PACE, PER_LAST, LAST_Z = 0.7, 1.0, (7.2, 8.2, 26.5, 27.5)

TIMES = {}
for _c in range(NCHUNK):
    for _what, _t in (BEFORE | BEFORE_FIRST.get(_c, {})).items():
        TIMES[_what, _c] = UNITS * (_c - 1) + _t
    _pace = PACE if _c == NCHUNK - 2 else 1
    for _what, _t in AFTER.items():
        TIMES[_what, _c] = UNITS * (_c + 1) + _pace * _t
    if _c == NCHUNK - 1:
        for _i, _t in enumerate(LAST_Z):
            TIMES[f"z{_i}", _c] = UNITS * _c + _t
            TIMES[f"silu{_i}", _c] = UNITS * _c + _t + 1.5
    _per = PER_LAST if _c >= NCHUNK - 2 else PER_BLOCK
    for _i in range(NJ):
        _t = UNITS * (_c + 1) + _pace * FIRST_G + _per * _i
        TIMES[f"g{_i}", _c] = _t + 0.7
        TIMES[f"h{_i}", _c] = _t + _per + 0.95
        TIMES[f"w{_i}", _c] = _t + 2 * _per + 0.6
    _t += 2 * _per + 0.7 if _c >= NCHUNK - 2 else max(2 * _per + 0.7, UNITS * (_c + 2) + 4.2 - _t)
    TIMES["y_done", _c] = _t
    TIMES["y_stats", _c] = _t + 1
    TIMES["result", _c] = _t + 2
for _what, _t in (("hide", 3.9), ("act", 5.2), ("ffn", 8.1), ("cen1", 9.1), ("var1", 10.1)):
    TIMES["last_" + _what, 0] = -UNITS + _t
ROUNDS = range(-2, NCHUNK + 2)


def pieces(k, u):
    now = UNITS * k + u
    return [key for key, t in sorted(TIMES.items(), key=lambda e: e[1]) if now <= t < now + 1]


ROUND0 = [("cen2", "Y"), ("cen1", "X"), ("var2", "Y"), ("var1", "X"), ("sig1", "X"), ("turn", "X"), ("hide", "Y"),
          ("scan", "X"), ("act", "Y"), ("add", "X"), ("ffn", "Y")]
ORDER0 = []
for _r in range(2 * DEPTH + 2):
    for _what, _who in ROUND0:
        _h = _r % 2 if _who == "X" else 1 - _r % 2
        _l = _r // 2 if _who == "X" else (_r - 1) // 2
        if _who == "X" and (_l < DEPTH or _what in ("cen1", "var1")) or _who == "Y" and 0 <= _l < DEPTH:
            ORDER0.append((_what, _l, _h))
_n = ORDER0.index(("hide", DEPTH - 1, 1))
ORDER0, _last = ORDER0[:_n], ORDER0[_n:]
LAST0 = {"last_" + step[0]: step for step in _last}
PAIRS0 = (0, 2, 1, 3)
UNPACK = 32
UNPACK_AT = ("var1", "var2", "sig1", "hide", "act")
LORA_AT = (("sig1", 3, 1), ("hide", 3, 0), ("scan", 3, 1), ("act", 3, 0))

RSTD_OF = {"a_norm": ("r1", 0), "x1": ("r2", 1), "f_stats": ("r3", 2), "x2": ("r4", 3),
           "o_stats": ("p5", 4), "x3": ("p6", 5), "y_stats": ("p7", 6)}


def parts(what):
    name = what.rstrip("0123456789")
    return name, int(what[len(name):] or 0)


SEGS = [(0, RK), (RK, RK + NS), (RK + NS, RK + 2 * NS)]


def build(nc, a, out):
    ctx = ExitStack()
    with ctx:
        def sb(name, shape, dt=F32):
            return ctx.enter_context(nc.sbuf_tensor(name, shape, dt))

        def sem(name):
            return ctx.enter_context(nc.semaphore(name))

        PS = ctx.enter_context(nc.psum_tensor("PS", [P, 8, 512], F32))
        TR = (0, 1)
        MMB = (2, 3)
        GUB = (4, 5)
        YAB = (6, 7)

        cst = sb("cst", [P, NCST])
        wp = sb("wp", [P, NWP])
        lw = sb("lw", [RK, NLW])
        boutb = sb("boutb", [P, W])
        rmsb = sb("rmsb", [P, 64])
        XR = sb("XR", [P, TOK // P, W])
        HT = sb("HT", [P, 2, KT, CH])
        XF = sb("XF", [P, KT, CH])
        LR = sb("LR", [P, TB, W])
        LP = sb("LP", [P, TB, W])
        weff = sb("weff", [P, 4, W])
        diagD = sb("diagD", [P, CT, P])
        ring = sb("ring", [P, SLOTS, 2048])
        DT = sb("DT", [P, 2, CT, CH])
        DTX = sb("DTX", [P, 2, CT, CH])
        XI = sb("XI", [P, CT, CH + 4])
        XC = sb("XC", [P, CT, CH])
        TH = sb("TH", [P, 2, CH])
        Y = sb("Y", [P, 2, TB, DIN])
        BB = sb("BB", [P, 2, 2, CH])
        DA = sb("DA", [P, DRING, HCT, CH])
        DBX = sb("DBX", [P, BRING, HCT, CH])
        H = sb("H", [P, 2, HCT, CH])
        HC = sb("HC", [P, UNITS, HCT])
        G = sb("G", [P, 2, W])
        GT = sb("GT", [P, 2, CH])
        HJ = sb("HJ", [P, 2, CH])
        SP = sb("SP", [P, TB, 64])
        SPN = sb("SPN", [P, 2, TB, 64])
        DR = sb("DR", [48, CH])
        HN = sb("HN", [P, SEQ])
        BS = sb("BS", [P, 8, TB, 6])
        MV = sb("MV", [P, 8, TB, 2])
        VE = sb("VE", [P, 8, TB])
        RS = sb("RS", [P, 8, TB])
        MS = sb("MS", [P, 3, TB])
        MSR = sb("MSR", [P, 3, TB])
        half = sb("half", [P, 8])
        NA = sb("NA", [P, P])
        scb = sb("scb", [P, 12 * NJ])
        cv = sb("cv", [P, CT, 3])

        XN0 = DTX[:, :, :, :].rearrange("p a c t -> p (a c t)").rearrange("p (n w) -> p n w", w=W)
        XT0 = DT[:, :, :, :].rearrange("p b (k e) t -> p b k (e t)", k=KT)
        COS = Y[:, 0, :, :].rearrange("p a (b t) -> p (a b) t", t=SEQ)
        SIN = Y[:, 1, :, :].rearrange("p a (b t) -> p (a b) t", t=SEQ)
        wk = DA[:, :, :, :].rearrange("p a c t -> p (a c t)").rearrange("p (n t) -> p n t", t=SEQ)
        wk2 = DBX[:, :, :, :].rearrange("p a c t -> p (a c t)").rearrange("p (n t) -> p n t", t=SEQ)
        hid = XC[:, :, :].rearrange("p c t -> p (c t)").rearrange("p (n t) -> p n t", t=SEQ)
        hth = H[:, :, :, :].rearrange("p a c t -> p (a c t)").rearrange("p (n t) -> p n t", t=SEQ)
        Hs, SQ, RSTD, Z, S, MR, MI = (wk[:, i, :] for i in range(7))
        T0 = wk[:, 7, :]
        UR, VI, HB = (wk2[:, i, :] for i in range(3))
        xi4 = XI[:, :, :].rearrange("p c t -> p (c t)")
        codes = LR[:, :, :].rearrange("p a t -> p (a t)").bitcast(I32).rearrange("p (h o) -> p h o", h=2)
        fieldf = LP[:, :, :].rearrange("p a t -> p (a t)").rearrange("p (h o) -> p h o", h=2)
        packed = XF[:, :, :].rearrange("p k t -> p (k t)").bitcast(I32).rearrange("p (h o) -> p h o", h=2)
        bsc = HT[:, 1, :, :].rearrange("p k t -> p (k t)").rearrange("p (h o) -> p h o", h=2)
        dtmp = wk2[:, 3:5, :]
        gsb = sb("gsb", [P, 1])
        FR = sb("FR", [P, DEPTH, FINE + 1])
        FI = sb("FI", [P, DEPTH, FINE + 1])
        CR = sb("CR", [P, DEPTH, COARSE + 1])
        CI = sb("CI", [P, DEPTH, COARSE + 1])
        gate_last = xi4[:, 0:2048].rearrange("p (i w) -> p i w", i=4)
        tt4 = [xi4[:, i * 512:(i + 1) * 512] for i in range(4)]
        pz = sb("pz", [P, 16, DEPTH])
        b1n = sb("b1n", [P, 8])

        def C(name, i=None):
            lo, hi = CST[name]
            return cst[:, lo:hi] if i is None else cst[:, lo + i:lo + i + 1]

        ident, cen_m, avg_m = C("ident"), C("cen"), C("avg")
        w1_at = BB[:, :, :, :].rearrange("p a b t -> p (a b t)")
        w2_at = G[:, 0, :]
        win_at = G[:, 1, 0:KT * DIM]
        winT = win_at.rearrange("p (k d) -> p k d", k=KT)
        w1T = w1_at.rearrange("p (l f) -> p l f", l=DEPTH)
        w2T = w2_at.rearrange("p (l f d) -> p l f d", l=DEPTH, f=2)
        woutT = wp[:, WP["wout"][0]:WP["wout"][1]]
        xpT = wp[:, WP["xp"][0]:WP["xp"][1]].rearrange("p (c e) -> p c e", c=CT)
        la_at = GT[0:16, :, :].rearrange("r a t -> r (a t)")
        loraA = la_at.rearrange("r (k i) -> r k i", k=4)
        loraB = HJ[0:16, :, :].rearrange("r a t -> r (a t)")
        dpT = lw[0:RK, :]
        convw = C("conv_w").rearrange("p (c k) -> p c k", c=CT)

        wsc = nc.dram_tensor("w_scaled", (NJ, P, 1536), F32, kind="Internal").ap()
        b_rows = nc.dram_tensor("b_rows", (NCHUNK, NS, CH), F32, kind="Internal").ap()

        names = """cst_in x_in0 x_in1 x_in2 x_in3 w_in deq_in misc_in
            pw0 pw1 pw2 scaled st0 st1 st2
            unit tables table_in bias_set
            ln0_stats ln0_rstd xn0 xn0_turned xt0_copied h_in powers
            h_new0 centred0 squared0 variance0 rstd0 normed0 exped0 clamped0 sigmoid0 hidden_sum0 hidden0 ffn_sum0 hn0
            h_new1 centred1 squared1 variance1 rstd1 normed1 exped1 clamped1 sigmoid1 hidden_sum1 hidden1 ffn_sum1 hn1
            lora_prod weff_ready diag_ready na_exp
            ld0 ld1 ld2 free0 free1 free2
            attn_out a_read r1_stats r1_rstd xn turned_xn xt
            ffn0_prod ffn0_copied r3_stats r3_rstd x2n turned_x2 ht r2_stats r2_rstd r4_stats r4_rstd
            in_prod in_copied carry tail_kept conv conv_tanh xc
            xp_prod sp_part sp ms ms_rstd spn turned_bc dr b_stored
            dt_prod dt_split dt_log dt_ready dtx
            skip_prod skip_copied
            bb0 bb1 dbx decay states state_kept turned_h y_sum
            z_prod z_tanh z_read gated turned_y yt out_prod out_copied
            p5_stats p5_rstd p6_stats p6_rstd x3n turned_x3 xf gu_prod gate_tanh hj y_copied
            p7_stats p7_rstd result stored_out
            dve_step act_step pool_step""".split()
        s = {n: sem(n) for n in names}

        readers = [("xt0_copied", i + 1) for i in range(8)]
        readers += [("weff_ready", i + 1) for i in range(4)]
        for k in ROUNDS:
            for n in range(UNITS):
                for what, c in pieces(k, n):
                    name, i = parts(what)
                    if what == "attn_out":
                        readers += [("a_read", TB * c + tb + 1) for tb in range(TB)]
                    elif name == "z":
                        readers.append(("z_read", 4 * c + i + 1))
                    elif what == "turn_xn":
                        readers += [("xt", TB * c + tb + 1) for tb in range(TB)]
                    elif name == "turn_y":
                        readers += [("yt", 4 * c + 2 * i + h + 1) for h in range(2)]
                    elif name == "ffn":
                        readers.append(("ffn0_copied", TB * c + i + 1))
                    elif name == "out" and i < TB:
                        readers.append(("out_copied", TB * c + i + 1))
                    elif what == "turn_x2":
                        readers += [("ht", TB * c + tb + 1) for tb in range(TB)]
                    elif what == "turn_x3":
                        readers += [("xf", TB * c + tb + 1) for tb in range(TB)]
                    elif name == "in":
                        readers.append(("in_copied", 4 * c + i + 1))
                    elif what == "x_proj0":
                        readers.append(("sp", c + 1))
                    elif what == "turn_bc":
                        readers.append(("dr", c + 1))
                    elif what in ("dt0", "dt1"):
                        readers += [("dt_split", 4 * c + 2 * i + m + 1) for m in range(2)]
                    elif name == "skip":
                        readers += [("skip_copied", 4 * c + 2 * i + m + 1) for m in range(2)]
        mm_index = {r: i for i, r in enumerate(readers)}

        def bank(name, value):
            return PS[:, MMB[mm_index[(name, value)] % 2], :]

        stream, last_use = [], {}
        for k in ROUNDS:
            for n in range(UNITS):
                for what, c in pieces(k, n):
                    name, i = parts(what)
                    uses = {"z": [("ip", c, 2 + i // 2)], "in": [("ip", c, i // 2)], "g": [("w", c, i)],
                            "w": [("w", c, i)], "out": [("op", c, i // 2)]
                            }.get(name, [])
                    for it in uses:
                        if it not in last_use:
                            stream.append(it)
                        last_use[it] = (k, n)
        item = {it: q for q, it in enumerate(stream)}

        def loaded(kind, c, i):
            q = item[(kind, c, i)]
            return q % SLOTS, s[f"ld{q % SLOTS}"], 16 * (q // SLOTS + 1)

        def freed(kind, c, i):
            q = item[(kind, c, i)]
            return s[f"free{q % SLOTS}"], q // SLOTS + 1

        def sp_part(c, h):
            return bank("sp", c + 1)[:, 128 * h:128 * (h + 1)].rearrange("p (b e) -> p b e", b=TB)

        def gate_of(c, i):
            return gate_last[:, i, :] if c == NCHUNK - 1 else G[:, i % 2, :]

        def turned_in(g):
            k, u = g // UNITS, g % UNITS
            idle = UNITS if k == 0 else int(FIRST_G * (PACE if k == NCHUNK - 1 else 1)) - 1
            return GUB if u % 2 and (0 if k == 0 else 3) <= u < idle else TR

        def turned_before(g):
            return next((f for f in range(g - 1, -1, -1) if turned_in(f) == turned_in(g)), None)

        def in_done(c, m):
            return freed("ip", c, m // 2) if m % 2 else (s["in_prod"], 2 * c + m // 2 + 1)

        def z_done(c, i):
            return freed("ip", c, 2 + i // 2) if i % 2 else (s["z_prod"], 2 * c + i // 2 + 1)

        def out_done(c, tb):
            return freed("op", c, 1) if tb else (s["out_prod"], c + 1)

        NB = [PS[:, h, 0:CH] for h in range(2)]
        VB = [PS[:, h, CH:2 * CH] for h in range(2)]
        HID = [PS[:, 4 + 2 * h:6 + 2 * h, :].rearrange("p b (f t) -> p b f t", f=2) for h in range(2)]

        def half_cols(h):
            return slice(h * CH, (h + 1) * CH)

        block = ctx.enter_context(nc.Block())

        @block.sync
        def _(sp):
            sp.dma_start(cst[:, :], a["cst"]).then_inc(s["cst_in"], 16)
            for h in range(2):
                for b in range(2):
                    n = 4 * b + 2 * h
                    sp.dma_start(XR[:, n:n + 2, :], a["x"].rearrange("(n p) v -> p n v", p=P)[:, n:n + 2, :]
                                 ).then_inc(s[f"x_in{2 * b + h}"], 16)
            for dst, n in ((w1_at, "w1"), (w2_at, "w2"), (win_at, "win"), (wp[:, :], "wp")):
                sp.dma_start(dst, a[n]).then_inc(s["w_in"], 16)
            sp.dma_start(packed, a["packed"].rearrange("h p o -> p h o")).then_inc(s["deq_in"], 16)
            for g in range(2):
                sp.dma_start(bsc[:, g, :], a["bs"][16 * g:16 * g + 16, None, :].to_broadcast((16, 8, W))
                             ).then_inc(s["deq_in"], 16)
            sp.dma_start(gsb[:, :], a["gs"][None, :].to_broadcast((P, 1))).then_inc(s["deq_in"], 16)
            for dst, n in ((lw[:, :], "lw"), (la_at, "la"), (loraB, "lb")):
                sp.dma_start(dst, a[n]).then_inc(s["deq_in"], 16)
            sp.dma_start(scb[:, :], a["sc"][None, :].to_broadcast((P, 12 * NJ))).then_inc(s["misc_in"], 16)
            sp.dma_start(boutb[:, :], a["bout"][None, :].to_broadcast((P, W))).then_inc(s["misc_in"], 16)
            sp.dma_start(rmsb[:, :], a["rms"][None, :].to_broadcast((P, 64))).then_inc(s["misc_in"], 16)
            for j in range(NJ + 1):
                if j < NJ:
                    if j >= SLOTS:
                        sp.wait_ge(s[f"st{j % SLOTS}"], 16 * (j // SLOTS))
                    sp.dma_start(ring[:, j % SLOTS, 0:1536], a["wq"][j]).then_inc(s[f"pw{j % SLOTS}"], 16)
                if j >= 1:
                    sp.wait_ge(s["scaled"], j)
                    sp.dma_start(wsc[j - 1], ring[:, (j - 1) % SLOTS, 0:1536]).then_inc(s[f"st{(j - 1) % SLOTS}"], 16)
            for i in range(SLOTS):
                sp.wait_ge(s[f"st{i}"], 16 * len(range(i, NJ, SLOTS)))

            def fetch(q):
                kind, c, i = stream[q]
                if q >= SLOTS:
                    sp.wait_ge(*freed(*stream[q - SLOTS]))
                dst = ring[:, q % SLOTS, :]
                src = {"ip": a["ip"], "op": a["op"], "w": wsc}[kind][i]
                if kind == "w":
                    dst = dst[:, 0:1536]
                sp.dma_start(dst, src).then_inc(s[f"ld{q % SLOTS}"], 16)

            def spread_b(g):
                c, m = g // (NS // 2), g % (NS // 2)
                if m == 0:
                    sp.wait_ge(s["b_stored"], 16 * (c + 1))
                if g >= 2:
                    sp.wait_ge(s["dbx"], 4 * (g - 1))
                sp.dma_start(BB[:, g % 2, :, :], b_rows[c, 2 * m:2 * m + 2, :][None, :, :].to_broadcast((P, 2, CH))
                             ).then_inc(s[f"bb{g % 2}"], 16)

            q = 0
            for _ in range(SLOTS):
                fetch(q)
                q += 1
            for k in ROUNDS:
                for u in range(UNITS):
                    pair = (UNITS * k + u) // 4 + 2
                    if u % 4 == 0 and 0 <= pair < NCHUNK * NS // 2:
                        spread_b(pair)
                    for what, c in pieces(k, u):
                        if what == "turn_bc":
                            sp.wait_ge(s["dr"], c + 1)
                            sp.dma_start(b_rows[c], DR[RK:RK + NS, :]).then_inc(s["b_stored"], 16)
                    while q < len(stream) and last_use[stream[q - SLOTS]] <= (k, u):
                        fetch(q)
                        q += 1
                    for what, c in pieces(k, u):
                        if what == "result":
                            sp.wait_ge(s["result"], TB * (c + 1))
                            sp.dma_start(out.rearrange("(n p) v -> p n v", p=P)[:, TB * c:TB * c + TB, :],
                                         XR[:, TB * c:TB * c + TB, :]).then_inc(s["stored_out"], 16)
            while q < len(stream):
                fetch(q)
                q += 1
            sp.wait_ge(s["stored_out"], 16 * NCHUNK)

        @block.tensor
        def _(pe):
            def turn(dst, src, srcs=4):
                for i in range(srcs):
                    last = pe.transpose(dst[:, i * P:(i + 1) * P], src(i), ident)
                return last

            def free(name, value):
                i = mm_index[(name, value)]
                if i >= 2:
                    pe.wait_ge(s[readers[i - 2][0]], readers[i - 2][1])

            pe.wait_ge(s["cst_in"], 16)
            for i in range(TOK // P):
                t = 2 * PAIRS0[i // 2] + i % 2
                pe.wait_ge(s["xn0"], i + 1)
                free("xt0_copied", i + 1)
                turn(bank("xt0_copied", i + 1), lambda e: XN0[:, t, e * P:(e + 1) * P]).then_inc(s["xn0_turned"], 1)
            pe.wait_ge(s["w_in"], 64)
            for h in range(2):
                pe.wait_ge(s["xt0_copied"], 4 * (h + 1))
                for b in range(2):
                    for kk in range(KT):
                        last = pe.matmul(NB[h][64 * b:64 * b + 64, :], winT[:, kk, :],
                                         XT0[:, b, kk, half_cols(h)], start=kk == 0, stop=kk == KT - 1)
                last.then_inc(s["h_in"], 1)
            def first_half(what, l, h):
                at = half_cols(h)
                if what in ("cen1", "cen2"):
                    i = 2 * l + (what == "cen2")
                    pe.wait_ge(s[f"h_new{h}"], i + 1)
                    pe.matmul(NB[h], cen_m, Hs[:, at], start=True, stop=True).then_inc(s[f"centred{h}"], 1)
                elif what in ("var1", "var2"):
                    i = 2 * l + (what == "var2")
                    pe.wait_ge(s[f"squared{h}"], i + 1)
                    pe.matmul(VB[h], avg_m, SQ[:, at], start=True, stop=True).then_inc(s[f"variance{h}"], 1)
                elif what == "hide":
                    pe.wait_ge(s[f"normed{h}"], 2 * l + 2)
                    for f in range(2):
                        for b in range(2):
                            last = pe.matmul(HID[h][:, b, f, :], w1T[64 * b:64 * b + 64, l, f * P:(f + 1) * P],
                                             Z[64 * b:64 * b + 64, at], start=True, stop=True)
                    last.then_inc(s[f"hidden_sum{h}"], 1)
                elif what == "ffn":
                    for b in range(2):
                        for f in range(2):
                            pe.wait_ge(s[f"hidden{h}"], 2 * l + f + 1)
                            last = pe.matmul(VB[h][64 * b:64 * b + 64, :], w2T[:, l, f, :], hid[:, 2 * b + f, at],
                                             start=f == 0, stop=f == 1)
                    last.then_inc(s[f"ffn_sum{h}"], 1)
                if (what, l, h) in LORA_AT:
                    i = LORA_AT.index((what, l, h))
                    pe.wait_ge(s["deq_in"], 16 * 7)
                    free("weff_ready", i + 1)
                    pe.matmul(bank("weff_ready", i + 1), loraA[:, i, :], loraB, start=True, stop=True
                              ).then_inc(s["lora_prod"], 1)

            for step0 in ORDER0:
                first_half(*step0)

            def scan_turn(g):
                pe.wait_ge(s["states"], g + 1)
                before = turned_before(g)
                if turned_in(g) == GUB and g >= 2 * UNITS:
                    pe.wait_ge(s["hj"], NJ * (g // UNITS - 1))
                for tb in range(TB):
                    if before is not None:
                        pe.wait_ge(s["y_sum"], 2 * before + tb + 1)
                    turn(PS[:, turned_in(g)[tb], :], lambda i: H[:, g % 2, i, tb * P:(tb + 1) * P]
                         ).then_inc(s["turned_h"], 1)

            for k in ROUNDS:
                for u in range(UNITS):
                    if 0 <= k < NCHUNK:
                        scan_turn(UNITS * k + u)
                    for what, c in pieces(k, u):
                        name, i = parts(what)
                        b = c // 2
                        if what in LAST0:
                            first_half(*LAST0[what])
                        if what == "attn_out":
                            pe.wait_ge(s[f"hn{c % 2}"], 1)
                            for tb in range(TB):
                                free("a_read", TB * c + tb + 1)
                                t0 = (c % 2) * CH + tb * P
                                pe.matmul(bank("a_read", TB * c + tb + 1), HN[64 * b:64 * b + 64, t0:t0 + P],
                                          woutT[64 * b:64 * b + 64, :], start=True, stop=True
                                          ).then_inc(s["attn_out"], 1)
                        elif what == "turn_xn":
                            for tb in range(TB):
                                pe.wait_ge(s["xn"], TB * c + tb + 1)
                                free("xt", TB * c + tb + 1)
                                turn(bank("xt", TB * c + tb + 1),
                                     lambda e: LR[:, tb, 256 * (e // 2) + e % 2:256 * (e // 2) + 256:2]
                                     ).then_inc(s["turned_xn"], 1)
                        elif name == "ffn":
                            pe.wait_ge(s["weff_ready"], 4)
                            pe.wait_ge(s["xt"], TB * c + i + 1)
                            free("ffn0_copied", TB * c + i + 1)
                            for e in range(4):
                                last = pe.matmul(bank("ffn0_copied", TB * c + i + 1),
                                                 HT[:, c % 2, e, i * P:(i + 1) * P], weff[:, e, :],
                                                 start=e == 0, stop=e == 3)
                            last.then_inc(s["ffn0_prod"], 1)
                        elif what == "turn_x2":
                            for tb in range(TB):
                                pe.wait_ge(s["x2n"], TB * c + tb + 1)
                                free("ht", TB * c + tb + 1)
                                turn(bank("ht", TB * c + tb + 1), lambda e: LR[:, tb, e * P:(e + 1) * P]
                                     ).then_inc(s["turned_x2"], 1)
                        elif name == "in":
                            slot, ld, v = loaded("ip", c, i // 2)
                            if i % 2 == 0:
                                pe.wait_ge(ld, v)
                                pe.wait_ge(s["ht"], TB * (c + 1))
                            wi = ring[:, slot, :].rearrange("p (k n) -> p k n", k=KT)
                            free("in_copied", 4 * c + i + 1)
                            dst = bank("in_copied", 4 * c + i + 1)
                            for e in range(2):
                                o = ((2 * i + e) % HCT) * P
                                for kk in range(KT):
                                    last = pe.matmul(dst[:, e * CH:(e + 1) * CH], wi[:, kk, o:o + P],
                                                     HT[:, c % 2, kk, :], start=kk == 0, stop=kk == KT - 1)
                            last.then_inc(in_done(c, i)[0], 1)
                        elif name == "x_proj":
                            pe.wait_ge(s["xc"], 4 * c + 2 * (i + 1))
                            if i == 0:
                                free("sp", c + 1)
                            dst = bank("sp", c + 1)
                            for tb in range(TB):
                                for e in range(HCT * i, HCT * (i + 1)):
                                    o = 64 * (TB * i + tb)
                                    last = pe.matmul(dst[:, o:o + 64], XC[:, e, tb * P:(tb + 1) * P],
                                                     xpT[:, e, :], start=e % HCT == 0, stop=e % HCT == HCT - 1)
                            if i == 1:
                                last.then_inc(s["xp_prod"], 1)
                        elif what == "turn_bc":
                            pe.wait_ge(s["spn"], 6 * (c + 1))
                            free("dr", c + 1)
                            dst = bank("dr", c + 1)
                            for tb in range(TB):
                                last = pe.transpose(dst[0:48, tb * P:(tb + 1) * P], SPN[:, c % 2, tb, 0:48], ident)
                            last.then_inc(s["turned_bc"], 1)
                        elif what in ("dt0", "dt1"):
                            pe.wait_ge(s["dr"], c + 1)
                            for m in (2 * i, 2 * i + 1):
                                free("dt_split", 4 * c + m + 1)
                                dst = bank("dt_split", 4 * c + m + 1)
                                for e in range(2):
                                    o = (2 * m + e) * P
                                    last = pe.matmul(dst[:, e * CH:(e + 1) * CH], dpT[:, o:o + P], DR[0:RK, :],
                                                     start=True, stop=True)
                                last.then_inc(s["dt_prod"], 1)
                        elif name == "skip":
                            pe.wait_ge(s["diag_ready"], 1)
                            for h in range(2):
                                r = 4 * c + 2 * i + h + 1
                                free("skip_copied", r)
                                for e in range(HCT):
                                    last = pe.matmul(bank("skip_copied", r)[:, e * P:(e + 1) * P],
                                                     XC[:, HCT * h + e, i * P:(i + 1) * P],
                                                     diagD[:, HCT * h + e, :], start=True, stop=True)
                                last.then_inc(s["skip_prod"], 1)
                        elif name == "z":
                            h, tb = i // 2, i % 2
                            slot, ld, v = loaded("ip", c, 2 + h)
                            pe.wait_ge(ld, v)
                            wi = ring[:, slot, :].rearrange("p (k n) -> p k n", k=KT)
                            free("z_read", 4 * c + i + 1)
                            for kk in range(KT):
                                last = pe.matmul(bank("z_read", 4 * c + i + 1), HT[:, c % 2, kk, tb * P:(tb + 1) * P],
                                                 wi[:, kk, :], start=kk == 0, stop=kk == KT - 1)
                            last.then_inc(z_done(c, i)[0], 1)
                        elif name == "turn_y":
                            for h in range(2):
                                r = 4 * c + 2 * i + h + 1
                                pe.wait_ge(s["gated"], 4 * c + 2 * h + i + 1)
                                free("yt", r)
                                turn(bank("yt", r), lambda e: Y[:, c % 2, i, h * 512 + e * P:h * 512 + (e + 1) * P]
                                     ).then_inc(s["turned_y"], 1)
                        elif name == "out":
                            h, tb = i // 2, i % 2
                            if h == 0:
                                free("out_copied", TB * c + tb + 1)
                            slot, ld, v = loaded("op", c, h)
                            pe.wait_ge(ld, v)
                            pe.wait_ge(s["yt"], 4 * c + 2 * tb + h + 1)
                            wo = ring[:, slot, :].rearrange("p (k n) -> p k n", k=HCT)
                            for e in range(HCT):
                                last = pe.matmul(bank("out_copied", TB * c + tb + 1),
                                                 XC[:, HCT * h + e, tb * P:(tb + 1) * P], wo[:, e, :],
                                                 start=h == 0 and e == 0, stop=h == 1 and e == HCT - 1)
                            if tb == 1:
                                last.then_inc(freed("op", c, h)[0], 1)
                            elif h == 1:
                                last.then_inc(s["out_prod"], 1)
                        elif what == "turn_x3":
                            for tb in range(TB):
                                pe.wait_ge(s["x3n"], TB * c + tb + 1)
                                free("xf", TB * c + tb + 1)
                                turn(bank("xf", TB * c + tb + 1), lambda e: LP[:, tb, e * P:(e + 1) * P]
                                     ).then_inc(s["turned_x3"], 1)
                        elif name == "g":
                            slot, ld, v = loaded("w", c, i)
                            pe.wait_ge(ld, v)
                            pe.wait_ge(s["xf"], TB * (c + 1))
                            g = NJ * c + i
                            if g >= 2:
                                pe.wait_ge(s["hj"], g - 1)
                            if i < 2 and c < NCHUNK - 1:
                                last = max(f for f in range(UNITS * (c + 2)) if turned_in(f) == GUB)
                                pe.wait_ge(s["y_sum"], 2 * (last + 1))
                            for e in range(2):
                                for kk in range(KT):
                                    last = pe.matmul(PS[:, GUB[g % 2], e * CH:(e + 1) * CH],
                                                     ring[:, slot, (e * KT + kk) * P:(e * KT + kk + 1) * P],
                                                     XF[:, kk, :], start=kk == 0, stop=kk == KT - 1)
                            last.then_inc(s["gu_prod"], 1)
                        elif name == "w":
                            slot, _, _ = loaded("w", c, i)
                            g = NJ * c + i
                            pe.wait_ge(s["hj"], g + 1)
                            if i == 0 and c >= 1:
                                pe.wait_ge(s["y_copied"], TB * c)
                            for tb in range(TB):
                                last = pe.matmul(PS[:, YAB[tb], :], HJ[:, g % 2, tb * P:(tb + 1) * P],
                                                 ring[:, slot, 1024:1536], start=i == 0, stop=i == NJ - 1)
                            last.then_inc(freed("w", c, i)[0], 1)

        @block.scalar
        def _(act):
            step = [0]

            def link(ins):
                step[0] += 1
                ins.then_inc(s["act_step"], 1)
                act.wait_ge(s["act_step"], step[0])

            act.add_instruction(mybir.InstLoadActFuncSet(
                name=nc.get_next_instruction_name(), act_func_set_id=6, ins=[], outs=[],
                engine=mybir.EngineType.Activation))
            act.wait_ge(s["cst_in"], 16)
            link(act.activation(NA[:, :], C("A_log"), ACT.Exp))
            act.mul(NA[:, :], NA[:, :], -1.0).then_inc(s["na_exp"], 1)
            act.wait_ge(s["unit"], 1)
            link(act.activation(pz[:, 1, :], pz[:, 0, :], ACT.Ln))
            act.activation(pz[:, 1, :], pz[:, 1, :], ACT.Exp, scale=-0.5).then_inc(s["table_in"], 1)
            act.wait_ge(s["unit"], 2)
            act.activation(pz[:, 8, :], pz[:, 7, :], ACT.Exp, scale=-2.0).then_inc(s["table_in"], 1)
            for i in range(TOK // P):
                t = 2 * PAIRS0[i // 2] + i % 2
                act.wait_ge(s["xn0_turned"], i + 1)
                act.activation(XT0[:, t // 4, :, (t % 4) * P:(t % 4 + 1) * P],
                               bank("xt0_copied", i + 1).rearrange("p (k t) -> p k t", k=KT), ACT.Copy
                               ).then_inc(s["xt0_copied"], 1)
            def first_half(what, l, h):
                at = half_cols(h)
                if what in ("cen1", "cen2"):
                    act.wait_ge(s[f"centred{h}"], 2 * l + (what == "cen2") + 1)
                    act.activation(SQ[:, at], NB[h], ACT.Square).then_inc(s[f"squared{h}"], 1)
                elif what in ("var1", "var2"):
                    act.wait_ge(s[f"variance{h}"], 2 * l + (what == "var2") + 1)
                    link(act.activation(RSTD[:, at], VB[h], ACT.Ln, bias=C("eps")))
                    act.activation(RSTD[:, at], RSTD[:, at], ACT.Exp, scale=-0.5).then_inc(s[f"rstd{h}"], 1)
                elif what == "sig1":
                    act.wait_ge(s[f"normed{h}"], 2 * l + 1)
                    act.activation(T0[:, at], Z[:, at], ACT.Exp, scale=-1.0).then_inc(s[f"exped{h}"], 1)
                    act.wait_ge(s[f"clamped{h}"], 3 * l + 1)
                    link(act.activation(T0[:, at], T0[:, at], ACT.Ln, bias=1.0))
                    act.activation(T0[:, at], T0[:, at], ACT.Exp, scale=-1.0).then_inc(s[f"sigmoid{h}"], 1)
                elif what == "hide":
                    act.wait_ge(s[f"hidden_sum{h}"], l + 1)
                    if l == 0:
                        act.wait_ge(s["bias_set"], 1)
                    for f in range(2):
                        act.activation(hth[:, f::2, at], HID[h][:, :, f, :], ACT.Exp, scale=-1.0,
                                       bias=b1n[:, 2 * l + f:2 * l + f + 1]).then_inc(s[f"exped{h}"], 1)
                elif what == "act":
                    for f in range(2):
                        act.wait_ge(s[f"clamped{h}"], 3 * l + 2 + f)
                        link(act.activation(hth[:, f::2, at], hth[:, f::2, at], ACT.Ln, bias=1.0))
                        act.activation(hth[:, f::2, at], hth[:, f::2, at], ACT.Exp, scale=-1.0
                                       ).then_inc(s[f"sigmoid{h}"], 1)

            for step0 in ORDER0:
                first_half(*step0)

            def decays(g):
                k, u = g // UNITS, g % UNITS
                n, h = u // 2, u % 2
                if u < 2:
                    act.wait_ge(s["dt_ready"], 2 * k + u + 1)
                if u == 0:
                    if k == 0:
                        act.wait_ge(s["na_exp"], 1)
                if g >= DRING:
                    act.wait_ge(s["states"], g - DRING + 1)
                for i in range(HCT):
                    ct = HCT * h + i
                    last = act.activation(DA[:, g % DRING, i, :], DT[:, k % 2, ct, :], ACT.Exp,
                                          scale=NA[:, ct * NS + n:ct * NS + n + 1])
                last.then_inc(s["decay"], 1)

            for k in ROUNDS:
                for u in range(UNITS):
                    if 0 <= UNITS * k + u + 2 < NCHUNK * UNITS:
                        decays(UNITS * k + u + 2)
                    for what, c in pieces(k, u):
                        name, i = parts(what)
                        if what in LAST0:
                            first_half(*LAST0[what])
                        elif what == "turn_xn":
                            for tb in range(TB):
                                act.wait_ge(s["turned_xn"], TB * c + tb + 1)
                                if c >= 2 and tb == 0:
                                    act.wait_ge(*z_done(c - 2, 3))
                                if c == 1 and tb == 0:
                                    act.wait_ge(s["weff_ready"], 4)
                                act.activation(HT[:, c % 2, :, tb * P:(tb + 1) * P],
                                               bank("xt", TB * c + tb + 1).rearrange("p (k t) -> p k t", k=KT),
                                               ACT.Copy).then_inc(s["xt"], 1)
                        elif name == "ffn":
                            act.wait_ge(s["ffn0_prod"], TB * c + i + 1)
                            act.activation(LR[:, i, :], bank("ffn0_copied", TB * c + i + 1), ACT.Copy
                                           ).then_inc(s["ffn0_copied"], 1)
                        elif what == "turn_x2":
                            for tb in range(TB):
                                act.wait_ge(s["turned_x2"], TB * c + tb + 1)
                                act.wait_ge(s["ffn0_prod"], TB * (c + 1))
                                act.activation(HT[:, c % 2, :, tb * P:(tb + 1) * P],
                                               bank("ht", TB * c + tb + 1).rearrange("p (k t) -> p k t", k=KT),
                                               ACT.Copy).then_inc(s["ht"], 1)
                        elif name == "in":
                            act.wait_ge(*in_done(c, i))
                            if i == 0:
                                act.wait_ge(s["carry"], c + 1)
                            act.activation(XI[:, 2 * i:2 * i + 2, 3:3 + CH],
                                           bank("in_copied", 4 * c + i + 1).rearrange("p (e t) -> p e t", e=2),
                                           ACT.Copy).then_inc(s["in_copied"], 1)
                        elif name == "conv":
                            act.wait_ge(s["conv"], 4 * c + i + 1)
                            act.activation(TH[:, :, :], XC[:, 2 * i:2 * i + 2, :], ACT.Tanh, scale=0.5
                                           ).then_inc(s["conv_tanh"], 1)
                        elif what == "x_proj1":
                            act.wait_ge(s["xp_prod"], c + 1)
                            if c:
                                act.wait_ge(s["spn"], 6 * c)
                            act.activation(SP[:, :, :], sp_part(c, 0), ACT.Copy).then_inc(s["sp_part"], 1)
                        elif what == "turn_bc":
                            act.wait_ge(s["turned_bc"], c + 1)
                            if c:
                                act.wait_ge(s["b_stored"], 16 * c)
                                act.wait_ge(s["dt_prod"], 4 * c)
                            act.activation(DR[:, :], bank("dr", c + 1)[0:48, 0:CH], ACT.Copy).then_inc(s["dr"], 1)
                        elif what in ("dt0", "dt1"):
                            if i == 0:
                                if c >= 2:
                                    act.wait_ge(s["states"], UNITS * (c - 1))
                                act.wait_ge(s["tail_kept"], c + 1)
                            for m in (2 * i, 2 * i + 1):
                                act.wait_ge(s["dt_prod"], 4 * c + m + 1)
                                src = bank("dt_split", 4 * c + m + 1)
                                for e in range(2):
                                    ct = 2 * m + e
                                    act.activation(XI[:, ct, 3:3 + CH], src[:, e * CH:(e + 1) * CH], ACT.Abs,
                                                   bias=C("dt_bias", ct))
                                    last = act.activation(DT[:, c % 2, ct, :], src[:, e * CH:(e + 1) * CH],
                                                          ACT.Relu, bias=C("dt_bias", ct))
                                last.then_inc(s["dt_split"], 1)
                        elif name == "log":
                            xi = XI[:, HCT * i:HCT * (i + 1), 3:3 + CH]
                            act.wait_ge(s["dt_split"], 4 * c + 2 * (i + 1))
                            link(act.activation(xi, xi, ACT.Exp, scale=-1.0))
                            act.activation(xi, xi, ACT.Ln, bias=1.0).then_inc(s["dt_log"], 1)
                        elif name == "skip":
                            for h in range(2):
                                r = 4 * c + 2 * i + h + 1
                                act.wait_ge(s["skip_prod"], r)
                                if r == 4 * c + 1 and c >= 2:
                                    act.wait_ge(s["turned_y"], 4 * (c - 1))
                                act.activation(Y[:, c % 2, i, h * 512:h * 512 + 512], bank("skip_copied", r), ACT.Copy
                                               ).then_inc(s["skip_copied"], 1)
                        elif name == "z":
                            r = 4 * c + i + 1
                            act.wait_ge(*z_done(c, i))
                            if c == NCHUNK - 1:
                                act.wait_ge(s["dt_ready"], 2 * (c + 1))
                            elif i < 2 and c >= 1:
                                act.wait_ge(s["gated"], r - 2)
                                if c >= 2:
                                    act.wait_ge(s["result"], TB * (c - 1))
                            elif r > 2:
                                act.wait_ge(s["gated"], r - 2)
                            act.activation(gate_of(c, i), bank("z_read", r), ACT.Tanh, scale=0.5
                                           ).then_inc(s["z_tanh"], 1)
                        elif name == "turn_y":
                            for h in range(2):
                                r = 4 * c + 2 * i + h + 1
                                act.wait_ge(s["turned_y"], r)
                                if r == 4 * c + 1:
                                    d = min(c + 1, NCHUNK - 1)
                                    act.wait_ge(s["skip_prod"], 4 * (d + 1))
                                    act.wait_ge(s["dtx"], 2 * (d + 1))
                                act.activation(XC[:, HCT * h:HCT * h + HCT, i * P:(i + 1) * P],
                                               bank("yt", r).rearrange("p (k t) -> p k t", k=HCT),
                                               ACT.Copy).then_inc(s["yt"], 1)
                        elif name == "out" and i >= TB:
                            tb = i - TB
                            act.wait_ge(*out_done(c, tb))
                            if c and tb == 0:
                                act.wait_ge(s["turned_x3"], TB * c)
                            if c == 0 and tb == 0:
                                act.wait_ge(s["weff_ready"], 4)
                            act.activation(LP[:, tb, :], bank("out_copied", TB * c + tb + 1), ACT.Copy
                                           ).then_inc(s["out_copied"], 1)
                        elif what == "turn_x3":
                            for tb in range(TB):
                                act.wait_ge(s["turned_x3"], TB * c + tb + 1)
                                if c and tb == 0:
                                    act.wait_ge(s["gu_prod"], NJ * c)
                                act.activation(XF[:, :, tb * P:(tb + 1) * P],
                                               bank("xf", TB * c + tb + 1).rearrange("p (k t) -> p k t", k=KT),
                                               ACT.Copy).then_inc(s["xf"], 1)
                        elif name == "g":
                            g = NJ * c + i
                            act.wait_ge(s["gu_prod"], g + 1)
                            if g >= 2:
                                act.wait_ge(s["hj"], g - 1)
                            act.activation(GT[:, g % 2, :], PS[:, GUB[g % 2], 0:CH], ACT.Tanh, scale=0.5
                                           ).then_inc(s["gate_tanh"], 1)
                        elif what == "y_done":
                            act.wait_ge(*freed("w", c, NJ - 1))
                            act.wait_ge(s["gated"], 4 * min(c + 2, NCHUNK - 1))
                            if c == NCHUNK - 1:
                                act.wait_ge(s["result"], TB * c)
                            for tb in range(TB):
                                act.activation(G[:, tb, :], PS[:, YAB[tb], :], ACT.Copy).then_inc(s["y_copied"], 1)

        @block.gpsimd
        def _(pool):
            step = [0]

            def link(ins):
                step[0] += 1
                ins.then_inc(s["pool_step"], 1)
                pool.wait_ge(s["pool_step"], step[0])

            link(pool.memset(half[:, :], -0.5))
            pool.memset(cv[:, :, :], 0.0)
            link(pool.memset(HC[:, :, :], 0.0))
            pool.wait_ge(s["cst_in"], 16)

            def rstd(st, v, dst, src, n, done):
                pool.wait_ge(s[st], v)
                pool.tensor_tensor(dst, src, half[:, 0:n], ALU.pow).then_inc(s[done], 1)

            for i, j in enumerate(PAIRS0):
                rstd("ln0_stats", i + 1, RS[:, j, :], VE[:, j, :], TB, "ln0_rstd")

            pool.wait_ge(s["powers"], 1)
            for l in range(DEPTH):
                shape = (P, COARSE, FINE)
                cr = CR[:, l, 0:COARSE][:, :, None].to_broadcast(shape)
                ci = CI[:, l, 0:COARSE][:, :, None].to_broadcast(shape)
                fr = FR[:, l, 0:FINE][:, None, :].to_broadcast(shape)
                fi = FI[:, l, 0:FINE][:, None, :].to_broadcast(shape)
                cos_l, sin_l, t_cos, t_sin = (t.rearrange("p (a b) -> p a b", a=COARSE)
                                              for t in (COS[:, l, :], SIN[:, l, :], tt4[0], tt4[1]))
                pool.tensor_tensor(cos_l, cr, fr, ALU.mult)
                pool.tensor_tensor(sin_l, cr, fi, ALU.mult)
                pool.tensor_tensor(t_cos, ci, fi, ALU.mult)
                link(pool.tensor_tensor(t_sin, ci, fr, ALU.mult))
                pool.tensor_tensor(cos_l, cos_l, t_cos, ALU.subtract)
                pool.tensor_tensor(sin_l, sin_l, t_sin, ALU.add).then_inc(s["tables"], 1)
                pool.wait_ge(s["tables"], l + 1)
            for ct in range(CT):
                last = pool.tensor_scalar(diagD[:, ct, :], ident, C("D", ct), None, ALU.mult)
            last.then_inc(s["diag_ready"], 1)
            pool.wait_ge(s["misc_in"], 48)
            for j in range(NJ):
                pool.wait_ge(s[f"pw{j % SLOTS}"], 16 * (j // SLOTS + 1))
                w = ring[:, j % SLOTS, 0:1536].rearrange("p (q m) -> p q m", q=12)
                pool.tensor_tensor(w, w, scb[:, 12 * j:12 * j + 12][:, :, None].to_broadcast((P, 12, P)), ALU.mult
                                   ).then_inc(s["scaled"], 1)

            def inputs(g):
                k, u = g // UNITS, g % UNITS
                n, h = u // 2, u % 2
                pair = 8 * k + n // 2
                if u < 2:
                    pool.wait_ge(s["dtx"], 2 * k + u + 1)
                if u % 4 == 0:
                    pool.wait_ge(s[f"bb{pair % 2}"], 16 * (pair // 2 + 1))
                if g >= BRING:
                    pool.wait_ge(s["states"], g - BRING + 1)
                pool.tensor_tensor(DBX[:, g % BRING, :, :], DTX[:, k % 2, HCT * h:HCT * h + HCT, :],
                                   BB[:, pair % 2, n % 2, :][:, None, :].to_broadcast((P, HCT, CH)), ALU.mult
                                   ).then_inc(s["dbx"], 1)

            def keep(g):
                pool.wait_ge(s["states"], g + 1)
                pool.tensor_copy(HC[:, g % UNITS, :], H[:, g % 2, :, CH - 1]).then_inc(s["state_kept"], 1)

            for k in ROUNDS:
                for u in range(UNITS):
                    if 0 <= UNITS * k + u + 2 < NCHUNK * UNITS:
                        inputs(UNITS * k + u + 2)
                    if 0 <= k < NCHUNK:
                        keep(UNITS * k + u)
                    for what, c in pieces(k, u):
                        if what in RSTD_OF:
                            kind, i = RSTD_OF[what]
                            rstd(kind + "_stats", c + 1, RS[:, i, :], VE[:, i, :], TB, kind + "_rstd")
                        elif what == "in0":
                            if c:
                                pool.wait_ge(s["dt_ready"], 2 * c)
                            pool.tensor_scalar(XI[:, :, 0:3], cv[:, :, :], 0.0 if c % 2 == 0 else 1.0, None, ALU.mult
                                               ).then_inc(s["carry"], 1)
                        elif what == "x_proj1":
                            pool.wait_ge(s["conv"], 4 * (c + 1))
                            pool.tensor_copy(cv[:, :, :], XI[:, :, CH:CH + 3]).then_inc(s["tail_kept"], 1)
                        elif what == "ms":
                            rstd("ms", c + 1, MSR[:, :, :].rearrange("p a b -> p (a b)"),
                                 MS[:, :, :].rearrange("p a b -> p (a b)"), 3 * TB, "ms_rstd")

        @block.vector
        def _(dve):
            step = [0]

            def mark(ins):
                step[0] += 1
                ins.then_inc(s["dve_step"], 1)

            def settle():
                dve.wait_ge(s["dve_step"], step[0])

            def link(ins):
                mark(ins)
                settle()

            def tt(o, x, y, op):
                return dve.tensor_tensor(o, x, y, op)

            def ts(o, x, s1, s2, op0, op1=None):
                return dve.tensor_scalar(o, x, s1, s2, op0) if op1 is None else dve.tensor_scalar(o, x, s1, s2, op0, op1)

            def stt(o, x, sc, y, op0, op1):
                return dve.scalar_tensor_tensor(o, x, sc, y, op0, op1)

            def stats(src, i, eps, done):
                for tb in range(TB):
                    mark(dve.bn_stats(BS[:, i, tb, :], src(tb)))
                settle()
                for tb in range(TB):
                    mark(dve.bn_aggr(MV[:, i, tb, :], BS[:, i, tb, :]))
                settle()
                ts(VE[:, i, :], MV[:, i, :, 1], eps, None, ALU.add).then_inc(s[done], 1)

            def normalise(dst, src, i, tb):
                return ts(dst, src, MV[:, i, tb, 0:1], RS[:, i, tb:tb + 1], ALU.subtract, ALU.mult)

            dve.wait_ge(s["cst_in"], 16)
            re, im = C("phz_re"), C("phz_im")
            mark(tt(pz[:, 2, :], re, re, ALU.mult))
            mark(tt(pz[:, 3, :], im, im, ALU.mult))
            settle()
            link(tt(pz[:, 4, :], pz[:, 2, :], pz[:, 3, :], ALU.add))
            ts(pz[:, 0, :], pz[:, 4, :], 1e-19, None, ALU.max).then_inc(s["unit"], 1)
            mark(ts(pz[:, 5, :], pz[:, 4, :], 1e-19, None, ALU.is_gt))
            mark(ts(pz[:, 6, :], pz[:, 4, :], 1e-19, None, ALU.is_le))
            ts(b1n[:, :], C("b1"), -1.0, None, ALU.mult).then_inc(s["bias_set"], 1)
            dve.wait_ge(s["table_in"], 1)
            for _ in range(2):
                link(tt(pz[:, 9, :], pz[:, 1, :], pz[:, 1, :], ALU.mult))
                link(tt(pz[:, 9, :], pz[:, 9, :], pz[:, 0, :], ALU.mult))
                link(ts(pz[:, 9, :], pz[:, 9, :], -0.5, 1.5, ALU.mult, ALU.add))
                link(tt(pz[:, 1, :], pz[:, 1, :], pz[:, 9, :], ALU.mult))
            tt(pz[:, 7, :], pz[:, 4, :], pz[:, 1, :], ALU.mult).then_inc(s["unit"], 1)
            link(tt(pz[:, 10, :], pz[:, 1, :], pz[:, 5, :], ALU.mult))
            for F in (FR, CR):
                mark(dve.memset(F[:, :, 0:1], 1.0))
            for F in (FI, CI):
                mark(dve.memset(F[:, :, 0:1], 0.0))
            mark(tt(FR[:, :, 1], re, pz[:, 10, :], ALU.mult))
            mark(tt(FI[:, :, 1], im, pz[:, 10, :], ALU.mult))
            settle()
            link(tt(FR[:, :, 1], FR[:, :, 1], pz[:, 6, :], ALU.add))
            dve.wait_ge(s["table_in"], 2)
            link(ts(pz[:, 11, :], pz[:, 8, :], 1.0, None, ALU.add))
            link(dve.reciprocal(pz[:, 11, :], pz[:, 11, :]))
            link(ts(pz[:, 12, :], pz[:, 8, :], -1.0, 1.0, ALU.mult, ALU.add))
            mark(tt(pz[:, 12, :], pz[:, 12, :], pz[:, 11, :], ALU.mult))
            settle()

            def cmul(outs, x, y, shape):
                (xr, xi), (yr, yi) = x, y
                n = 1
                for d in shape:
                    n *= d
                tmp = [t[:, 0:n] for t in tt4]
                if len(shape) == 2:
                    tmp = [t.rearrange("p (a b) -> p a b", a=shape[0]) for t in tmp]
                mark(tt(tmp[0], xr, yr, ALU.mult))
                mark(tt(tmp[1], xi, yi, ALU.mult))
                mark(tt(tmp[2], xr, yi, ALU.mult))
                mark(tt(tmp[3], xi, yr, ALU.mult))
                settle()
                mark(tt(outs[0], tmp[0], tmp[1], ALU.subtract))
                mark(tt(outs[1], tmp[2], tmp[3], ALU.add))
                settle()

            def powers(R, I, top):
                m = 1
                while m < top:
                    bc = (P, DEPTH, m)
                    cmul((R[:, :, m + 1:2 * m + 1], I[:, :, m + 1:2 * m + 1]),
                         (R[:, :, 1:m + 1], I[:, :, 1:m + 1]),
                         (R[:, :, m:m + 1].to_broadcast(bc), I[:, :, m:m + 1].to_broadcast(bc)), (DEPTH, m))
                    m *= 2

            for j in PAIRS0:
                dve.wait_ge(s[f"x_in{j}"], 16)
                stats(lambda tb: XR[:, 2 * j + tb, :], j, 1e-5, "ln0_stats")
            for i, j in enumerate(PAIRS0):
                dve.wait_ge(s["ln0_rstd"], i + 1)
                for tb in range(TB):
                    normalise(XN0[:, 2 * j + tb, :], XR[:, 2 * j + tb, :], j, tb).then_inc(s["xn0"], 1)

            powers(FR, FI, FINE)
            mark(dve.tensor_copy(CR[:, :, 1], FR[:, :, FINE]))
            link(dve.tensor_copy(CI[:, :, 1], FI[:, :, FINE]))
            powers(CR, CI, COARSE)

            cmul((pz[:, 13, :], pz[:, 14, :]), (C("lc_re"), C("lc_im")), (FR[:, :, 1], FI[:, :, 1]), (DEPTH,))
            link(ts(pz[:, 14, :], pz[:, 14, :], -1.0, None, ALU.mult))
            ts(pz[:, 15, :], pz[:, 12, :], 1.0, None, ALU.mult).then_inc(s["powers"], 1)

            for h in range(2):
                dve.wait_ge(s["h_in"], h + 1)
                ts(Hs[:, half_cols(h)], NB[h], C("bin"), None, ALU.add).then_inc(s[f"h_new{h}"], 1)

            def unpack(step):
                par, hh, step = step // 16, step // 8 % 2, step % 8
                w = weff[:, 2 * hh + par, :]
                code, field, tmp, pk = codes[:, hh, :], fieldf[:, hh, :], dtmp[:, hh, :], packed[:, hh, :]
                settle()
                if step == 0:
                    if par == 0 and hh == 0:
                        dve.wait_ge(s["deq_in"], 16 * 7)
                    mark(ts(code, pk, 4 * par, 7, ALU.logical_shift_right, ALU.bitwise_and))
                elif step == 1:
                    mark(ts(w, code, 0.5, None, ALU.mult))
                    mark(ts(field, code, 4.0, 0.0, ALU.subtract, ALU.max))
                elif step == 2:
                    mark(ts(tmp, code, 6.0, 0.0, ALU.subtract, ALU.max))
                elif step == 3:
                    mark(stt(w, field, 0.5, w, ALU.mult, ALU.add))
                elif step == 4:
                    mark(tt(w, w, tmp, ALU.add))
                    mark(ts(code, pk, 4 * par + 3, 1, ALU.logical_shift_right, ALU.bitwise_and))
                elif step == 5:
                    mark(ts(field, code, -2.0, 1.0, ALU.mult, ALU.add))
                    mark(tt(tmp, bsc[:, hh, :], w, ALU.mult))
                elif step == 6:
                    mark(tt(w, tmp, field, ALU.mult))
                else:
                    mark(ts(w, w, gsb[:, 0:1], None, ALU.mult))

            unpacked = [0]

            def first_half(what, l, h):
                at = half_cols(h)
                if what in ("cen1", "cen2"):
                    return
                if what in ("var1", "var2"):
                    i = 2 * l + (what == "var2")
                    dve.wait_ge(s[f"rstd{h}"], i + 1)
                    link(tt(S[:, at], NB[h], RSTD[:, at], ALU.mult))
                    if l == DEPTH:
                        ts(HN[:, at], S[:, at], C("lnl_w"), C("lnl_b"), ALU.mult, ALU.add).then_inc(s[f"hn{h}"], 1)
                    else:
                        ln = "ln" + what[-1]
                        ts(Z[:, at], S[:, at], C(ln + "_w", l), C(ln + "_b", l), ALU.mult, ALU.add
                           ).then_inc(s[f"normed{h}"], 1)
                elif what == "sig1":
                    dve.wait_ge(s[f"exped{h}"], 3 * l + 1)
                    ts(T0[:, at], T0[:, at], 1e18, None, ALU.min).then_inc(s[f"clamped{h}"], 1)
                elif what == "turn":
                    dve.wait_ge(s[f"sigmoid{h}"], 3 * l + 1)
                    link(tt(S[:, at], T0[:, at], Z[:, at], ALU.mult))
                    if h == 0:
                        dve.wait_ge(s["tables"], l + 1)
                    mark(tt(MR[:, at], S[:, at], COS[:, l, at], ALU.mult))
                    mark(tt(MI[:, at], S[:, at], SIN[:, l, at], ALU.mult))
                elif what == "scan":
                    settle()
                    decay = pz[:, 12, l:l + 1].to_broadcast((P, CH))
                    first = [pz[:, 13, l:l + 1], pz[:, 14, l:l + 1]] if h == 0 else [UR[:, CH - 1:CH], VI[:, CH - 1:CH]]
                    mark(dve.tensor_tensor_scan(UR[:, at], decay, MR[:, at], first[0], ALU.mult, ALU.add))
                    mark(dve.tensor_tensor_scan(VI[:, at], decay, MI[:, at], first[1], ALU.mult, ALU.add))
                    settle()
                    mark(tt(MR[:, at], UR[:, at], COS[:, l, at], ALU.mult))
                    mark(tt(MI[:, at], VI[:, at], SIN[:, l, at], ALU.mult))
                elif what == "add":
                    settle()
                    link(tt(MR[:, at], MR[:, at], MI[:, at], ALU.add))
                    stt(Hs[:, at], MR[:, at], C("scl", l), Hs[:, at], ALU.mult, ALU.add).then_inc(s[f"h_new{h}"], 1)
                    dve.wait_ge(s[f"h_new{h}"], 2 * l + 2)
                    mark(ts(HB[:, at], Hs[:, at], C("b2", l), None, ALU.add))
                elif what == "hide":
                    for f in range(2):
                        dve.wait_ge(s[f"exped{h}"], 3 * l + 2 + f)
                        ts(hth[:, f::2, at], hth[:, f::2, at], 1e18, None, ALU.min).then_inc(s[f"clamped{h}"], 1)
                elif what == "act":
                    for f in range(2):
                        dve.wait_ge(s[f"sigmoid{h}"], 3 * l + 2 + f)
                        stt(hid[:, f::2, at], HID[h][:, :, f, :], C("b1", 2 * l + f), hth[:, f::2, at],
                            ALU.add, ALU.mult).then_inc(s[f"hidden{h}"], 1)
                elif what == "ffn":
                    dve.wait_ge(s[f"ffn_sum{h}"], l + 1)
                    settle()
                    tt(Hs[:, at], VB[h], HB[:, at], ALU.add).then_inc(s[f"h_new{h}"], 1)
                if what in UNPACK_AT and unpacked[0] < UNPACK:
                    unpack(unpacked[0])
                    unpacked[0] += 1
                if (what, l, h) in LORA_AT:
                    i = LORA_AT.index((what, l, h))
                    if i == 0:
                        settle()
                    dve.wait_ge(s["lora_prod"], i + 1)
                    tt(weff[:, i, :], weff[:, i, :], bank("weff_ready", i + 1), ALU.add).then_inc(s["weff_ready"], 1)

            for step0 in ORDER0:
                first_half(*step0)

            def scan(g):
                k, u = g // UNITS, g % UNITS
                dve.wait_ge(s["decay"], g + 1)
                dve.wait_ge(s["dbx"], g + 1)
                if g >= 2:
                    dve.wait_ge(s["turned_h"], 2 * (g - 1))
                    dve.wait_ge(s["state_kept"], g - 1)
                for i in range(HCT):
                    first = HC[:, u, i:i + 1] if k % 2 else 0.0
                    last = dve.tensor_tensor_scan(H[:, g % 2, i, :], DA[:, g % DRING, i, :], DBX[:, g % BRING, i, :],
                                                  first, ALU.mult, ALU.add)
                last.then_inc(s["states"], 1)

            def add_y(g):
                k, u = g // UNITS, g % UNITS
                n, h = u // 2, u % 2
                if u == 0:
                    dve.wait_ge(s["skip_copied"], 4 * (k + 1))
                for tb in range(TB):
                    dve.wait_ge(s["turned_h"], 2 * g + tb + 1)
                    if u >= 2:
                        dve.wait_ge(s["y_sum"], 2 * (g - 2) + tb + 1)
                    y = Y[:, k % 2, tb, 512 * h:512 * h + 512]
                    cn = SPN[:, k % 2, tb, 48 + n:49 + n]
                    stt(y, PS[:, turned_in(g)[tb], :], cn, y, ALU.mult, ALU.add).then_inc(s["y_sum"], 1)

            def norm_and_add(src, i, c, stat):
                for tb in range(TB):
                    mark(normalise(src[:, tb, :], src[:, tb, :], i, tb))
                settle()
                for tb in range(TB):
                    x = XR[:, TB * c + tb, :]
                    mark(tt(x, x, src[:, tb, :], ALU.add))
                settle()
                stats(lambda tb: XR[:, TB * c + tb, :], i + 1, 1e-5, stat)

            for k in ROUNDS:
                for u in range(UNITS):
                    if 0 <= k < NCHUNK:
                        scan(UNITS * k + u)
                        if u:
                            add_y(UNITS * k + u - 1)
                        if u == UNITS - 1:
                            add_y(UNITS * k + u)
                    for what, c in pieces(k, u):
                        name, i = parts(what)
                        if what in LAST0:
                            first_half(*LAST0[what])
                        elif what == "a_norm":
                            dve.wait_ge(s["misc_in"], 48)
                            if c:
                                dve.wait_ge(s["turned_x2"], TB * c)
                            for tb in range(TB):
                                dve.wait_ge(s["attn_out"], TB * c + tb + 1)
                                tt(LR[:, tb, :], bank("a_read", TB * c + tb + 1), boutb[:, :], ALU.add
                                   ).then_inc(s["a_read"], 1)
                            dve.wait_ge(s["a_read"], TB * (c + 1))
                            stats(lambda tb: LR[:, tb, :], 0, 1e-5, "r1_stats")
                        elif what == "x1":
                            dve.wait_ge(s["r1_rstd"], c + 1)
                            norm_and_add(LR, 0, c, "r2_stats")
                        elif what == "xn":
                            dve.wait_ge(s["r2_rstd"], c + 1)
                            for tb in range(TB):
                                normalise(LR[:, tb, :], XR[:, TB * c + tb, :], 1, tb).then_inc(s["xn"], 1)
                        elif what == "f_stats":
                            dve.wait_ge(s["ffn0_copied"], TB * (c + 1))
                            stats(lambda tb: LR[:, tb, :], 2, 1e-5, "r3_stats")
                        elif what == "x2":
                            dve.wait_ge(s["r3_rstd"], c + 1)
                            norm_and_add(LR, 2, c, "r4_stats")
                        elif what == "x2n":
                            dve.wait_ge(s["r4_rstd"], c + 1)
                            for tb in range(TB):
                                normalise(LR[:, tb, :], XR[:, TB * c + tb, :], 3, tb).then_inc(s["x2n"], 1)
                        elif name == "conv":
                            if i == 0 and c >= 2:
                                dve.wait_ge(*out_done(c - 2, 1))
                            dve.wait_ge(s["in_copied"], 4 * c + i + 1)
                            for tap in range(4):
                                for e in range(2):
                                    ct = 2 * i + e
                                    wt = convw[:, ct, tap:tap + 1]
                                    if tap == 0:
                                        mark(ts(XC[:, ct, :], XI[:, ct, 0:CH], wt, C("conv_b", ct),
                                                ALU.mult, ALU.add))
                                        continue
                                    ins = stt(XC[:, ct, :], XI[:, ct, tap:tap + CH], wt, XC[:, ct, :],
                                              ALU.mult, ALU.add)
                                    if tap < 3 or e == 0:
                                        mark(ins)
                                    else:
                                        ins.then_inc(s["conv"], 1)
                                if tap < 3:
                                    settle()
                        elif name == "silu_conv":
                            dve.wait_ge(s["conv_tanh"], 4 * c + i + 1)
                            link(stt(TH[:, :, :], TH[:, :, :], 1.0, XC[:, 2 * i:2 * i + 2, :], ALU.add, ALU.mult))
                            ts(XC[:, 2 * i:2 * i + 2, :], TH[:, :, :], 0.5, None, ALU.mult).then_inc(s["xc"], 1)
                            dve.wait_ge(s["xc"], 4 * c + i + 1)
                        elif what == "ms":
                            dve.wait_ge(s["sp_part"], c + 1)
                            tt(SP[:, :, :], SP[:, :, :], sp_part(c, 1), ALU.add).then_inc(s["sp"], 1)
                            dve.wait_ge(s["sp"], c + 1)
                            tmp = TH[:, 0, 0:64 * TB].rearrange("p (b e) -> p b e", b=TB)
                            link(tt(tmp, SP[:, :, :], SP[:, :, :], ALU.mult))
                            for e, (lo, hi) in enumerate(SEGS):
                                mark(dve.tensor_reduce(MS[:, e, :], tmp[:, :, lo:hi], AX_X, ALU.add))
                            settle()
                            link(ts(MS[:, 0, :], MS[:, 0, :], 1.0 / RK, 1e-6, ALU.mult, ALU.add))
                            ts(MS[:, 1:3, :], MS[:, 1:3, :], 1.0 / NS, 1e-6, ALU.mult, ALU.add).then_inc(s["ms"], 1)
                        elif what == "norm_bc":
                            dve.wait_ge(s["ms_rstd"], c + 1)
                            for e, (lo, hi) in enumerate(SEGS):
                                for tb in range(TB):
                                    stt(SPN[:, c % 2, tb, lo:hi], SP[:, tb, lo:hi], MSR[:, e, tb:tb + 1],
                                        rmsb[:, lo:hi], ALU.mult, ALU.mult).then_inc(s["spn"], 1)
                        elif name == "dtx":
                            half_ct = slice(HCT * i, HCT * (i + 1))
                            dve.wait_ge(s["dt_log"], 2 * c + i + 1)
                            tt(DT[:, c % 2, half_ct, :], DT[:, c % 2, half_ct, :], XI[:, half_ct, 3:3 + CH], ALU.add
                               ).then_inc(s["dt_ready"], 1)
                            dve.wait_ge(s["dt_ready"], 2 * c + i + 1)
                            tt(DTX[:, c % 2, half_ct, :], DT[:, c % 2, half_ct, :], XC[:, half_ct, :], ALU.mult
                               ).then_inc(s["dtx"], 1)
                        elif name == "silu":
                            r = 4 * c + i + 1
                            dve.wait_ge(s["z_tanh"], r)
                            stt(gate_of(c, i), gate_of(c, i), 1.0, bank("z_read", r), ALU.add, ALU.mult
                                ).then_inc(s["z_read"], 1)
                        elif name == "gate":
                            h, tb = i // 2, i % 2
                            dve.wait_ge(s["z_read"], 4 * c + i + 1)
                            if i == 0:
                                dve.wait_ge(s["y_sum"], 2 * UNITS * (c + 1))
                            y = Y[:, c % 2, tb, 512 * h:512 * h + 512]
                            stt(y, gate_of(c, i), 0.5, y, ALU.mult, ALU.mult).then_inc(s["gated"], 1)
                        elif what == "o_stats":
                            dve.wait_ge(s["out_copied"], TB * (c + 1))
                            stats(lambda tb: LP[:, tb, :], 4, 1e-5, "p5_stats")
                        elif what == "x3":
                            dve.wait_ge(s["p5_rstd"], c + 1)
                            norm_and_add(LP, 4, c, "p6_stats")
                        elif what == "x3n":
                            dve.wait_ge(s["p6_rstd"], c + 1)
                            for tb in range(TB):
                                normalise(LP[:, tb, :], XR[:, TB * c + tb, :], 5, tb).then_inc(s["x3n"], 1)
                        elif name == "h":
                            g = NJ * c + i
                            dve.wait_ge(s["gate_tanh"], g + 1)
                            link(stt(GT[:, g % 2, :], GT[:, g % 2, :], 1.0, PS[:, GUB[g % 2], 0:CH],
                                     ALU.add, ALU.mult))
                            if g >= 2:
                                dve.wait_ge(*freed("w", (g - 2) // NJ, (g - 2) % NJ))
                            stt(HJ[:, g % 2, :], GT[:, g % 2, :], 0.5, PS[:, GUB[g % 2], CH:2 * CH],
                                ALU.mult, ALU.mult).then_inc(s["hj"], 1)
                        elif what == "y_stats":
                            dve.wait_ge(s["y_copied"], TB * (c + 1))
                            stats(lambda tb: G[:, tb, :], 6, 1e-5, "p7_stats")
                        elif what == "result":
                            dve.wait_ge(s["p7_rstd"], c + 1)
                            for tb in range(TB):
                                mark(normalise(G[:, tb, :], G[:, tb, :], 6, tb))
                            settle()
                            for tb in range(TB):
                                x = XR[:, TB * c + tb, :]
                                tt(x, x, G[:, tb, :], ALU.add).then_inc(s["result"], 1)


def kernel(**inputs):
    import numpy as np
    import concourse.bacc as bacc
    from concourse.bass_utils import run_bass_kernel_spmd

    v = {n: np.ascontiguousarray(np.asarray(x)) for n, x in inputs.items()}
    A0, F0, A1, F1 = "L0_attn_", "L0_ffn_", "L1_attn_", "L1_ffn_"

    def twice(m):
        m = m.reshape(-1, DIM).T
        return np.concatenate([m, m])

    def tiles(m):
        return m.reshape(CT, P, -1).transpose(1, 0, 2).reshape(P, -1)

    one = np.zeros((P, P), np.float32)
    one[:DIM, :DIM] = one[DIM:, DIM:] = 1.0 / DIM
    eye = np.eye(P, dtype=np.float32)
    c = {"ident": eye, "cen": eye - one, "avg": one, "eps": np.full((P, 1), 1e-5, np.float32),
         "bin": twice(v[A0 + "bin"]), "b1": v[A0 + "b1"].reshape(DEPTH * 2, P).T,
         "lnl_w": twice(v[A0 + "lnl_w"]), "lnl_b": twice(v[A0 + "lnl_b"]), "scl": twice(v[A0 + "sc_lin"]),
         "dt_bias": tiles(v[A1 + "dt_bias"]), "D": tiles(v[A1 + "D_param"]), "conv_b": tiles(v[A1 + "conv_b"]),
         "conv_w": tiles(v[A1 + "conv_w"]), "A_log": tiles(v[A1 + "A_log"])}
    for n in ("ln1_w", "ln1_b", "ln2_w", "ln2_b", "b2", "phz_re", "phz_im", "lc_re", "lc_im"):
        c[n] = twice(v[A0 + n])
    cst = np.concatenate([c[n].reshape(P, -1) for n in CST], axis=1)
    assert cst.shape == (P, NCST)

    w1 = v[A0 + "W1"].transpose(2, 0, 1).reshape(DIM, -1)
    w2 = v[A0 + "W2"].reshape(DEPTH, DIM, 2, P).transpose(3, 0, 2, 1).reshape(P, -1)
    wo = v[A0 + "Wout"].T
    win = v[A0 + "Win"].T.reshape(KT, P, DIM).transpose(1, 0, 2).reshape(P, -1)
    wp = np.concatenate([np.concatenate([wo, wo]), tiles(v[A1 + "x_proj_w"].T)], axis=1)
    assert wp.shape == (P, NWP)

    la = v[F0 + "lora_A"].reshape(16, 2, P, 2).transpose(0, 1, 3, 2).reshape(16, 4 * P)
    lw = v[A1 + "dt_proj_w"].T
    packed = v[F0 + "packed_weight"].astype(np.int32).T.reshape(2, P, W)

    ipw = v[A1 + "in_proj_w"].reshape(KT, P, 4, 512).transpose(2, 1, 0, 3).reshape(4, P, 2048)
    opw = v[A1 + "out_proj_w"].T.reshape(2, HCT, P, W).transpose(0, 2, 1, 3).reshape(2, P, 2048)
    g = v[F1 + "w1"].T.reshape(KT, P, NJ, P).transpose(2, 1, 0, 3).reshape(NJ, P, 512)
    u = v[F1 + "w3"].T.reshape(KT, P, NJ, P).transpose(2, 1, 0, 3).reshape(NJ, P, 512)
    d = v[F1 + "w2"].T.reshape(NJ, P, W)
    wq = np.concatenate([g, u, d], axis=2)
    sc = np.concatenate([v[F1 + "w1_scale"], v[F1 + "w3_scale"], v[F1 + "w2_scale"].T], axis=1).reshape(-1)
    arrays = {"cst": cst, "x": v[A0 + "x"].reshape(TOK, W), "wp": wp, "w1": np.concatenate([w1, w1]), "w2": w2,
              "win": win, "lw": lw, "la": la, "lb": v[F0 + "lora_B"].T, "packed": packed,
              "bs": v[F0 + "block_scales"].T, "gs": v[F0 + "global_scale"], "sc": sc, "bout": v[A0 + "bout"],
              "rms": np.concatenate([v[A1 + "dt_ln_w"], v[A1 + "B_ln_w"], v[A1 + "C_ln_w"]]),
              "ip": ipw, "op": opw, "wq": wq}
    arrays = {n: np.ascontiguousarray(x) for n, x in arrays.items()}
    nc = bacc.Bacc("TRN2", target_bir_lowering=False, num_devices=1)
    aps = {n: nc.dram_tensor(f"in_{n}", x.shape, mybir.dt.from_np(x.dtype), kind="ExternalInput").ap()
           for n, x in arrays.items()}
    out = nc.dram_tensor("out_0", (TOK, W), F32, kind="ExternalOutput").ap()
    build(nc, aps, out)
    r = run_bass_kernel_spmd(nc, [{f"in_{n}": x for n, x in arrays.items()}], core_ids=[0])
    return r.results[0]["out_0"].reshape(2, SEQ, W)
```
